# Optimizing a Trainium2 kernel written in Bass

```python
import numpy as np
import jax
import jax.numpy as jnp

def _softmax(x, axis=-1):
    return jax.nn.softmax(x, axis=axis)

def _gelu(x):
    return jax.nn.gelu(x, approximate=True)

def _silu(x):
    return jax.nn.silu(x)

def _sigmoid(x):
    return jax.nn.sigmoid(x)

def _layernorm(x, axis=-1, eps=1e-05):
    m = jnp.mean(x, axis=axis, keepdims=True)
    v = jnp.var(x, axis=axis, keepdims=True)
    return (x - m) / jnp.sqrt(v + eps)

def _scatter_add(tgt, idx, src, axis=0):
    return tgt.at[idx].add(src)

def _segment_sum(src, seg, n):
    return jax.ops.segment_sum(src, seg, n)
kernel_name = 'mk_adaln_d1_jaxref_r4_30b40e'

def setup_inputs(seed: int=0):
    np.random.seed(seed)
    _w = jnp.asarray

    def _L0_attn_setup():
        import jax, jax.numpy as jnp
        from jax import lax
        import numpy as np
        import math
        B, T, HID = (4, 512, 256)
        NH, KS, INTER = (8, 4, 704)
        HD = HID // NH
        CHUNK = 32
        EPS = 1e-06

        def rmsnorm(x, w, eps=EPS):
            ms = jnp.mean(jnp.square(x), axis=-1, keepdims=True)
            return x * lax.rsqrt(ms + eps) * w

        def decay_scan(x, decay, init):
            b, h, t, d = x.shape
            c = min(CHUNK, t)
            log_d = jnp.log(jnp.maximum(decay.astype(jnp.float32), 1e-08))
            idx = jnp.arange(c, dtype=jnp.float32)
            log_p = log_d[..., None] * idx[None, None, :, None]
            p, inv_p = (jnp.exp(log_p), jnp.exp(-log_p))
            init_p = jnp.exp(log_d[..., None] * (idx + 1.0)[None, None, :, None])
            xc = x.astype(jnp.float32).reshape(b, h, t // c, c, d)
            xc = jnp.moveaxis(xc, 2, 0)

            def step(state, chunk):
                cs = jnp.cumsum(chunk * inv_p, axis=2)
                out = cs * p + state[:, :, None, :] * init_p
                return (out[:, :, -1, :], out)
            _, outs = lax.scan(step, init.astype(jnp.float32), xc)
            out = jnp.moveaxis(outs, 0, 2).reshape(b, h, t, d)
            return out.astype(x.dtype)

        def _forward(x, qkv_w, out_proj_w, out_gate_w, out_gate_b, decay_param, conv_w, conv_b, pw_w, gate_w, w1, w2, w3, norm1_w, norm2_w):
            b, t, _ = x.shape
            h = rmsnorm(x, norm1_w)
            xc = jnp.transpose(h, (0, 2, 1))
            pad = jnp.zeros((b, HID, KS - 1), x.dtype)
            xc = jnp.concatenate([pad, xc], axis=2)
            conv = lax.conv_general_dilated(xc, conv_w, (1,), 'VALID', dimension_numbers=('NCH', 'OIH', 'NCH'), feature_group_count=HID)
            conv = conv + conv_b[None, :, None]
            conv = jnp.transpose(conv, (0, 2, 1))
            local = jnp.einsum('bth,oh->bto', jax.nn.silu(conv), pw_w)
            qkv = jnp.einsum('bth,oh->bto', h, qkv_w)
            q, k, v = jnp.split(qkv, 3, axis=-1)

            def heads(z):
                return jnp.transpose(z.reshape(b, t, NH, HD), (0, 2, 1, 3))
            q, k, v = (heads(q), heads(k), heads(v))
            q = jax.nn.elu(q) + 1.0
            k = jax.nn.elu(k) + 1.0
            decay = jax.nn.sigmoid(decay_param).reshape(1, NH, 1)
            zero_state = jnp.zeros((b, NH, HD), x.dtype)
            running_kv = decay_scan(k * v, decay, zero_state)
            running_ks = decay_scan(k, decay, zero_state)
            den = jnp.maximum(jnp.sum(q * running_ks, axis=-1, keepdims=True), 1e-06)
            o = q * running_kv / den
            v_direct = jnp.transpose(v, (0, 2, 1, 3)).reshape(b, t, HID)
            o = jnp.transpose(o, (0, 2, 1, 3)).reshape(b, t, HID)
            g = jax.nn.sigmoid(jnp.einsum('bth,oh->bto', o, out_gate_w) + out_gate_b)
            o = g * o + (1.0 - g) * v_direct
            attn = jnp.einsum('bth,oh->bto', o, out_proj_w)
            comb = jnp.concatenate([local, attn], axis=-1)
            gmix = jax.nn.sigmoid(jnp.einsum('bth,oh->bto', comb, gate_w))
            x = x + gmix * local + (1.0 - gmix) * attn
            h2 = rmsnorm(x, norm2_w)
            ffn = jnp.einsum('bti,oi->bto', jax.nn.silu(jnp.einsum('bth,ih->bti', h2, w1)) * jnp.einsum('bth,ih->bti', h2, w2), w3)
            return x + ffn
        key = jax.random.key(seed)
        ks = jax.random.split(key, 16)

        def w(k, shape, fan_in):
            return jax.random.normal(k, shape, jnp.float32) * (1.0 / math.sqrt(fan_in))
        logit = math.log(0.95 / 0.05)
        return {'x': jax.random.normal(ks[0], (B, T, HID), jnp.float32), 'qkv_w': w(ks[1], (3 * HID, HID), HID), 'out_proj_w': w(ks[2], (HID, HID), HID), 'out_gate_w': w(ks[3], (HID, HID), HID), 'out_gate_b': jnp.zeros((HID,), jnp.float32), 'decay_param': jnp.full((NH,), logit, jnp.float32), 'conv_w': w(ks[4], (HID, 1, KS), KS), 'conv_b': jnp.zeros((HID,), jnp.float32), 'pw_w': w(ks[5], (HID, HID), HID), 'gate_w': w(ks[6], (HID, 2 * HID), 2 * HID), 'w1': w(ks[7], (INTER, HID), HID), 'w2': w(ks[8], (INTER, HID), HID), 'w3': w(ks[9], (HID, INTER), INTER), 'norm1_w': jnp.ones((HID,), jnp.float32), 'norm2_w': jnp.ones((HID,), jnp.float32)}
    _L0_attn_in = _L0_attn_setup()

    def _L0_ffn_setup():
        import jax, jax.numpy as jnp
        import numpy as np
        B, S, H, E = (4, 512, 256, 8)
        key = jax.random.key(seed)
        k1, k2, k3 = jax.random.split(key, 3)
        scale = 1.0 / np.sqrt(H)
        return {'x': jax.random.normal(k1, (B, S, H), dtype=jnp.float32), 'router_w': jax.random.normal(k2, (H, E), dtype=jnp.float32) * scale, 'router_b': jnp.zeros((E,), dtype=jnp.float32), 'expert_w': jax.random.normal(k3, (E, H, H), dtype=jnp.float32) * scale, 'expert_b': jnp.zeros((E, H), dtype=jnp.float32)}
    _L0_ffn_in = _L0_ffn_setup()
    _L0_c = _w((lambda *s: np.random.randn(*s).astype(np.float32) * 0.05)(2, 256))
    _L0_wmod = _w((lambda *s: np.random.randn(*s).astype(np.float32) * 0.05)(256, 6 * 256) * 256 ** (-0.5))
    _d = {'L0_attn_x': _L0_attn_in['x'], 'L0_attn_qkv_w': _L0_attn_in['qkv_w'], 'L0_attn_out_proj_w': _L0_attn_in['out_proj_w'], 'L0_attn_out_gate_w': _L0_attn_in['out_gate_w'], 'L0_attn_out_gate_b': _L0_attn_in['out_gate_b'], 'L0_attn_decay_param': _L0_attn_in['decay_param'], 'L0_attn_conv_w': _L0_attn_in['conv_w'], 'L0_attn_conv_b': _L0_attn_in['conv_b'], 'L0_attn_pw_w': _L0_attn_in['pw_w'], 'L0_attn_gate_w': _L0_attn_in['gate_w'], 'L0_attn_w1': _L0_attn_in['w1'], 'L0_attn_w2': _L0_attn_in['w2'], 'L0_attn_w3': _L0_attn_in['w3'], 'L0_attn_norm1_w': _L0_attn_in['norm1_w'], 'L0_attn_norm2_w': _L0_attn_in['norm2_w'], 'L0_ffn_router_w': _L0_ffn_in['router_w'], 'L0_ffn_router_b': _L0_ffn_in['router_b'], 'L0_ffn_expert_w': _L0_ffn_in['expert_w'], 'L0_ffn_expert_b': _L0_ffn_in['expert_b'], 'L0_c': _L0_c, 'L0_wmod': _L0_wmod}
    _x0 = _d['L0_attn_x']
    _d['L0_attn_x'] = jax.random.normal(jax.random.fold_in(jax.random.key(seed), 1), (2, 2048, 256), dtype=_x0.dtype)
    del _x0
    return _d

def reference(L0_attn_x, L0_attn_qkv_w, L0_attn_out_proj_w, L0_attn_out_gate_w, L0_attn_out_gate_b, L0_attn_decay_param, L0_attn_conv_w, L0_attn_conv_b, L0_attn_pw_w, L0_attn_gate_w, L0_attn_w1, L0_attn_w2, L0_attn_w3, L0_attn_norm1_w, L0_attn_norm2_w, L0_ffn_router_w, L0_ffn_router_b, L0_ffn_expert_w, L0_ffn_expert_b, L0_c, L0_wmod):

    def _L0_attn_ref(x, qkv_w, out_proj_w, out_gate_w, out_gate_b, decay_param, conv_w, conv_b, pw_w, gate_w, w1, w2, w3, norm1_w, norm2_w):
        import jax, jax.numpy as jnp
        from jax import lax
        import numpy as np
        import math
        B, T, HID = (4, 512, 256)
        NH, KS, INTER = (8, 4, 704)
        HD = HID // NH
        CHUNK = 32
        EPS = 1e-06

        def rmsnorm(x, w, eps=EPS):
            ms = jnp.mean(jnp.square(x), axis=-1, keepdims=True)
            return x * lax.rsqrt(ms + eps) * w

        def decay_scan(x, decay, init):
            b, h, t, d = x.shape
            c = min(CHUNK, t)
            log_d = jnp.log(jnp.maximum(decay.astype(jnp.float32), 1e-08))
            idx = jnp.arange(c, dtype=jnp.float32)
            log_p = log_d[..., None] * idx[None, None, :, None]
            p, inv_p = (jnp.exp(log_p), jnp.exp(-log_p))
            init_p = jnp.exp(log_d[..., None] * (idx + 1.0)[None, None, :, None])
            xc = x.astype(jnp.float32).reshape(b, h, t // c, c, d)
            xc = jnp.moveaxis(xc, 2, 0)

            def step(state, chunk):
                cs = jnp.cumsum(chunk * inv_p, axis=2)
                out = cs * p + state[:, :, None, :] * init_p
                return (out[:, :, -1, :], out)
            _, outs = lax.scan(step, init.astype(jnp.float32), xc)
            out = jnp.moveaxis(outs, 0, 2).reshape(b, h, t, d)
            return out.astype(x.dtype)

        def _forward(x, qkv_w, out_proj_w, out_gate_w, out_gate_b, decay_param, conv_w, conv_b, pw_w, gate_w, w1, w2, w3, norm1_w, norm2_w):
            b, t, _ = x.shape
            h = rmsnorm(x, norm1_w)
            xc = jnp.transpose(h, (0, 2, 1))
            pad = jnp.zeros((b, HID, KS - 1), x.dtype)
            xc = jnp.concatenate([pad, xc], axis=2)
            conv = lax.conv_general_dilated(xc, conv_w, (1,), 'VALID', dimension_numbers=('NCH', 'OIH', 'NCH'), feature_group_count=HID)
            conv = conv + conv_b[None, :, None]
            conv = jnp.transpose(conv, (0, 2, 1))
            local = jnp.einsum('bth,oh->bto', jax.nn.silu(conv), pw_w)
            qkv = jnp.einsum('bth,oh->bto', h, qkv_w)
            q, k, v = jnp.split(qkv, 3, axis=-1)

            def heads(z):
                return jnp.transpose(z.reshape(b, t, NH, HD), (0, 2, 1, 3))
            q, k, v = (heads(q), heads(k), heads(v))
            q = jax.nn.elu(q) + 1.0
            k = jax.nn.elu(k) + 1.0
            decay = jax.nn.sigmoid(decay_param).reshape(1, NH, 1)
            zero_state = jnp.zeros((b, NH, HD), x.dtype)
            running_kv = decay_scan(k * v, decay, zero_state)
            running_ks = decay_scan(k, decay, zero_state)
            den = jnp.maximum(jnp.sum(q * running_ks, axis=-1, keepdims=True), 1e-06)
            o = q * running_kv / den
            v_direct = jnp.transpose(v, (0, 2, 1, 3)).reshape(b, t, HID)
            o = jnp.transpose(o, (0, 2, 1, 3)).reshape(b, t, HID)
            g = jax.nn.sigmoid(jnp.einsum('bth,oh->bto', o, out_gate_w) + out_gate_b)
            o = g * o + (1.0 - g) * v_direct
            attn = jnp.einsum('bth,oh->bto', o, out_proj_w)
            comb = jnp.concatenate([local, attn], axis=-1)
            gmix = jax.nn.sigmoid(jnp.einsum('bth,oh->bto', comb, gate_w))
            x = x + gmix * local + (1.0 - gmix) * attn
            h2 = rmsnorm(x, norm2_w)
            ffn = jnp.einsum('bti,oi->bto', jax.nn.silu(jnp.einsum('bth,ih->bti', h2, w1)) * jnp.einsum('bth,ih->bti', h2, w2), w3)
            return x + ffn
        return _forward(x, qkv_w, out_proj_w, out_gate_w, out_gate_b, decay_param, conv_w, conv_b, pw_w, gate_w, w1, w2, w3, norm1_w, norm2_w)

    def _L0_ffn_ref(x, router_w, router_b, expert_w, expert_b):
        import jax, jax.numpy as jnp
        import numpy as np
        B, S, H, E = (4, 512, 256, 8)
        b, s, h = x.shape
        hs = x.reshape(-1, h)
        logits = hs @ router_w + router_b
        probs = jax.nn.softmax(logits, axis=-1)
        idx = jnp.argmax(probs, axis=-1)
        gate = jnp.take_along_axis(probs, idx[:, None], axis=-1)
        expert_out = jnp.einsum('th,ehd->ted', hs, expert_w) + expert_b
        dispatch = jax.nn.one_hot(idx, expert_w.shape[0], dtype=hs.dtype) * gate
        out = jnp.einsum('te,ted->td', dispatch, expert_out)
        return out.reshape(b, s, h)
    x = L0_attn_x
    mod = (_silu(L0_c) @ L0_wmod).reshape(L0_c.shape[0], 6, 1, -1)
    sa, ca, ga, sb, cb, gb = (mod[:, 0], mod[:, 1], mod[:, 2], mod[:, 3], mod[:, 4], mod[:, 5])
    ga = (2 * (ga >= 0) - 1) * jnp.maximum(jnp.abs(ga), 0.25)
    gb = (2 * (gb >= 0) - 1) * jnp.maximum(jnp.abs(gb), 0.25)
    h = _layernorm(x, axis=-1) * (1 + ca) + sa
    x = x + ga * _L0_attn_ref(h, L0_attn_qkv_w, L0_attn_out_proj_w, L0_attn_out_gate_w, L0_attn_out_gate_b, L0_attn_decay_param, L0_attn_conv_w, L0_attn_conv_b, L0_attn_pw_w, L0_attn_gate_w, L0_attn_w1, L0_attn_w2, L0_attn_w3, L0_attn_norm1_w, L0_attn_norm2_w)
    h = _layernorm(x, axis=-1) * (1 + cb) + sb
    x = x + gb * _L0_ffn_ref(h, L0_ffn_router_w, L0_ffn_router_b, L0_ffn_expert_w, L0_ffn_expert_b)
    return x

_drawn_inputs = setup_inputs


def setup_inputs(seed=0):
    import zlib

    import numpy as np

    out = dict(_drawn_inputs(seed))
    spreads = {'L0_attn_out_gate_b': (0.0, 0.8),
     'L0_attn_decay_param': (2.944438934326172, 0.6),
     'L0_attn_conv_b': (0.0, 0.624),
     'L0_attn_norm1_w': (1.0, 0.2),
     'L0_attn_norm2_w': (1.0, 0.2),
     'L0_ffn_router_b': (0.0, 0.403),
     'L0_ffn_expert_b': (0.0, 0.8)}
    factors = {'L0_attn_out_gate_w': 64.0}
    for name, (base, spread) in spreads.items():
        noise = np.random.default_rng([zlib.crc32(name.encode()), seed]).standard_normal(out[name].shape)
        drawn = base * np.exp(spread * noise) if base else spread * noise
        out[name] = jnp.asarray(drawn.astype(out[name].dtype))
    for name, factor in factors.items():
        out[name] = (out[name] * factor).astype(out[name].dtype)
    return out
```

```python
from contextlib import ExitStack

import concourse.bass as bass
from concourse import mybir

ALU = mybir.AluOpType
ACT = mybir.ActivationFunctionType
F32 = mybir.dt.float32
F32R = mybir.dt.float32r
P = 128

BATCH, SEQ, HID = 2, 2048, 256
KC = HID // P
HEADS, TAPS, INTER, EXPERTS = 8, 4, 704, 8
TILE = 512
BLK = TILE // P
TILES = BATCH * SEQ // TILE
CHUNKS = -(-INTER // P)
INTER_PAD = CHUNKS * P
HALO = TAPS - 1
LN_EPS, RMS_EPS = 1e-5, 1e-6

W_QKV = 0
W_PW = W_QKV + KC * 3 * HID
W_GATE = W_PW + KC * HID
W_OUT = W_GATE + KC * HID
W_MIX = W_OUT + KC * HID
W_1 = W_MIX + 2 * KC * HID
W_2 = W_1 + KC * INTER_PAD
W_3 = W_2 + KC * INTER_PAD
W_COLS = W_3 + CHUNKS * HID
PIECE = KC * TILE

C_N1, C_N2, C_CW, C_CB, C_GB, C_DEC, C_C, C_RW, C_RB = 0, 2, 4, 12, 14, 16, 18, 22, 38
C_COLS = 46
K_ID, K_HS, K_HX = 0, 128, 144
K_TRI = K_HX + 2 * P
K_IOTA = K_TRI + P
K_RANK = K_IOTA + P
K_TOK = K_RANK + EXPERTS
K_COLS = K_TOK + BATCH * SEQ // P

NBLK = BATCH * SEQ // P
SLOTS = NBLK + EXPERTS - 1
RING = 3
GROUPS = SLOTS // RING
assert SLOTS == RING * GROUPS


def count(n, per, k):
    return per * n + k


def reuse(eng, sem, value):
    if isinstance(value, int) and value <= 0:
        return
    eng.wait_ge(sem, value)


def build(nc, x, wall, wexp, wmod, params, consts, ebias, out, rec):
    with ExitStack() as ctx:
        def sb(name, shape, dt=F32):
            return ctx.enter_context(nc.sbuf_tensor(name, shape, dt))

        def sem(name):
            return ctx.enter_context(nc.semaphore(name))

        bank = [ctx.enter_context(nc.psum_tensor(f"bank{i}", [P, TILE], F32)) for i in range(8)]
        small = bank[3]

        w_hi, w_lo = sb("w_hi", [P, W_COLS], F32R), sb("w_lo", [P, W_COLS], F32R)
        par, con = sb("par", [P, C_COLS]), sb("con", [P, K_COLS])
        ident = con[:, K_ID:K_ID + P]
        head_sum = con[:, K_HS:K_HS + 16].rearrange("p (f h) -> p f h", f=KC)
        head_spread = con[0:32, K_HX:K_HX + 2 * P].rearrange("p (f m) -> p f m", f=KC)
        ones = sb("ones", [P, 2])
        xln_all = sb("xln", [P, 2, BLK, HID])
        xln = [xln_all[:, p] for p in range(2)]
        xres = sb("xres", [P, BLK, HID])
        xn = sb("xn", [P, BLK, HID])
        h = sb("h", [P, KC, TILE])
        esq = sb("esq", [P, KC, TILE])
        hn = sb("hn", [P, KC, HALO + TILE])
        halo = [sb(f"halo{p}", [P, KC, HALO]) for p in range(2)]
        a_hi, a_lo = sb("a_hi", [P, KC, TILE], F32R), sb("a_lo", [P, KC, TILE], F32R)
        s_hi, s_lo = sb("s_hi", [P, KC, TILE], F32R), sb("s_lo", [P, KC, TILE], F32R)
        l_hi, l_lo = sb("l_hi", [P, KC, TILE], F32R), sb("l_lo", [P, KC, TILE], F32R)
        t_hi, t_lo = sb("t_hi", [P, KC, TILE], F32R), sb("t_lo", [P, KC, TILE], F32R)
        n_hi, n_lo = sb("n_hi", [P, KC, TILE], F32R), sb("n_lo", [P, KC, TILE], F32R)
        p_hi, p_lo = sb("p_hi", [P, 2, TILE], F32R), sb("p_lo", [P, 2, TILE], F32R)
        cbuf = sb("cbuf", [P, KC, TILE])
        th = sb("th", [P, KC, TILE])
        qb, kb = sb("qb", [P, KC, TILE]), sb("kb", [P, KC, TILE])
        vb, kvb = sb("vb", [P, KC, TILE]), sb("kvb", [P, KC, TILE])
        x2 = sb("x2", [P, KC, TILE])
        tha = sb("tha", [P, 2, TILE])
        gated = sb("gated", [P, 2, TILE])
        x1 = sb("x1", [P, BLK, HID])
        ht = sb("ht", [P, BLK, HID])
        hT = sb("hT", [P, KC, TILE])
        logits = sb("logits", [P, BATCH, SEQ // P, EXPERTS])
        bn1, bn2 = sb("bn1", [P, BLK, 6]), sb("bn2", [P, BLK, 6])
        sm1, sm2 = sb("sm1", [P, BLK]), sb("sm2", [P, BLK])
        dm1, dm2 = sb("dm1", [P, BLK]), sb("dm2", [P, BLK])
        ve1, ve2 = sb("ve1", [P, BLK]), sb("ve2", [P, BLK])
        rs1, rs2 = sb("rs1", [P, BLK]), sb("rs2", [P, BLK])
        nm1, nm2 = sb("nm1", [P, BLK]), sb("nm2", [P, BLK])
        mse1, mse2 = sb("mse1", [P, BLK]), sb("mse2", [P, BLK])
        rms1, rms2 = sb("rms1", [P, BLK]), sb("rms2", [P, BLK])
        mhalf = sb("mhalf", [P, BLK])
        den = sb("den", [P, BLK, HEADS])
        rec_tok = sb("rec_tok", [P, 160])
        rec_diag = rec_tok[:, :].rearrange("p (b c) -> p b c", c=40)[:, :, 0:HEADS]
        recT = sb("recT", [32, TILE])
        dec = sb("dec", [P, KC])
        kss_c = [sb(f"kss_c{p}", [P, KC]) for p in range(2)]
        kvs_c = [sb(f"kvs_c{p}", [P, KC]) for p in range(2)]
        csil = sb("csil", [P, KC * BATCH])
        cth = sb("cth", [P, KC * BATCH])
        hgb = sb("hgb", [P, KC])
        mod = sb("mod", [P, 6, BATCH])
        mods = sb("mods", [P, 2, BATCH])
        sbt = sb("sbt", [P, BATCH, HID])
        cbt = sb("cbt", [P, BATCH, HID])
        gbt = sb("gbt", [P, BATCH, HID])

        names = """par_in con_in wmod_in hc_th hc_silu mod_ps mod_done prep w_hi_done w_lo_done ones_set mhalf_set
            ln1_bn ln1_mv ln1_ve ln1_rstd ln1_nm xn_ready t_ps h_ready sq_ready st1_ps ms1 rms1_ready r1_ps hn_ready hn_hi
            hn_lo halo_in conv k_ps q_ps v_ps ek ekm k_ready eq eqm q_ready v_ready kv_ready kss kvs carry
            ths s_ready s_hi_done s_lo_done l_ps loc loc_hi loc_lo qk den_ps den_max den_rec recT_ps recT_ready rec_ps
            qv o_ready o_hi o_lo g_ps thg dgate ugate o2 o2_hi o2_lo o_ps att att_hi att_lo m_ps thm dmix hatt umix
            x2_ready sq2 st2_ps ms2 rms2_ready r2_ps hn2 hn2_hi hn2_lo a_ps b_ps th_a gate_a prod p_hi_done p_lo_done
            f_ps w3_used x2g y_ready y_ps x1_ready ln2_bn ln2_mv ln2_ve ln2_rstd ln2_nm xn2 ht_mul ht_add hT_ps hT_ready
            lg_ps lg xres_in h_stored x1_stored
            ebias_in we_hi_done we_lo_done route route_exp count_ps place_oh place_id place_ps place_done place_free
            g_clear tr_ps th_hi th_lo y_e_ps y_e scattered meta_c gb_row scaled fin""".split()
        s = {n: sem(n) for n in names}
        w_in = [sem(f"w_in{i}") for i in range(4)]
        x_in = [sem(f"x_in{p}") for p in range(2)]
        we_in = [sem(f"we_in{i}") for i in range(4)]
        g_in = [sem(f"g_in{r}") for r in range(RING)]
        sc_done = [sem(f"sc_done{r}") for r in range(RING)]

        x_flat = x.rearrange("b t d -> (b t d)")
        rec_flat = rec.rearrange("t d -> (t d)")
        stage = [qb, kb, vb, kvb]
        PIECES = [(a, min(PIECE, W_COLS - a)) for a in range(0, W_COLS, PIECE)]
        wm = [esq, cbuf, th]

        def w(t, base, kc, width, a, m=P):
            return t[:, base + kc * width + a:base + kc * width + a + m]

        WE_COLS = EXPERTS * KC * HID
        ebt = xln_all[:, :, :, :].rearrange("p a k d -> p (a k d)")
        rows_in = [cbuf[:, 0, :], cbuf[:, 1, :], th[:, 0, :]]
        hs_hi = [a_hi[:, :, :].rearrange("p f t -> p (f t)")[:, r * HID:(r + 1) * HID] for r in range(RING)]
        hs_lo = [a_lo[:, :, :].rearrange("p f t -> p (f t)")[:, r * HID:(r + 1) * HID] for r in range(RING)]
        rows_out = [hT[:, :, :].rearrange("p f t -> p (f t)")[:, r * HID:(r + 1) * HID] for r in range(RING)]
        with_bias = [esq[:, :, :].rearrange("p f t -> p (f t)")[:, r * HID:(r + 1) * HID] for r in range(RING)]
        gb_rows = [tha[:, :, :].rearrange("p f t -> p (f t)")[:, r * HID:(r + 1) * HID] for r in range(RING)]
        lall = logits[:, :, :, :].rearrange("p b k e -> p (b k) e")
        rt = [xn[:, i, :].rearrange("p (k e) -> p k e", e=EXPERTS) for i in range(BLK)]
        small_f, used = gated[:, :, :].rearrange("p f t -> p (f t)"), [0]
        INT = mybir.dt.int32

        def part(n):
            used[0] += n
            return small_f[:, used[0] - n:used[0]]

        by_blk = part(8 * NBLK).rearrange("p (i k) -> p i k", k=NBLK)
        by_exp = part(6 * EXPERTS).rearrange("p (i e) -> p i e", e=EXPERTS)
        by_exp_i = part(EXPERTS).bitcast(INT)
        pos_i = part(3 * NBLK).bitcast(INT).rearrange("p (i k) -> p i k", k=NBLK)
        gate_lo_t = part(NBLK)
        slot_meta = part(2 * SLOTS).rearrange("p (s m) -> p s m", m=2)
        slot_sum = part(SLOTS)[0:1, :]
        slot_e = part(SLOTS).bitcast(INT)[0:1, :]
        meta_now = [part(2) for r in range(RING)]
        slot_idx = part(SLOTS).bitcast(INT)
        grt = p_hi[:, 0, 0:NBLK]
        SP_ = 40
        place_hi = x1[:, :, :].rearrange("p k d -> p (k d)")
        assert NBLK * EXPERTS == HID
        gneg = xn[:, 0:BATCH, :]

        block = ctx.enter_context(nc.Block())

        def pipeline(eng, step):
            step(0, 0, 0)
            step(1, 0, 1)
            with eng.Fori(1, TILES // 2 - 1) as j:
                step(2 * j, j, 0)
                step(2 * j + 1, j, 1)
            step(TILES - 2, TILES // 2 - 1, 0)
            step(TILES - 1, TILES // 2 - 1, 1)
            step(TILES, TILES // 2, 0)

        def slots(eng, body):
            def group(i):
                for r in range(RING):
                    body(RING * i + r, i, r)
            group(0)
            with eng.Fori(1, GROUPS - 1) as i:
                group(i)
            group(GROUPS - 1)

        def is_first(n):
            return isinstance(n, int) and n == 0

        def is_last(n):
            return isinstance(n, int) and n == TILES

        def has_next(n):
            return not (isinstance(n, int) and n >= TILES - 1)

        def tile_of(eng, flat, width, q, jq):
            at = q * SEQ * width + jq * (TILE * width)
            if not isinstance(at, int):
                at = eng.snap(at)
            return flat[bass.ds(at, TILE * width)].rearrange("(k p d) -> p k d", p=P, d=width)

        slot_oh_all = l_hi[:, :, :].rearrange("p f t -> p (f t)")[:, 0:2 * BLK * 3 * SP_].rearrange(
            "p (k v) -> p k v", v=3 * SP_)

        def slot_oh(b):
            return slot_oh_all[:, b % (2 * BLK), :]

        def lane_oh(b):
            return s_hi[:, :, :].rearrange("p f t -> p (f t)")[:, (b % 8) * P:(b % 8 + 1) * P]

        @block.sync
        def _(sp):
            sp.dma_start(xln[0][:, :, :], tile_of(sp, x_flat, HID, 0, 0)).then_inc(x_in[0], 16)
            sp.dma_start(par[:, :], params).then_inc(s["par_in"], 16)
            sp.dma_start(con[:, :], consts).then_inc(s["con_in"], 16)
            for i in range(3):
                sp.dma_start(wm[i][:, :, :], wmod[:, :, i * TILE:(i + 1) * TILE]).then_inc(s["wmod_in"], 16)
            for i, (a, m) in enumerate(PIECES):
                if i >= 4:
                    sp.wait_ge(s["w_lo_done"], i - 3)
                sp.dma_start(stage[i % 4][:, :, :].rearrange("p f t -> p (f t)")[:, 0:m],
                             wall[:, a:a + m]).then_inc(w_in[i % 4], 16)

            def step(n, j, p):
                m = n - 1
                if has_next(n):
                    q, jq = (1, j) if p == 0 else (0, j + 1)
                    src = tile_of(sp, x_flat, HID, q, jq)
                    if not is_first(n):
                        sp.wait_ge(s["xn_ready"], count(n, BLK, 0))
                    sp.dma_start(xln[q][:, :, :], src).then_inc(x_in[q], 16)

            pipeline(sp, step)
            sp.wait_ge(s["xn_ready"], count(TILES - 1, BLK, BLK))
            sp.dma_start(ebt, ebias).then_inc(s["ebias_in"], 16)
            for i, (name, per) in enumerate((("x2_ready", KC), ("hn2_lo", KC), ("o2_lo", KC), ("o2_lo", KC))):
                sp.wait_ge(s[name], per * TILES)
                sp.dma_start(stage[i][:, :, :].rearrange("p f t -> p (f t)"),
                             wexp[:, i * PIECE:(i + 1) * PIECE]).then_inc(we_in[i], 16)
            for r in range(RING):
                sp.wait_ge(sc_done[r], 16 * GROUPS)

        @block.tensor
        def _(pe):
            mm = pe.matmul
            pe.wait_ge(s["hc_silu"], 2)
            pe.wait_ge(s["wmod_in"], 48)
            for i in range(6):
                for kc in range(KC):
                    a = i * P
                    mm(small[:, 2 * i:2 * i + 2], wm[a // TILE][:, kc, a % TILE:a % TILE + P],
                       csil[:, kc * BATCH:(kc + 1) * BATCH], start=kc == 0, stop=kc == 1)
                    last = None
            for b in range(BATCH):
                for kc in range(KC):
                    lhs = csil[:, kc * BATCH + b:kc * BATCH + b + 1].to_broadcast([P, P])
                    mm(bank[b][:, 0:256], lhs, wm[1][:, kc, 256:512], start=kc == 0, stop=kc == 1)
                for kc in range(KC):
                    lhs = csil[:, kc * BATCH + b:kc * BATCH + b + 1].to_broadcast([P, P])
                    last = mm(bank[4 + b][:, :], lhs, wm[2][:, kc, :], start=kc == 0, stop=kc == 1)
            last.then_inc(s["mod_ps"], 1)

            def product(out_, terms, done, start=True, stop=True):
                k, last_ = 0, None
                todo = [(wh, ah) for wh, wl, ah, al in terms] + [(wl, ah) for wh, wl, ah, al in terms] + [
                    (wh, al) for wh, wl, ah, al in terms]
                for k, (a, b) in enumerate(todo):
                    last_ = mm(out_, a, b, start=start and k == 0, stop=stop and k == len(todo) - 1)
                if done is not None:
                    last_.then_inc(done, 1)
                return last_

            def dense(out_, base, width, a, hi, lo, done):
                product(out_, [(w(w_hi, base, kc, width, a), w(w_lo, base, kc, width, a), hi[:, kc, :], lo[:, kc, :])
                               for kc in range(KC)], done)

            def step(n, j, p):
                m = n - 1
                front, back = not is_last(n), not is_first(n)

                def chunk(c):
                    if not back:
                        return
                    if c == 0:
                        pe.wait_ge(s["hn2_lo"], count(m, KC, KC))
                        pe.wait_ge(s["hn2_hi"], count(m, KC, KC))
                    if c == 0:
                        reuse(pe, s["hT_ready"], count(m, KC, 0))
                    else:
                        pe.wait_ge(s["gate_a"], count(m, CHUNKS, c))
                    dense(bank[6][:, :], W_1, INTER_PAD, c * P, n_hi, n_lo, s["a_ps"])
                    if c > 0:
                        pe.wait_ge(s["prod"], count(m, CHUNKS, c))
                    dense(bank[7][:, :], W_2, INTER_PAD, c * P, n_hi, n_lo, s["b_ps"])

                def w3(c):
                    if not back:
                        return
                    if c == 0:
                        reuse(pe, s["y_ready"], count(m, KC, 0))
                    pe.wait_ge(s["p_hi_done"], count(m, CHUNKS, c + 1))
                    pe.wait_ge(s["p_lo_done"], count(m, CHUNKS, c + 1))
                    for f in range(KC):
                        last_ = product(bank[4 + f][:, :],
                                        [(w(w_hi, W_3, c, HID, f * P), w(w_lo, W_3, c, HID, f * P),
                                          p_hi[:, c % 2, :], p_lo[:, c % 2, :])],
                                        s["f_ps"] if c == CHUNKS - 1 and f == 0 else s["w3_used"] if f == 1 else None,
                                        start=c == 0, stop=c == CHUNKS - 1)

                if front:
                    pe.wait_ge(s["xn_ready"], count(n, BLK, BLK))
                    reuse(pe, s["thm"], count(n, KC, 0))
                    for f in range(KC):
                        for b in range(BLK):
                            last_ = pe.transpose(bank[f][:, b * P:(b + 1) * P], xn[:, b, f * P:(f + 1) * P], ident)
                        last_.then_inc(s["t_ps"], 1)
                chunk(0)
                if front:
                    pe.wait_ge(s["sq_ready"], count(n, KC, KC))
                    reuse(pe, s["ms2"], count(n, 1, 0))
                    for b in range(BLK):
                        for f in range(KC):
                            last_ = mm(small[:, b:b + 1], esq[:, f, b * P:(b + 1) * P], ones[:, 0:1],
                                       start=f == 0, stop=f == KC - 1)
                    last_.then_inc(s["st1_ps"], 1)
                chunk(1)
                w3(0)
                if front:
                    pe.wait_ge(s["rms1_ready"], count(n, 1, 1))
                    reuse(pe, s["hn2"], count(n, KC, 0))
                    for b in range(BLK):
                        last_ = mm(bank[2][:, b * P:(b + 1) * P], rms1[:, b:b + 1].to_broadcast([P, P]), ident,
                                   start=True, stop=True)
                    last_.then_inc(s["r1_ps"], 1)
                chunk(2)
                w3(1)
                if front:
                    pe.wait_ge(s["hn_hi"], count(n, KC, KC))
                    pe.wait_ge(s["hn_lo"], count(n, KC, KC))
                    if is_first(n):
                        pe.wait_ge(s["w_hi_done"], len(PIECES))
                        pe.wait_ge(s["w_lo_done"], len(PIECES))
                    dense(bank[0][:, :], W_QKV, 3 * HID, HID, a_hi, a_lo, s["k_ps"])
                    dense(bank[1][:, :], W_QKV, 3 * HID, HID + P, a_hi, a_lo, s["k_ps"])
                    dense(bank[2][:, :], W_QKV, 3 * HID, 0, a_hi, a_lo, s["q_ps"])
                    pe.wait_ge(s["k_ready"], count(n, KC, 1))
                    dense(bank[0][:, :], W_QKV, 3 * HID, P, a_hi, a_lo, s["q_ps"])
                    pe.wait_ge(s["k_ready"], count(n, KC, 2))
                    dense(bank[1][:, :], W_QKV, 3 * HID, 2 * HID, a_hi, a_lo, s["v_ps"])
                    pe.wait_ge(s["q_ready"], count(n, KC, 1))
                    dense(bank[2][:, :], W_QKV, 3 * HID, 2 * HID + P, a_hi, a_lo, s["v_ps"])
                chunk(3)
                w3(2)
                if front:
                    pe.wait_ge(s["s_hi_done"], count(n, KC, KC))
                    pe.wait_ge(s["s_lo_done"], count(n, KC, KC))
                    pe.wait_ge(s["q_ready"], count(n, KC, 2))
                    dense(bank[0][:, :], W_PW, HID, 0, s_hi, s_lo, s["l_ps"])
                    pe.wait_ge(s["v_ready"], count(n, KC, 1))
                    dense(bank[1][:, :], W_PW, HID, P, s_hi, s_lo, s["l_ps"])
                chunk(4)
                w3(3)
                if front:
                    pe.wait_ge(s["qk"], count(n, KC, KC))
                    for b in range(BLK):
                        for f in range(KC):
                            last_ = mm(small[:, b * HEADS:(b + 1) * HEADS], kb[:, f, b * P:(b + 1) * P],
                                       head_sum[:, f, :], start=f == 0, stop=f == KC - 1)
                    last_.then_inc(s["den_ps"], 1)
                chunk(5)
                w3(4)
                if front:
                    pe.wait_ge(s["den_rec"], count(n, 1, 1))
                    for b in range(BLK):
                        last_ = pe.transpose(small[0:32, b * P:(b + 1) * P], rec_tok[:, 32 * b:32 * b + 32], ident)
                    last_.then_inc(s["recT_ps"], 1)
                w3(5)
                if front:
                    pe.wait_ge(s["recT_ready"], count(n, 1, 1))
                    pe.wait_ge(s["v_ready"], count(n, KC, 2))
                    mm(bank[2][:, :], head_spread[:, 0, :], recT[:, :], start=True, stop=True).then_inc(s["rec_ps"], 1)
                    pe.wait_ge(s["loc"], count(n, KC, 1))
                    mm(bank[0][:, :], head_spread[:, 1, :], recT[:, :], start=True, stop=True).then_inc(s["rec_ps"], 1)
                    pe.wait_ge(s["o_hi"], count(n, KC, KC))
                    pe.wait_ge(s["o_lo"], count(n, KC, KC))
                    pe.wait_ge(s["loc"], count(n, KC, 2))
                    dense(bank[1][:, :], W_GATE, HID, 0, a_hi, a_lo, s["g_ps"])
                    dense(bank[2][:, :], W_GATE, HID, P, a_hi, a_lo, s["g_ps"])
                if back:
                    pe.wait_ge(s["y_ready"], count(m, KC, KC))
                    for i in range(2):
                        for b in range(2):
                            for f in range(KC):
                                last_ = pe.transpose(bank[6 + i][:, b * HID + f * P:b * HID + (f + 1) * P],
                                                     x2[:, f, (2 * i + b) * P:(2 * i + b + 1) * P], ident)
                        last_.then_inc(s["y_ps"], 1)
                if front:
                    pe.wait_ge(s["o2_hi"], count(n, KC, KC))
                    pe.wait_ge(s["o2_lo"], count(n, KC, KC))
                    dense(bank[0][:, :], W_OUT, HID, 0, s_hi, s_lo, s["o_ps"])
                    dense(bank[1][:, :], W_OUT, HID, P, s_hi, s_lo, s["o_ps"])
                if back:
                    pe.wait_ge(s["ht_add"], count(m, 1, 1))
                    for f in range(KC):
                        for b in range(BLK):
                            last_ = pe.transpose(bank[6 + f][:, b * P:(b + 1) * P], ht[:, b, f * P:(f + 1) * P], ident)
                        last_.then_inc(s["hT_ps"], 1)
                if front:
                    pe.wait_ge(s["loc_hi"], count(n, KC, KC))
                    pe.wait_ge(s["loc_lo"], count(n, KC, KC))
                    pe.wait_ge(s["att_hi"], count(n, KC, KC))
                    pe.wait_ge(s["att_lo"], count(n, KC, KC))
                    for f, bk in ((0, 2), (1, 0)):
                        product(bank[bk][:, :],
                                [(w(w_hi, W_MIX, kc, HID, f * P), w(w_lo, W_MIX, kc, HID, f * P),
                                  (l_hi if kc < KC else t_hi)[:, kc % KC, :], (l_lo if kc < KC else t_lo)[:, kc % KC, :])
                                 for kc in range(2 * KC)], s["m_ps"])
                if back:
                    pe.wait_ge(s["hT_ready"], count(m, KC, KC))
                    for b in range(BLK):
                        for f in range(KC):
                            last_ = mm(small[:, b * EXPERTS:(b + 1) * EXPERTS], hT[:, f, b * P:(b + 1) * P],
                                       par[:, C_RW + f * EXPERTS:C_RW + (f + 1) * EXPERTS], start=f == 0, stop=f == KC - 1)
                    last_.then_inc(s["lg_ps"], 1)
                if front:
                    pe.wait_ge(s["sq2"], count(n, KC, KC))
                    if back:
                        pe.wait_ge(s["lg"], count(m, 1, 1))
                    for b in range(BLK):
                        for f in range(KC):
                            last_ = mm(small[:, b:b + 1], esq[:, f, b * P:(b + 1) * P], ones[:, 0:1],
                                       start=f == 0, stop=f == KC - 1)
                    last_.then_inc(s["st2_ps"], 1)
                    pe.wait_ge(s["rms2_ready"], count(n, 1, 1))
                    for b in range(BLK):
                        last_ = mm(bank[2][:, b * P:(b + 1) * P], rms2[:, b:b + 1].to_broadcast([P, P]), ident,
                                   start=True, stop=True)
                    last_.then_inc(s["r2_ps"], 1)

            pe.wait_ge(s["con_in"], 16)
            pe.wait_ge(s["mod_done"], 1)
            pe.wait_ge(s["ones_set"], 1)
            pipeline(pe, step)

            onehot = rt[2][:, :, :].rearrange("p k e -> p (k e)")
            pe.wait_ge(s["route"], 9)
            mm(bank[0][:, 0:HID], con[:, K_TRI:K_TRI + P], onehot, start=True, stop=True)
            mm(bank[1][:, 0:HID], ones[:, 0:1].to_broadcast([P, P]), onehot, start=True, stop=True).then_inc(s["count_ps"], 1)
            for b in range(NBLK):
                pe.wait_ge(s["place_oh"], b + 1)
                if b % BLK == 0:
                    pe.wait_ge(s["place_id"], 3 * (b // BLK + 1))
                mm(bank[2][:, 0:3 * SP_], lane_oh(b), slot_oh(b), start=b == 0, stop=b == NBLK - 1).then_inc(s["place_ps"], 1)

            def turn(t, i, r):
                pe.wait_ge(g_in[r], 16 * (i + 1))
                reuse(pe, s["th_lo"], t - RING + 1)
                for kc in range(KC):
                    last_ = pe.transpose(bank[r][:, kc * P:(kc + 1) * P], rows_in[r][:, kc * P:(kc + 1) * P], ident)
                last_.then_inc(s["tr_ps"], 1)

            def expert(t, i, r):
                e = nc.values_load(slot_e[0:1, bass.ds(t, 1)], engines=[mybir.EngineType.PE], min_val=0, max_val=EXPERTS - 1,
                                   skip_runtime_bounds_check_because="slot_e is a count of experts, at most EXPERTS - 1")
                pe.wait_ge(s["th_lo"], t + 1)
                pe.wait_ge(s["th_hi"], t + 1)
                reuse(pe, s["y_e"], t - RING + 1)
                k = 0
                for a, wt in ((hs_hi[r], w_hi), (hs_hi[r], w_lo), (hs_lo[r], w_hi)):
                    for kc in range(KC):
                        last_ = mm(bank[4 + r][:, 0:HID], a[:, kc * P:(kc + 1) * P],
                                   wt[:, bass.ds(e * (KC * HID) + kc * HID, HID)], start=k == 0, stop=k == 2 * KC + 1)
                        k += 1
                last_.then_inc(s["y_e_ps"], 1)

            def body(t, i, r):
                if not (isinstance(t, int) and t == SLOTS - 1):
                    turn(t + 1, i if r < RING - 1 else i + 1, (r + 1) % RING)
                if isinstance(t, int) and t == 0:
                    pe.wait_ge(s["we_lo_done"], 4)
                expert(t, i, r)

            pe.wait_ge(s["place_done"], 1)
            turn(0, 0, 0)
            slots(pe, body)

        @block.scalar
        def _(act):
            A = act.activation
            act.wait_ge(s["par_in"], 16)
            A(cth[:, :], par[:, C_C:C_C + 4], ACT.Tanh, scale=0.5).then_inc(s["hc_th"], 1)
            A(dec[:, :], par[:, C_DEC:C_DEC + KC], ACT.Tanh, scale=0.5).then_inc(s["hc_th"], 1)
            for i, (a, m) in enumerate(PIECES):
                act.wait_ge(w_in[i % 4], 16 * (i // 4 + 1))
                A(w_hi[:, a:a + m], stage[i % 4][:, :, :].rearrange("p f t -> p (f t)")[:, 0:m],
                  ACT.Copy).then_inc(s["w_hi_done"], 1)

            def step(n, j, p):
                m = n - 1
                front, back = not is_last(n), not is_first(n)

                def gate(c):
                    if not back:
                        return
                    act.wait_ge(s["a_ps"], count(m, CHUNKS, c + 1))
                    reuse(act, s["gate_a"], count(m, CHUNKS, c - 1))
                    A(tha[:, c % 2, :], bank[6][:, :], ACT.Tanh, scale=0.5).then_inc(s["th_a"], 1)

                def split(c):
                    if not back:
                        return
                    act.wait_ge(s["prod"], count(m, CHUNKS, c + 1))
                    reuse(act, s["w3_used"], count(m, CHUNKS, c - 1))
                    A(p_hi[:, c % 2, :], gated[:, c % 2, :], ACT.Copy).then_inc(s["p_hi_done"], 1)

                def round_hi(dst, src, ready, done):
                    for f in range(KC):
                        act.wait_ge(ready, count(n, KC, f + 1))
                        A(dst[:, f, :], src[:, f, :], ACT.Copy).then_inc(done, 1)

                if front:
                    if is_first(n):
                        act.wait_ge(s["mod_done"], 1)
                        norm1(0, 0)
                    for f in range(KC):
                        act.wait_ge(s["t_ps"], count(n, KC, f + 1))
                        if f == 0:
                            reuse(act, s["hatt"], count(n, KC, 0))
                        A(h[:, f, :], bank[f][:, :], ACT.Identity, scale=mod[:, 2 + f, p:p + 1],
                          bias=mod[:, f, p:p + 1]).then_inc(s["h_ready"], 1)
                    reuse(act, s["st2_ps"], count(n, 1, 0))
                    for f in range(KC):
                        act.wait_ge(s["h_ready"], count(n, KC, f + 1))
                        A(esq[:, f, :], h[:, f, :], ACT.Square).then_inc(s["sq_ready"], 1)
                gate(0)
                gate(1)
                split(0)
                if front:
                    round_hi(a_hi, hn[:, :, HALO:], s["hn_ready"], s["hn_hi"])
                gate(2)
                split(1)
                if front:
                    for f in range(KC):
                        act.wait_ge(s["k_ps"], count(n, KC, f + 1))
                        A(esq[:, f, :], bank[f][:, :], ACT.Exp).then_inc(s["ek"], 1)
                    for f in range(KC):
                        act.wait_ge(s["conv"], count(n, KC * TAPS, KC * (TAPS - 1) + f + 1))
                        A(th[:, f, :], cbuf[:, f, :], ACT.Tanh, scale=0.5).then_inc(s["ths"], 1)
                    for f, bk in ((0, 2), (1, 0)):
                        act.wait_ge(s["q_ps"], count(n, KC, f + 1))
                        act.wait_ge(s["k_ready"], count(n, KC, f + 1))
                        A(esq[:, f, :], bank[bk][:, :], ACT.Exp).then_inc(s["eq"], 1)
                    for f, bk in ((0, 1), (1, 2)):
                        act.wait_ge(s["v_ps"], count(n, KC, f + 1))
                        A(vb[:, f, :], bank[bk][:, :], ACT.Copy).then_inc(s["v_ready"], 1)
                    round_hi(s_hi, cbuf, s["s_ready"], s["s_hi_done"])
                gate(3)
                split(2)
                if front:
                    for f in range(KC):
                        act.wait_ge(s["l_ps"], count(n, KC, f + 1))
                        A(cbuf[:, f, :], bank[f][:, :], ACT.Copy, scale=0.5).then_inc(s["loc"], 1)
                    round_hi(l_hi, cbuf, s["loc"], s["loc_hi"])
                gate(4)
                split(3)
                gate(5)
                split(4)
                if front:
                    act.wait_ge(s["recT_ps"], count(n, 1, 1))
                    A(recT[:, :], small[0:32, :], ACT.Copy).then_inc(s["recT_ready"], 1)
                split(5)
                if back:
                    q = 1 - p
                    for f in range(KC):
                        act.wait_ge(s["hn2"], count(m, KC, f + 1))
                        A(x2[:, f, :], x2[:, f, :], ACT.Copy, scale=mod[:, 4 + f, q:q + 1]).then_inc(s["x2g"], 1)
                if front:
                    round_hi(a_hi, kvb, s["o_ready"], s["o_hi"])
                    for f in range(KC):
                        act.wait_ge(s["g_ps"], count(n, KC, f + 1))
                        A(th[:, f, :], bank[1 + f][:, :], ACT.Tanh, scale=0.5, bias=hgb[:, f:f + 1]).then_inc(s["thg"], 1)
                    round_hi(s_hi, kvb, s["o2"], s["o2_hi"])
                    for f in range(KC):
                        act.wait_ge(s["o_ps"], count(n, KC, f + 1))
                        A(qb[:, f, :], bank[f][:, :], ACT.Copy).then_inc(s["att"], 1)
                    round_hi(t_hi, qb, s["att"], s["att_hi"])
                if back:
                    act.wait_ge(s["ln2_nm"], count(m, 1, 1))
                    reuse(act, s["hT_ps"], count(m, KC, 0))
                    reuse(act, s["h_stored"], count(m, 16, 0))
                    for b in range(BLK):
                        A(ht[:, b, :], x1[:, b, :], ACT.Identity, scale=rs2[:, b:b + 1],
                          bias=nm2[:, b:b + 1]).then_inc(s["xn2"], 1)
                    q, jq = (1, j - 1) if p == 0 else (0, j)
                    dst = tile_of(act, rec_flat, 2 * HID, q, jq)
                    act.wait_ge(s["x1_ready"], count(m, KC, KC))
                    act.dma_start(dst[:, :, HID:2 * HID], x1[:, :, :]).then_inc(s["x1_stored"], 16)
                if front:
                    act.dma_start(xres[:, :, :], tile_of(act, x_flat, HID, p, j)).then_inc(s["xres_in"], 16)
                if front:
                    for f, bk in ((0, 2), (1, 0)):
                        act.wait_ge(s["m_ps"], count(n, KC, f + 1))
                        A(th[:, f, :], bank[bk][:, :], ACT.Tanh, scale=0.5).then_inc(s["thm"], 1)
                if back:
                    for f in range(KC):
                        act.wait_ge(s["hT_ps"], count(m, KC, f + 1))
                        A(hT[:, f, :], bank[6 + f][:, :], ACT.Copy).then_inc(s["hT_ready"], 1)
                    act.wait_ge(s["ht_add"], count(m, 1, 1))
                    act.dma_start(dst[:, :, 0:HID], ht[:, :, :]).then_inc(s["h_stored"], 16)
                if front:
                    for f in range(KC):
                        act.wait_ge(s["x2_ready"], count(n, KC, f + 1))
                        A(esq[:, f, :], x2[:, f, :], ACT.Square).then_inc(s["sq2"], 1)
                    round_hi(n_hi, kb, s["hn2"], s["hn2_hi"])
                    if has_next(n):
                        norm1(n + 1, 1 - p)

            def norm1(n, p):
                act.wait_ge(s["ln1_nm"], count(n, 1, 1))
                reuse(act, s["t_ps"], count(n, KC, 0))
                for b in range(BLK):
                    A(xn[:, b, :], xln[p][:, b, :], ACT.Identity, scale=rs1[:, b:b + 1],
                      bias=nm1[:, b:b + 1]).then_inc(s["xn_ready"], 1)

            pipeline(act, step)
            act.wait_ge(s["route"], 2)
            A(rt[1], rt[0], ACT.Exp).then_inc(s["route_exp"], 1)
            for i in range(4):
                act.wait_ge(we_in[i], 16)
                A(w_hi[:, i * PIECE:(i + 1) * PIECE], stage[i][:, :, :].rearrange("p f t -> p (f t)"),
                  ACT.Copy).then_inc(s["we_hi_done"], 1)

            def body(t, i, r):
                act.wait_ge(s["tr_ps"], t + 1)
                reuse(act, s["y_e_ps"], t - RING + 1)
                A(hs_hi[r], bank[r][:, 0:HID], ACT.Copy).then_inc(s["th_hi"], 1)

            slots(act, body)

        @block.vector
        def _(dve):
            TT, TS, STT = dve.tensor_tensor, dve.tensor_scalar, dve.scalar_tensor_tensor
            dve.memset(ones[:, :], 1.0).then_inc(s["ones_set"], 1)
            dve.memset(rec_tok[:, :], 0.0).then_inc(s["prep"], 1)
            for p in range(2):
                dve.memset(halo[p][:, :, :], 0.0).then_inc(s["prep"], 1)
                dve.memset(kss_c[p][:, :], 0.0).then_inc(s["prep"], 1)
                dve.memset(kvs_c[p][:, :], 0.0).then_inc(s["prep"], 1)
            dve.wait_ge(s["hc_th"], 1)
            STT(out=csil[:, :], in0=cth[:, :], scalar=1.0, in1=par[:, C_C:C_C + 4], op0=ALU.add,
                op1=ALU.mult).then_inc(s["hc_silu"], 1)
            dve.wait_ge(s["hc_silu"], 1)
            TS(csil[:, :], csil[:, :], 0.5, None, ALU.mult).then_inc(s["hc_silu"], 1)
            dve.wait_ge(s["hc_th"], 2)
            TS(dec[:, :], dec[:, :], 0.5, 0.5, ALU.mult, ALU.add).then_inc(s["prep"], 1)
            dve.wait_ge(s["prep"], 8)
            TS(dec[:, :], dec[:, :], 1e-8, None, ALU.max).then_inc(s["prep"], 1)
            TS(hgb[:, :], par[:, C_GB:C_GB + KC], 0.5, None, ALU.mult).then_inc(s["prep"], 1)

            def stats(n, xt, bn, sm, dm, ve, stat, comb):
                for b in range(BLK):
                    dve.bn_stats(bn[:, b, :], xt[:, b, :]).then_inc(stat, 1)
                dve.wait_ge(stat, count(n, BLK, BLK))
                TT(sm[:, :], bn[:, :, 1], bn[:, :, 4], ALU.add).then_inc(comb, 1)
                TT(dm[:, :], bn[:, :, 1], bn[:, :, 4], ALU.subtract).then_inc(comb, 1)
                TT(ve[:, :], bn[:, :, 2], bn[:, :, 5], ALU.add).then_inc(comb, 1)
                dve.wait_ge(comb, count(n, 6, 2))
                STT(out=dm[:, :], in0=dm[:, :], scalar=0.25, in1=dm[:, :], op0=ALU.mult, op1=ALU.mult).then_inc(comb, 1)
                dve.wait_ge(comb, count(n, 6, 3))
                TS(ve[:, :], ve[:, :], 1.0 / HID, LN_EPS, ALU.mult, ALU.add).then_inc(comb, 1)
                dve.wait_ge(comb, count(n, 6, 5))
                TT(ve[:, :], ve[:, :], dm[:, :], ALU.add).then_inc(comb, 1)

            def stats1(n, j, p):
                dve.wait_ge(x_in[p], count(j, 16, 16))
                stats(n, xln[p], bn1, sm1, dm1, ve1, s["ln1_bn"], s["ln1_ve"])

            def neg_mean(n, sm, rs, nm, ready, done):
                dve.wait_ge(ready, count(n, 1, 1))
                STT(out=nm[:, :], in0=sm[:, :], scalar=-0.5, in1=rs[:, :], op0=ALU.mult, op1=ALU.mult).then_inc(done, 1)

            stats1(0, 0, 0)
            neg_mean(0, sm1, rs1, nm1, s["ln1_rstd"], s["ln1_nm"])
            dve.wait_ge(s["mod_ps"], 1)
            TS(mod[:, 0:2, :], small[:, 0:4].rearrange("p (i b) -> p i b", b=2), 0.0, None, ALU.add).then_inc(s["prep"], 1)
            TS(mod[:, 2:4, :], small[:, 4:8].rearrange("p (i b) -> p i b", b=2), 1.0, None, ALU.add).then_inc(s["prep"], 1)
            ga = small[:, 8:12].rearrange("p (i b) -> p i b", b=2)
            TS(mods[:, :, :], ga, -1.0, None, ALU.mult).then_inc(s["prep"], 1)
            TS(mod[:, 4:6, :], ga, 0.0, 2.0, ALU.is_ge, ALU.mult).then_inc(s["prep"], 1)
            for b in range(BATCH):
                dve.tensor_copy(sbt[:, b, :], bank[b][:, 0:HID]).then_inc(s["prep"], 1)
                TS(cbt[:, b, :], bank[4 + b][:, 0:HID], 1.0, None, ALU.add).then_inc(s["prep"], 1)
                TS(gneg[:, b, :], bank[4 + b][:, HID:], -1.0, None, ALU.mult).then_inc(s["prep"], 1)
                TS(gbt[:, b, :], bank[4 + b][:, HID:], 0.0, 2.0, ALU.is_ge, ALU.mult).then_inc(s["prep"], 1)
            dve.wait_ge(s["prep"], 22)
            STT(out=mods[:, :, :], in0=ga, scalar=0.25, in1=mods[:, :, :], op0=ALU.max, op1=ALU.max).then_inc(s["prep"], 1)
            for b in range(BATCH):
                STT(out=gneg[:, b, :], in0=bank[4 + b][:, HID:], scalar=0.25, in1=gneg[:, b, :], op0=ALU.max,
                    op1=ALU.max).then_inc(s["prep"], 1)
            dve.wait_ge(s["prep"], 25)
            STT(out=mod[:, 4:6, :], in0=mod[:, 4:6, :], scalar=-1.0, in1=mods[:, :, :], op0=ALU.add,
                op1=ALU.mult).then_inc(s["prep"], 1)
            STT(out=gbt[:, :, :], in0=gbt[:, :, :], scalar=-1.0, in1=gneg, op0=ALU.add, op1=ALU.mult).then_inc(s["mod_done"], 1)
            for i, (a, m) in enumerate(PIECES):
                dve.wait_ge(s["w_hi_done"], i + 1)
                TT(w_lo[:, a:a + m], stage[i % 4][:, :, :].rearrange("p f t -> p (f t)")[:, 0:m],
                   w_hi[:, a:a + m].bitcast(F32), ALU.subtract).then_inc(s["w_lo_done"], 1)

            def step(n, j, p):
                m = n - 1
                front, back = not is_last(n), not is_first(n)

                def glu(c):
                    if not back:
                        return
                    dve.wait_ge(s["th_a"], count(m, CHUNKS, c + 1))
                    reuse(dve, s["p_lo_done"], count(m, CHUNKS, c - 1))
                    STT(out=gated[:, c % 2, :], in0=tha[:, c % 2, :], scalar=1.0, in1=bank[6][:, :], op0=ALU.add,
                        op1=ALU.mult).then_inc(s["gate_a"], 1)
                    dve.wait_ge(s["b_ps"], count(m, CHUNKS, c + 1))
                    dve.wait_ge(s["gate_a"], count(m, CHUNKS, c + 1))
                    STT(out=gated[:, c % 2, :], in0=gated[:, c % 2, :], scalar=0.5, in1=bank[7][:, :], op0=ALU.mult,
                        op1=ALU.mult).then_inc(s["prod"], 1)

                def elu1(bk, dst, e, em, done):
                    for f in range(KC):
                        dve.wait_ge(e, count(n, KC, f + 1))
                        TS(esq[:, f, :], esq[:, f, :], 1.0, None, ALU.min).then_inc(em, 1)
                    for f in range(KC):
                        dve.wait_ge(em, count(n, KC, f + 1))
                        STT(out=dst[:, f, :], in0=bank[bk[f]][:, :], scalar=0.0, in1=esq[:, f, :], op0=ALU.max,
                            op1=ALU.add).then_inc(done, 1)

                def scan(buf, carry, done):
                    for f in range(KC):
                        dve.tensor_tensor_scan(buf[:, f, :], dec[:, f:f + 1].to_broadcast([P, TILE]), buf[:, f, :],
                                               carry[:, f:f + 1], ALU.mult, ALU.add).then_inc(done, 1)
                    for f in range(KC):
                        dve.wait_ge(done, count(n, KC, f + 1))
                        dve.tensor_copy(carry[:, f:f + 1], buf[:, f, TILE - 1:TILE]).then_inc(s["carry"], 1)

                glu(0)
                if front:
                    dve.wait_ge(s["st1_ps"], count(n, 1, 1))
                    TS(mse1[:, :], small[:, 0:BLK], 1.0 / HID, RMS_EPS, ALU.mult, ALU.add).then_inc(s["ms1"], 1)
                    reuse(dve, s["conv"], count(n, KC * TAPS, 0))
                    if is_first(n):
                        dve.wait_ge(s["prep"], 7)
                    dve.tensor_copy(hn[:, :, 0:HALO], halo[p][:, :, :]).then_inc(s["halo_in"], 1)
                glu(1)
                if front:
                    dve.wait_ge(s["r1_ps"], count(n, 1, 1))
                    for f in range(KC):
                        STT(out=hn[:, f, HALO:], in0=h[:, f, :], scalar=par[:, C_N1 + f:C_N1 + f + 1], in1=bank[2][:, :],
                            op0=ALU.mult, op1=ALU.mult).then_inc(s["hn_ready"], 1)
                    dve.wait_ge(s["hn_ready"], count(n, KC, KC))
                    dve.wait_ge(s["halo_in"], count(n, 2, 1))
                    dve.tensor_copy(halo[p][:, :, :], hn[:, :, TILE:TILE + HALO]).then_inc(s["halo_in"], 1)
                glu(2)
                if front:
                    for t in range(TAPS):
                        for f in range(KC):
                            tap = par[:, C_CW + f * TAPS + t:C_CW + f * TAPS + t + 1]
                            src = hn[:, f, t:t + TILE]
                            if t == 0:
                                last = TS(cbuf[:, f, :], src, tap, par[:, C_CB + f:C_CB + f + 1], ALU.mult, ALU.add)
                            else:
                                dve.wait_ge(s["conv"], count(n, KC * TAPS, KC * (t - 1) + f + 1))
                                last = STT(out=cbuf[:, f, :], in0=src, scalar=tap, in1=cbuf[:, f, :], op0=ALU.mult, op1=ALU.add)
                            last.then_inc(s["conv"], 1)
                    elu1((0, 1), kb, s["ek"], s["ekm"], s["k_ready"])
                    elu1((2, 0), qb, s["eq"], s["eqm"], s["q_ready"])
                    for f in range(KC):
                        dve.wait_ge(s["ths"], count(n, KC, f + 1))
                        STT(out=cbuf[:, f, :], in0=th[:, f, :], scalar=1.0, in1=cbuf[:, f, :], op0=ALU.add,
                            op1=ALU.mult).then_inc(s["s_ready"], 1)
                    dve.wait_ge(s["kv_ready"], count(n, KC, KC))
                    if is_first(n):
                        dve.wait_ge(s["prep"], 9)
                    scan(kb, kss_c[p], s["kss"])
                glu(3)
                if front:
                    scan(kvb, kvs_c[p], s["kvs"])
                    if has_next(n):
                        nn, nj, np_ = (n + 1, j, 1) if p == 0 else (n + 1, j + 1, 0)
                glu(4)
                if front:
                    dve.wait_ge(s["den_ps"], count(n, 1, 1))
                    TS(den[:, :, :], small[:, 0:BLK * HEADS].rearrange("p (b h) -> p b h", h=HEADS), 1e-6, None,
                       ALU.max).then_inc(s["den_max"], 1)
                    dve.wait_ge(s["den_max"], count(n, 1, 1))
                    dve.reciprocal(rec_diag, den[:, :, :]).then_inc(s["den_rec"], 1)
                glu(5)
                if front:
                    for f, bk in ((0, 2), (1, 0)):
                        dve.wait_ge(s["qv"], count(n, KC, f + 1))
                        dve.wait_ge(s["rec_ps"], count(n, KC, f + 1))
                        TT(kvb[:, f, :], kvb[:, f, :], bank[bk][:, :], ALU.mult).then_inc(s["o_ready"], 1)
                if back:
                    dve.wait_ge(s["w3_used"], count(m, CHUNKS, CHUNKS))
                    q = 1 - p
                    for f in range(KC):
                        dve.wait_ge(s["x2g"], count(m, KC, f + 1))
                        STT(out=x2[:, f, :], in0=bank[4 + f][:, :], scalar=mod[:, 4 + f, q:q + 1], in1=x2[:, f, :],
                            op0=ALU.mult, op1=ALU.add).then_inc(s["y_ready"], 1)
                if front:
                    for f in range(KC):
                        dve.wait_ge(s["thg"], count(n, KC, f + 1))
                        dve.wait_ge(s["dgate"], count(n, KC, f + 1))
                        STT(out=th[:, f, :], in0=th[:, f, :], scalar=1.0, in1=kvb[:, f, :], op0=ALU.add,
                            op1=ALU.mult).then_inc(s["ugate"], 1)
                    for f in range(KC):
                        dve.wait_ge(s["ugate"], count(n, KC, f + 1))
                        STT(out=kvb[:, f, :], in0=th[:, f, :], scalar=0.5, in1=vb[:, f, :], op0=ALU.mult,
                            op1=ALU.add).then_inc(s["o2"], 1)
                if back:
                    dve.wait_ge(s["xres_in"], count(m, 16, 16))
                    reuse(dve, s["x1_stored"], count(m, 16, 0))
                    for i in range(2):
                        dve.wait_ge(s["y_ps"], count(m, 2, i + 1))
                        TT(x1[:, 2 * i:2 * i + 2, :], bank[6 + i][:, :].rearrange("p (b d) -> p b d", b=2),
                           xres[:, 2 * i:2 * i + 2, :], ALU.add).then_inc(s["x1_ready"], 1)
                    dve.wait_ge(s["x1_ready"], count(m, 2, 2))
                    reuse(dve, s["xn2"], count(m, BLK, 0))
                    stats(m, x1, bn2, sm2, dm2, ve2, s["ln2_bn"], s["ln2_ve"])
                    neg_mean(m, sm2, rs2, nm2, s["ln2_rstd"], s["ln2_nm"])
                if front:
                    if has_next(n):
                        dve.wait_ge(s["xn_ready"], count(n, BLK, BLK))
                        stats1(nn, nj, np_)
                        neg_mean(nn, sm1, rs1, nm1, s["ln1_rstd"], s["ln1_nm"])
                    for f in range(KC):
                        dve.wait_ge(s["thm"], count(n, KC, f + 1))
                        dve.wait_ge(s["dmix"], count(n, KC, f + 1))
                        STT(out=cbuf[:, f, :], in0=th[:, f, :], scalar=1.0, in1=cbuf[:, f, :], op0=ALU.add,
                            op1=ALU.mult).then_inc(s["umix"], 1)
                    for f in range(KC):
                        dve.wait_ge(s["umix"], count(n, KC, f + 1))
                        dve.wait_ge(s["hatt"], count(n, KC, f + 1))
                        STT(out=x2[:, f, :], in0=cbuf[:, f, :], scalar=0.5, in1=qb[:, f, :], op0=ALU.mult,
                            op1=ALU.add).then_inc(s["x2_ready"], 1)
                if back:
                    dve.wait_ge(s["lg_ps"], count(m, 1, 1))
                    q, jq = (1, j - 1) if p == 0 else (0, j)
                    if isinstance(jq, int):
                        dst = logits[:, q, jq * BLK:(jq + 1) * BLK, :]
                    else:
                        dst = logits[:, q, bass.ds(jq * BLK, BLK), :]
                    TT(dst, small[:, 0:BLK * EXPERTS].rearrange("p (b e) -> p b e", e=EXPERTS),
                       par[:, C_RB:C_RB + EXPERTS].rearrange("p (o e) -> p o e", o=1).to_broadcast([P, BLK, EXPERTS]),
                       ALU.add).then_inc(s["lg"], 1)
                if front:
                    dve.wait_ge(s["st2_ps"], count(n, 1, 1))
                    TS(mse2[:, :], small[:, 0:BLK], 1.0 / HID, RMS_EPS, ALU.mult, ALU.add).then_inc(s["ms2"], 1)
                    dve.wait_ge(s["r2_ps"], count(n, 1, 1))
                    for f in range(KC):
                        dve.wait_ge(s["x2_ready"], count(n, KC, f + 1))
                        STT(out=kb[:, f, :], in0=x2[:, f, :], scalar=par[:, C_N2 + f:C_N2 + f + 1], in1=bank[2][:, :],
                            op0=ALU.mult, op1=ALU.mult).then_inc(s["hn2"], 1)

            pipeline(dve, step)

            k = [0]

            def routed(ins):
                k[0] += 1
                ins.then_inc(s["route"], 1)
                dve.wait_ge(s["route"], k[0])

            def bc(a):
                return a.rearrange("p (k o) -> p k o", o=1).to_broadcast([P, NBLK, EXPERTS])

            best, esum, gate, best_rank, pos, slot_f, lane_f, gate_hi = (by_blk[:, i, :] for i in range(8))
            dve.wait_ge(s["lg"], TILES)
            routed(dve.tensor_reduce(best, lall, mybir.AxisListType.X, ALU.max))
            routed(TT(rt[0], lall, bc(best), ALU.subtract))
            routed(TS(rt[2], rt[0], 0.0, None, ALU.is_ge))
            rank = con[:, K_RANK:K_RANK + EXPERTS].rearrange("p (o e) -> p o e", o=1).to_broadcast([P, NBLK, EXPERTS])
            routed(TT(rt[2], rt[2], rank, ALU.mult))
            routed(dve.tensor_reduce(best_rank, rt[2], mybir.AxisListType.X, ALU.max))
            routed(TT(rt[2], rt[2], bc(best_rank), ALU.is_equal))
            dve.wait_ge(s["route_exp"], 1)
            routed(dve.tensor_reduce(esum, rt[1], mybir.AxisListType.X, ALU.add))
            routed(dve.reciprocal(gate, esum))
            routed(dve.tensor_copy(grt[:, :], gate))
            dve.wait_ge(s["count_ps"], 1)
            tot = bank[1][:, 0:HID].rearrange("p (k e) -> p e k", e=EXPERTS)
            cnt, nslots, ends, first, _, _ = (by_exp[:, i, :] for i in range(6))
            routed(dve.tensor_reduce(cnt, tot, mybir.AxisListType.X, ALU.add))
            routed(TS(by_exp_i[:, :], cnt, float(P - 1), None, ALU.add))
            routed(TS(by_exp_i[:, :], by_exp_i[:, :], 7, None, ALU.logical_shift_right))
            routed(dve.tensor_copy(nslots, by_exp_i[:, :]))
            routed(dve.tensor_tensor_scan(ends, ones[:, 0:1].to_broadcast([P, EXPERTS]), nslots, 0.0, ALU.mult, ALU.add))
            routed(TT(first, ends, nslots, ALU.subtract))
            routed(TS(first, first, float(P), None, ALU.mult))
            dve.wait_ge(s["x1_stored"], 16 * TILES)
            se = x1[0:1, 0:2, :].rearrange("p k d -> p (k d)")[:, 0:SLOTS * EXPERTS].rearrange("p (s e) -> p s e", e=EXPERTS)
            routed(TT(se, ends[0:1, :].rearrange("p (o e) -> p o e", o=1).to_broadcast([1, SLOTS, EXPERTS]),
                      con[0:1, K_IOTA:K_IOTA + SLOTS].rearrange("p (k o) -> p k o", o=1).to_broadcast([1, SLOTS, EXPERTS]),
                      ALU.is_le))
            routed(dve.tensor_reduce(slot_sum[:, :], se, mybir.AxisListType.X, ALU.add))
            routed(TS(slot_e[:, :], slot_sum[:, :], float(EXPERTS - 1), None, ALU.min))
            for e in range(EXPERTS):
                last = dve.tensor_tensor_scan(rt[1][:, :, e], ones[:, 0:1].to_broadcast([P, NBLK]), tot[:, e, :],
                                              first[:, e:e + 1], ALU.mult, ALU.add)
            routed(last)
            routed(TT(rt[1], rt[1], bank[1][:, 0:HID].rearrange("p (k e) -> p k e", e=EXPERTS), ALU.subtract))
            routed(TT(rt[1], rt[1], bank[0][:, 0:HID].rearrange("p (k e) -> p k e", e=EXPERTS), ALU.add))
            routed(TT(rt[1], rt[1], rt[2], ALU.mult))
            routed(dve.tensor_reduce(pos, rt[1], mybir.AxisListType.X, ALU.add))
            routed(dve.tensor_copy(pos_i[:, 0, :], pos))
            routed(TS(pos_i[:, 1, :], pos_i[:, 0, :], 7, None, ALU.logical_shift_right))
            routed(TS(pos_i[:, 2, :], pos_i[:, 0, :], P - 1, None, ALU.bitwise_and))
            routed(dve.tensor_copy(slot_f, pos_i[:, 1, :]))
            routed(dve.tensor_copy(lane_f, pos_i[:, 2, :]))
            tok = con[:, K_TOK:K_TOK + NBLK]
            for g in range(NBLK // BLK):
                def bs(a):
                    return a[:, g * BLK:(g + 1) * BLK].rearrange("p (k o) -> p k o", o=1).to_broadcast([P, BLK, SP_])
                oh = place_hi[:, (g % 2) * BLK * SP_:(g % 2 + 1) * BLK * SP_].rearrange("p (k t) -> p k t", t=SP_)
                if g == 0:
                    routed(TT(gate_lo_t[:, :], gate, grt[:, :].bitcast(F32), ALU.subtract))
                routed(TT(oh, con[:, K_IOTA:K_IOTA + SP_].rearrange("p (o t) -> p o t", o=1).to_broadcast([P, BLK, SP_]),
                          bs(slot_f), ALU.is_equal))
                reuse(dve, s["place_ps"], (g - 1) * BLK)
                for v, val in enumerate((tok, gate, None)):
                    dst = slot_oh_all[:, (g % 2) * BLK:(g % 2 + 1) * BLK, v * SP_:(v + 1) * SP_]
                    if v < 2:
                        TT(dst, oh, bs(val), ALU.mult).then_inc(s["place_id"], 1)
                    else:
                        dve.wait_ge(s["place_id"], 3 * g + 2)
                        TT(dst, oh, bs(gate_lo_t[:, :]), ALU.mult).then_inc(s["place_id"], 1)
                for b in range(g * BLK, (g + 1) * BLK):
                    TS(lane_oh(b), con[:, K_IOTA:K_IOTA + P], lane_f[:, b:b + 1], None, ALU.is_equal).then_inc(s["place_oh"], 1)
            dve.wait_ge(s["place_ps"], NBLK)
            tok_ps = bank[2][:, 0:SLOTS]
            routed(TS(place_hi[:, 0:SLOTS], tok_ps, 0.0, float(2 * BATCH * SEQ), ALU.is_equal, ALU.mult))
            routed(STT(out=slot_idx[:, :], in0=tok_ps, scalar=-1.0, in1=place_hi[:, 0:SLOTS], op0=ALU.add, op1=ALU.add))
            routed(TS(slot_meta[:, :, 1], tok_ps, float(SEQ) + 0.5, None, ALU.is_gt))
            routed(dve.tensor_copy(slot_meta[:, :, 0], bank[2][:, SP_:SP_ + SLOTS]))
            routed(TT(slot_meta[:, :, 0], slot_meta[:, :, 0], bank[2][:, 2 * SP_:2 * SP_ + SLOTS], ALU.add))
            TT(gbt[:, 1, :], gbt[:, 1, :], gbt[:, 0, :], ALU.subtract).then_inc(s["place_done"], 1)
            for i in range(4):
                dve.wait_ge(s["we_hi_done"], i + 1)
                TT(w_lo[:, i * PIECE:(i + 1) * PIECE], stage[i][:, :, :].rearrange("p f t -> p (f t)"),
                   w_hi[:, i * PIECE:(i + 1) * PIECE].bitcast(F32), ALU.subtract).then_inc(s["we_lo_done"], 1)

            def low(t, i, r):
                dve.wait_ge(s["th_hi"], t + 1)
                reuse(dve, s["y_e_ps"], t - RING + 1)
                TT(hs_lo[r], bank[r][:, 0:HID], hs_hi[r].bitcast(F32), ALU.subtract).then_inc(s["th_lo"], 1)

            def finish(t, i, r):
                e = nc.values_load(slot_e[0:1, bass.ds(t, 1)], engines=[mybir.EngineType.DVE], min_val=0, max_val=EXPERTS - 1,
                                   skip_runtime_bounds_check_because="slot_e is a count of experts, at most EXPERTS - 1")
                dve.tensor_copy(meta_now[r][:, :], slot_meta[:, bass.ds(t, 1), :].rearrange("p o m -> p (o m)")).then_inc(s["meta_c"], 1)
                dve.wait_ge(s["meta_c"], t + 1)
                STT(out=gb_rows[r], in0=gbt[:, 1, :], scalar=meta_now[r][:, 1:2], in1=gbt[:, 0, :], op0=ALU.mult,
                    op1=ALU.add).then_inc(s["gb_row"], 1)
                dve.wait_ge(s["y_e_ps"], t + 1)
                TT(with_bias[r], bank[4 + r][:, 0:HID], ebt[:, bass.ds(e * HID, HID)], ALU.add).then_inc(s["y_e"], 1)
                dve.wait_ge(s["y_e"], t + 1)
                dve.wait_ge(s["gb_row"], t + 1)
                STT(out=with_bias[r], in0=with_bias[r], scalar=meta_now[r][:, 0:1], in1=gb_rows[r], op0=ALU.mult,
                    op1=ALU.mult).then_inc(s["scaled"], 1)
                dve.wait_ge(s["scaled"], t + 1)
                if not (isinstance(i, int) and i == 0):
                    dve.wait_ge(sc_done[r], 16 * i)
                TT(rows_out[r], with_bias[r], rows_in[r][:, HID:2 * HID], ALU.add).then_inc(s["fin"], 1)

            def body(t, i, r):
                if not (isinstance(t, int) and t == SLOTS - 1):
                    low(t + 1, i if r < RING - 1 else i + 1, (r + 1) % RING)
                finish(t, i, r)

            dve.wait_ge(s["ebias_in"], 16)
            low(0, 0, 0)
            slots(dve, body)

        @block.gpsimd
        def _(pool):
            TT = pool.tensor_tensor
            pool.memset(mhalf[:, :], -0.5).then_inc(s["mhalf_set"], 1)
            pool.wait_ge(s["mhalf_set"], 1)

            def rsqrt(n, dst, src, ready, done, per=1):
                pool.wait_ge(ready, count(n, per, per))
                TT(dst[:, :], src[:, :], mhalf[:, :], ALU.pow).then_inc(done, 1)

            rsqrt(0, rs1, ve1, s["ln1_ve"], s["ln1_rstd"], 6)

            def step(n, j, p):
                m = n - 1
                front, back = not is_last(n), not is_first(n)

                def low(dst, src, hi, ready, done):
                    for f in range(KC):
                        pool.wait_ge(ready, count(n, KC, f + 1))
                        TT(dst[:, f, :], src[:, f, :], hi[:, f, :].bitcast(F32), ALU.subtract).then_inc(done, 1)

                def split(c):
                    if not back:
                        return
                    pool.wait_ge(s["p_hi_done"], count(m, CHUNKS, c + 1))
                    TT(p_lo[:, c % 2, :], gated[:, c % 2, :], p_hi[:, c % 2, :].bitcast(F32),
                       ALU.subtract).then_inc(s["p_lo_done"], 1)

                if front:
                    rsqrt(n, rms1, mse1, s["ms1"], s["rms1_ready"])
                split(0)
                if front:
                    low(a_lo, hn[:, :, HALO:], a_hi, s["hn_hi"], s["hn_lo"])
                split(1)
                if front:
                    for f in range(KC):
                        pool.wait_ge(s["v_ready"], count(n, KC, f + 1))
                        pool.wait_ge(s["k_ready"], count(n, KC, f + 1))
                        TT(kvb[:, f, :], kb[:, f, :], vb[:, f, :], ALU.mult).then_inc(s["kv_ready"], 1)
                    low(s_lo, cbuf, s_hi, s["s_hi_done"], s["s_lo_done"])
                split(2)
                if front:
                    pool.wait_ge(s["carry"], count(n, 2 * KC, KC))
                    for f in range(KC):
                        TT(kb[:, f, :], kb[:, f, :], qb[:, f, :], ALU.mult).then_inc(s["qk"], 1)
                    low(l_lo, cbuf, l_hi, s["loc_hi"], s["loc_lo"])
                split(3)
                if front:
                    pool.wait_ge(s["carry"], count(n, 2 * KC, 2 * KC))
                    for f in range(KC):
                        TT(kvb[:, f, :], kvb[:, f, :], qb[:, f, :], ALU.mult).then_inc(s["qv"], 1)
                split(4)
                split(5)
                if front:
                    low(a_lo, kvb, a_hi, s["o_hi"], s["o_lo"])
                    for f in range(KC):
                        pool.wait_ge(s["o_lo"], count(n, KC, f + 1))
                        TT(kvb[:, f, :], kvb[:, f, :], vb[:, f, :], ALU.subtract).then_inc(s["dgate"], 1)
                    low(s_lo, kvb, s_hi, s["o2_hi"], s["o2_lo"])
                if back:
                    rsqrt(m, rs2, ve2, s["ln2_ve"], s["ln2_rstd"], 6)
                if front:
                    low(t_lo, qb, t_hi, s["att_hi"], s["att_lo"])
                    for f in range(KC):
                        if f == 0:
                            pool.wait_ge(s["att_lo"], count(n, KC, KC))
                            pool.wait_ge(s["loc_lo"], count(n, KC, KC))
                        TT(cbuf[:, f, :], cbuf[:, f, :], qb[:, f, :], ALU.subtract).then_inc(s["dmix"], 1)
                    pool.wait_ge(s["dmix"], count(n, KC, KC))
                    for f in range(KC):
                        TT(qb[:, f, :], qb[:, f, :], h[:, f, :], ALU.add).then_inc(s["hatt"], 1)
                if back:
                    q = 1 - p
                    pool.wait_ge(s["xn2"], count(m, BLK, BLK))
                    TT(ht[:, :, :], ht[:, :, :], cbt[:, q:q + 1, :].to_broadcast([P, BLK, HID]), ALU.mult).then_inc(s["ht_mul"], 1)
                    pool.wait_ge(s["ht_mul"], count(m, 1, 1))
                    TT(ht[:, :, :], ht[:, :, :], sbt[:, q:q + 1, :].to_broadcast([P, BLK, HID]), ALU.add).then_inc(s["ht_add"], 1)
                if front:
                    if has_next(n):
                        rsqrt(n + 1, rs1, ve1, s["ln1_ve"], s["ln1_rstd"], 6)
                    rsqrt(n, rms2, mse2, s["ms2"], s["rms2_ready"])
                    low(n_lo, kb, n_hi, s["hn2_hi"], s["hn2_lo"])

            pipeline(pool, step)

            h1 = rec
            for r in range(RING):
                pool.memset(rows_in[r], 0.0).then_inc(s["g_clear"], 1)
            pool.wait_ge(s["g_clear"], RING)
            pool.wait_ge(s["h_stored"], 16 * TILES)
            pool.wait_ge(s["x1_stored"], 16 * TILES)
            pool.wait_ge(s["place_done"], 1)

            def gather(t):
                r = t % RING
                reuse(pool, s["fin"], t - RING + 1)
                pool.indirect_dma_start(out=rows_in[r], out_offset=None, in_=rec,
                                        in_offset=bass.IndirectOffsetOnAxis(ap=slot_idx[:, t:t + 1], axis=0),
                                        bounds_check=BATCH * SEQ - 1, oob_is_err=False).then_inc(g_in[r], 16)

            gather(0)
            gather(1)
            for t in range(SLOTS):
                if t + 2 < SLOTS:
                    gather(t + 2)
                pool.wait_ge(s["fin"], t + 1)
                pool.indirect_dma_start(out=out.rearrange("b t d -> (b t) d"),
                                        out_offset=bass.IndirectOffsetOnAxis(ap=slot_idx[:, t:t + 1], axis=0),
                                        in_=rows_out[t % RING], in_offset=None,
                                        bounds_check=BATCH * SEQ - 1, oob_is_err=False).then_inc(sc_done[t % RING], 16)


def kernel(L0_attn_x, L0_attn_qkv_w, L0_attn_out_proj_w, L0_attn_out_gate_w, L0_attn_out_gate_b, L0_attn_decay_param,
           L0_attn_conv_w, L0_attn_conv_b, L0_attn_pw_w, L0_attn_gate_w, L0_attn_w1, L0_attn_w2, L0_attn_w3,
           L0_attn_norm1_w, L0_attn_norm2_w, L0_ffn_router_w, L0_ffn_router_b, L0_ffn_expert_w, L0_ffn_expert_b,
           L0_c, L0_wmod):
    import numpy as np
    import concourse.bacc as bacc
    from concourse.bass_utils import run_bass_kernel_spmd

    def rows(a, pad_to=None):
        t = np.asarray(a).T
        if pad_to:
            full = np.zeros(pad_to, t.dtype)
            full[:t.shape[0], :t.shape[1]] = t
            t = full
        return t.reshape(t.shape[0] // P, P, t.shape[1]).transpose(1, 0, 2).reshape(P, -1)

    def cols(v):
        return np.asarray(v).reshape(KC, P).T

    wall = np.ascontiguousarray(np.concatenate([
        rows(L0_attn_qkv_w), rows(L0_attn_pw_w), rows(L0_attn_out_gate_w), rows(L0_attn_out_proj_w), rows(L0_attn_gate_w),
        rows(L0_attn_w1, (HID, INTER_PAD)), rows(L0_attn_w2, (HID, INTER_PAD)), rows(L0_attn_w3, (INTER_PAD, HID))], axis=1))
    wexp = np.ascontiguousarray(np.asarray(L0_ffn_expert_w).reshape(EXPERTS, KC, P, HID).transpose(2, 0, 1, 3)
                                .reshape(P, EXPERTS * KC * HID))
    wmod = np.ascontiguousarray(np.asarray(L0_wmod).reshape(KC, P, 6 * HID).transpose(1, 0, 2))
    params = np.ascontiguousarray(np.concatenate([
        cols(L0_attn_norm1_w), cols(L0_attn_norm2_w),
        np.asarray(L0_attn_conv_w).reshape(KC, P, TAPS).transpose(1, 0, 2).reshape(P, KC * TAPS),
        cols(L0_attn_conv_b), cols(L0_attn_out_gate_b), cols(np.repeat(np.asarray(L0_attn_decay_param), HID // HEADS)),
        np.asarray(L0_c).reshape(BATCH, KC, P).transpose(2, 1, 0).reshape(P, KC * BATCH),
        np.asarray(L0_ffn_router_w).reshape(KC, P, EXPERTS).transpose(1, 0, 2).reshape(P, KC * EXPERTS),
        np.broadcast_to(np.asarray(L0_ffn_router_b), (P, EXPERTS))], axis=1))
    consts = np.zeros((P, K_COLS), np.float32)
    consts[:, K_ID:K_ID + P] = np.eye(P)
    per_head = HID // HEADS
    for f in range(KC):
        for r in range(P):
            head = (f * P + r) // per_head
            consts[r, K_HS + f * HEADS + head] = 1.0
            for b in range(BLK):
                consts[b * HEADS + head, K_HX + f * P + r] = 1.0
    consts[:, K_TRI:K_TRI + P] = np.triu(np.ones((P, P)), 1)
    consts[:, K_IOTA:K_IOTA + P] = np.arange(P)
    consts[:, K_RANK:K_RANK + EXPERTS] = EXPERTS - np.arange(EXPERTS)
    consts[:, K_TOK:] = 1 + np.arange(NBLK) * P + np.arange(P)[:, None]
    ebias = np.ascontiguousarray(np.broadcast_to(np.asarray(L0_ffn_expert_b).reshape(1, -1), (P, EXPERTS * HID)))

    arrays = {"x": np.ascontiguousarray(L0_attn_x), "wall": wall, "wexp": wexp, "wmod": wmod, "params": params,
              "consts": consts, "ebias": ebias}
    nc = bacc.Bacc("TRN2", target_bir_lowering=False, num_devices=1)
    aps = [nc.dram_tensor(f"in_{k}", a.shape, F32, kind="ExternalInput").ap() for k, a in arrays.items()]
    out = nc.dram_tensor("out_0", (BATCH, SEQ, HID), F32, kind="ExternalOutput").ap()
    rec = nc.dram_tensor("rec", (BATCH * SEQ, 2 * HID), F32, kind="Internal").ap()
    build(nc, *aps, out, rec)
    r = run_bass_kernel_spmd(nc, [{f"in_{k}": a for k, a in arrays.items()}], core_ids=[0])
    return r.results[0]["out_0"]
```

```python
from contextlib import ExitStack

import concourse.bass as bass
from concourse import mybir

ALU = mybir.AluOpType
ACT = mybir.ActivationFunctionType
F32 = mybir.dt.float32
F32R = mybir.dt.float32r
P = 128

BATCH, SEQ, HID = 2, 2048, 256
KC = HID // P
HEADS, TAPS, INTER, EXPERTS = 8, 4, 704, 8
TILE = 512
BLK = TILE // P
TILES = BATCH * SEQ // TILE
CHUNKS = -(-INTER // P)
INTER_PAD = CHUNKS * P
HALO = TAPS - 1
LN_EPS, RMS_EPS = 1e-5, 1e-6

W_QKV = 0
W_PW = W_QKV + KC * 3 * HID
W_GATE = W_PW + KC * HID
W_OUT = W_GATE + KC * HID
W_MIX = W_OUT + KC * HID
W_1 = W_MIX + 2 * KC * HID
W_2 = W_1 + KC * INTER_PAD
W_3 = W_2 + KC * INTER_PAD
W_COLS = W_3 + CHUNKS * HID
PIECE = KC * TILE

C_N1, C_N2, C_CW, C_CB, C_GB, C_DEC, C_C, C_RW, C_RB = 0, 2, 4, 12, 14, 16, 18, 22, 38
C_COLS = 46
K_ID, K_HS, K_HX = 0, 128, 144
K_TRI = K_HX + 2 * P
K_IOTA = K_TRI + P
K_RANK = K_IOTA + P
K_TOK = K_RANK + EXPERTS
K_COLS = K_TOK + BATCH * SEQ // P

NBLK = BATCH * SEQ // P
SLOTS = NBLK + EXPERTS - 1
RING = 3
GROUPS = SLOTS // RING
assert SLOTS == RING * GROUPS


def count(n, per, k):
    return per * n + k


def reuse(eng, sem, value):
    if isinstance(value, int) and value <= 0:
        return
    eng.wait_ge(sem, value)


def build(nc, x, wall, wexp, wmod, params, consts, ebias, out, rec):
    with ExitStack() as ctx:
        def sb(name, shape, dt=F32):
            return ctx.enter_context(nc.sbuf_tensor(name, shape, dt))

        def sem(name):
            return ctx.enter_context(nc.semaphore(name))

        bank = [ctx.enter_context(nc.psum_tensor(f"bank{i}", [P, TILE], F32)) for i in range(8)]
        small = bank[3]

        w_hi, w_lo = sb("w_hi", [P, W_COLS], F32R), sb("w_lo", [P, W_COLS], F32R)
        par, con = sb("par", [P, C_COLS]), sb("con", [P, K_COLS])
        ident = con[:, K_ID:K_ID + P]
        head_sum = con[:, K_HS:K_HS + 16].rearrange("p (f h) -> p f h", f=KC)
        head_spread = con[0:32, K_HX:K_HX + 2 * P].rearrange("p (f m) -> p f m", f=KC)
        ones = sb("ones", [P, 2])
        xln_all = sb("xln", [P, 2, BLK, HID])
        xln = [xln_all[:, p] for p in range(2)]
        xn = sb("xn", [P, BLK, HID])
        h = [sb(f"h{p}", [P, KC, TILE]) for p in range(2)]
        esq = sb("esq", [P, KC, TILE])
        hn = sb("hn", [P, KC, HALO + TILE])
        halo = [sb(f"halo{p}", [P, KC, HALO]) for p in range(2)]
        a_hi, a_lo = sb("a_hi", [P, KC, TILE], F32R), sb("a_lo", [P, KC, TILE], F32R)
        s_hi, s_lo = sb("s_hi", [P, KC, TILE], F32R), sb("s_lo", [P, KC, TILE], F32R)
        l_hi, l_lo = sb("l_hi", [P, KC, TILE], F32R), sb("l_lo", [P, KC, TILE], F32R)
        t_hi, t_lo = sb("t_hi", [P, KC, TILE], F32R), sb("t_lo", [P, KC, TILE], F32R)
        n_hi, n_lo = sb("n_hi", [P, KC, TILE], F32R), sb("n_lo", [P, KC, TILE], F32R)
        p_hi, p_lo = sb("p_hi", [P, 2, TILE], F32R), sb("p_lo", [P, 2, TILE], F32R)
        cbuf = sb("cbuf", [P, KC, TILE])
        th = sb("th", [P, KC, TILE])
        qb, kb = sb("qb", [P, KC, TILE]), sb("kb", [P, KC, TILE])
        vb, kvb = sb("vb", [P, KC, TILE]), sb("kvb", [P, KC, TILE])
        x2 = sb("x2", [P, KC, TILE])
        tha = sb("tha", [P, 2, TILE])
        gated = sb("gated", [P, 2, TILE])
        x1 = sb("x1", [P, BLK, HID])
        ht = sb("ht", [P, BLK, HID])
        hT = sb("hT", [P, KC, TILE])
        logits = sb("logits", [P, BATCH, SEQ // P, EXPERTS])
        bn1, bn2 = sb("bn1", [P, BLK, 6]), sb("bn2", [P, BLK, 6])
        sm1, sm2 = sb("sm1", [P, BLK]), sb("sm2", [P, BLK])
        dm1, dm2 = sb("dm1", [P, BLK]), sb("dm2", [P, BLK])
        ve1, ve2 = sb("ve1", [P, BLK]), sb("ve2", [P, BLK])
        rs1, rs2 = sb("rs1", [P, BLK]), sb("rs2", [P, BLK])
        nm1, nm2 = sb("nm1", [P, BLK]), sb("nm2", [P, BLK])
        mse1, mse2 = sb("mse1", [P, BLK]), sb("mse2", [P, BLK])
        rms1, rms2 = sb("rms1", [P, BLK]), sb("rms2", [P, BLK])
        mhalf = sb("mhalf", [P, BLK])
        den = sb("den", [P, BLK, HEADS])
        rec_tok = sb("rec_tok", [P, 160])
        rec_diag = rec_tok[:, :].rearrange("p (b c) -> p b c", c=40)[:, :, 0:HEADS]
        recT = sb("recT", [32, TILE])
        dec = sb("dec", [P, KC])
        kss_c = [sb(f"kss_c{p}", [P, KC]) for p in range(2)]
        kvs_c = [sb(f"kvs_c{p}", [P, KC]) for p in range(2)]
        csil = sb("csil", [P, KC * BATCH])
        cth = sb("cth", [P, KC * BATCH])
        hgb = sb("hgb", [P, KC])
        mod = sb("mod", [P, 6, BATCH])
        mods = sb("mods", [P, 2, BATCH])
        sbt = sb("sbt", [P, BATCH, HID])
        cbt = sb("cbt", [P, BATCH, HID])
        gbt = sb("gbt", [P, BATCH, HID])

        names = """par_in con_in wmod_in hc_th hc_silu mod_ps mod_done prep w_hi_done w_lo_done ones_set mhalf_set
            ln1_bn ln1_mv ln1_ve ln1_rstd ln1_nm xn_ready t_ps h_ready sq_ready st1_ps ms1 rms1_ready r1_ps hn_ready hn_hi
            hn_lo halo_in conv k_ps q_ps v_ps ek ekm k_ready st1_read eq eqm q_ready v_ready kv_ready kss kvs carry
            ths s_ready s_hi_done s_lo_done l_ps loc loc_hi loc_lo qk den_ps den_max den_rec recT_ps recT_ready rec_ps
            qv o_ready o_hi o_lo g_ps thg dgate ugate o2 o2_hi o2_lo o_ps att att_hi att_lo m_ps thm dmix hatt umix
            x2_ready sq2 st2_ps ms2 rms2_ready r2_ps hn2 hn2_hi hn2_lo a_ps b_ps th_a gate_a prod p_hi_done p_lo_done
            f_ps w3_used x2g y_ready y_ps x1_ready ln2_bn ln2_mv ln2_ve ln2_rstd ln2_nm xn2 ht_mul ht_add hT_ps hT_ready
            lg_ps lg xres_in h_stored x1_stored
            ebias_in we_hi_done we_lo_done route route_exp count_ps place_oh place_id place_ps place_done g_clear tr_ps th_hi th_lo y_e_ps y_e scattered meta_c gb_row scaled fin""".split()
        s = {n: sem(n) for n in names}
        w_in = [sem(f"w_in{i}") for i in range(4)]
        x_in = [sem(f"x_in{p}") for p in range(2)]
        we_in = [sem(f"we_in{i}") for i in range(4)]
        g_in = [sem(f"g_in{r}") for r in range(RING)]
        sc_done = [sem(f"sc_done{r}") for r in range(RING)]

        x_flat = x.rearrange("b t d -> (b t d)")
        rec_flat = rec.rearrange("t d -> (t d)")
        stage = [qb, kb, vb, kvb]
        PIECES = [(a, min(PIECE, W_COLS - a)) for a in range(0, W_COLS, PIECE)]
        wm = [esq, cbuf, th]

        def w(t, base, kc, width, a, m=P):
            return t[:, base + kc * width + a:base + kc * width + a + m]

        WE_COLS = EXPERTS * KC * HID
        ebt = xln_all[:, :, :, :].rearrange("p a k d -> p (a k d)")
        rows_in = [cbuf[:, 0, :], cbuf[:, 1, :], th[:, 0, :]]
        hs_hi = [a_hi[:, :, :].rearrange("p f t -> p (f t)")[:, r * HID:(r + 1) * HID] for r in range(RING)]
        hs_lo = [a_lo[:, :, :].rearrange("p f t -> p (f t)")[:, r * HID:(r + 1) * HID] for r in range(RING)]
        rows_out = [hT[:, :, :].rearrange("p f t -> p (f t)")[:, r * HID:(r + 1) * HID] for r in range(RING)]
        with_bias = [esq[:, :, :].rearrange("p f t -> p (f t)")[:, r * HID:(r + 1) * HID] for r in range(RING)]
        gb_rows = [tha[:, :, :].rearrange("p f t -> p (f t)")[:, r * HID:(r + 1) * HID] for r in range(RING)]
        lall = logits[:, :, :, :].rearrange("p b k e -> p (b k) e")
        rt = [xn[:, i, :].rearrange("p (k e) -> p k e", e=EXPERTS) for i in range(BLK)]
        small_f, used = gated[:, :, :].rearrange("p f t -> p (f t)"), [0]
        INT = mybir.dt.int32

        def part(n):
            used[0] += n
            return small_f[:, used[0] - n:used[0]]

        by_blk = part(8 * NBLK).rearrange("p (i k) -> p i k", k=NBLK)
        by_exp = part(6 * EXPERTS).rearrange("p (i e) -> p i e", e=EXPERTS)
        by_exp_i = part(EXPERTS).bitcast(INT)
        pos_i = part(3 * NBLK).bitcast(INT).rearrange("p (i k) -> p i k", k=NBLK)
        gate_lo_t = part(NBLK)
        slot_meta = part(2 * SLOTS).rearrange("p (s m) -> p s m", m=2)
        slot_sum = part(SLOTS)[0:1, :]
        slot_e = part(SLOTS).bitcast(INT)[0:1, :]
        meta_now = [part(2) for r in range(RING)]
        slot_idx = part(SLOTS).bitcast(INT)
        grt = p_hi[:, 0, 0:NBLK]
        SP_ = 40
        place_hi = x1[:, :, :].rearrange("p k d -> p (k d)")
        assert NBLK * EXPERTS == HID
        gneg = xn[:, 0:BATCH, :]

        block = ctx.enter_context(nc.Block())

        def pipeline(eng, step):
            step(0, 0, 0)
            step(1, 0, 1)
            with eng.Fori(1, TILES // 2 - 1) as j:
                step(2 * j, j, 0)
                step(2 * j + 1, j, 1)
            for n in range(TILES - 2, TILES + 2):
                step(n, n // 2, n % 2)

        def has(n):
            return not isinstance(n, int) or 0 <= n < TILES

        def has_late(n):
            return not isinstance(n, int) or n >= 2

        def slots(eng, body):
            def group(i):
                for r in range(RING):
                    body(RING * i + r, i, r)
            group(0)
            with eng.Fori(1, GROUPS - 1) as i:
                group(i)
            group(GROUPS - 1)

        def is_first(n):
            return isinstance(n, int) and n == 0

        def tile_of(eng, flat, width, q, jq):
            at = q * SEQ * width + jq * (TILE * width)
            if not isinstance(at, int):
                at = eng.snap(at)
            return flat[bass.ds(at, TILE * width)].rearrange("(k p d) -> p k d", p=P, d=width)

        slot_oh_all = l_hi[:, :, :].rearrange("p f t -> p (f t)")[:, 0:2 * BLK * 3 * SP_].rearrange(
            "p (k v) -> p k v", v=3 * SP_)

        def slot_oh(b):
            return slot_oh_all[:, b % (2 * BLK), :]

        def lane_oh(b):
            return s_hi[:, :, :].rearrange("p f t -> p (f t)")[:, (b % 8) * P:(b % 8 + 1) * P]

        @block.sync
        def _(sp):
            sp.dma_start(xln[0][:, :, :], tile_of(sp, x_flat, HID, 0, 0)).then_inc(x_in[0], 16)
            sp.dma_start(par[:, :], params).then_inc(s["par_in"], 16)
            sp.dma_start(con[:, :], consts).then_inc(s["con_in"], 16)
            for i in range(3):
                sp.dma_start(wm[i][:, :, :], wmod[:, :, i * TILE:(i + 1) * TILE]).then_inc(s["wmod_in"], 16)
            for i, (a, m) in enumerate(PIECES):
                if i >= 4:
                    sp.wait_ge(s["w_lo_done"], i - 3)
                sp.dma_start(stage[i % 4][:, :, :].rearrange("p f t -> p (f t)")[:, 0:m],
                             wall[:, a:a + m]).then_inc(w_in[i % 4], 16)

            def step(n, j, p):
                if has(n + 1):
                    q, jq = (1, j) if p == 0 else (0, j + 1)
                    src = tile_of(sp, x_flat, HID, q, jq)
                    if not is_first(n):
                        sp.wait_ge(s["xn_ready"], count(n, BLK, 0))
                    sp.dma_start(xln[q][:, :, :], src).then_inc(x_in[q], 16)

            pipeline(sp, step)
            sp.wait_ge(s["xn_ready"], count(TILES - 1, BLK, BLK))
            sp.dma_start(ebt, ebias).then_inc(s["ebias_in"], 16)
            for i, (name, per) in enumerate((("x2_ready", KC), ("den_ps", 1), ("o2", KC), ("hn2_lo", KC))):
                sp.wait_ge(s[name], per * TILES)
                sp.dma_start(stage[i][:, :, :].rearrange("p f t -> p (f t)"),
                             wexp[:, i * PIECE:(i + 1) * PIECE]).then_inc(we_in[i], 16)
            for r in range(RING):
                sp.wait_ge(sc_done[r], 16 * GROUPS)

        @block.tensor
        def _(pe):
            mm = pe.matmul
            pe.wait_ge(s["hc_silu"], 2)
            pe.wait_ge(s["wmod_in"], 48)
            for i in range(6):
                for kc in range(KC):
                    a = i * P
                    mm(small[:, 2 * i:2 * i + 2], wm[a // TILE][:, kc, a % TILE:a % TILE + P],
                       csil[:, kc * BATCH:(kc + 1) * BATCH], start=kc == 0, stop=kc == 1)
            for b in range(BATCH):
                for kc in range(KC):
                    lhs = csil[:, kc * BATCH + b:kc * BATCH + b + 1].to_broadcast([P, P])
                    mm(bank[b][:, 0:256], lhs, wm[1][:, kc, 256:512], start=kc == 0, stop=kc == 1)
                for kc in range(KC):
                    lhs = csil[:, kc * BATCH + b:kc * BATCH + b + 1].to_broadcast([P, P])
                    last = mm(bank[4 + b][:, :], lhs, wm[2][:, kc, :], start=kc == 0, stop=kc == 1)
            last.then_inc(s["mod_ps"], 1)

            def product(out_, terms, done, start=True, stop=True):
                k, last_ = 0, None
                todo = [(wh, ah) for wh, wl, ah, al in terms] + [(wl, ah) for wh, wl, ah, al in terms] + [
                    (wh, al) for wh, wl, ah, al in terms]
                for k, (a, b) in enumerate(todo):
                    last_ = mm(out_, a, b, start=start and k == 0, stop=stop and k == len(todo) - 1)
                if done is not None:
                    last_.then_inc(done, 1)
                return last_

            def dense(out_, base, width, a, hi, lo, done):
                product(out_, [(w(w_hi, base, kc, width, a), w(w_lo, base, kc, width, a), hi[:, kc, :], lo[:, kc, :])
                               for kc in range(KC)], done)

            def rows_of(bk, col, done):
                for b in range(BLK):
                    last_ = mm(bk[:, b * P:(b + 1) * P], col[:, b:b + 1].to_broadcast([P, P]), ident, start=True, stop=True)
                last_.then_inc(done, 1)

            def sums(src, done):
                for b in range(BLK):
                    for f in range(KC):
                        last_ = mm(small[:, b:b + 1], src[:, f, b * P:(b + 1) * P], ones[:, 0:1],
                                   start=f == 0, stop=f == KC - 1)
                last_.then_inc(done, 1)

            def head_t(n):
                pe.wait_ge(s["xn_ready"], count(n, BLK, BLK))
                for f, bk in ((0, 0), (1, 2)):
                    if not is_first(n):
                        pe.wait_ge(s["loc" if f else "q_ready"], count(n - 1, KC, KC - f))
                    for b in range(BLK):
                        last_ = pe.transpose(bank[bk][:, b * P:(b + 1) * P], xn[:, b, f * P:(f + 1) * P], ident)
                    last_.then_inc(s["t_ps"], 1)

            def head_sums(n):
                pe.wait_ge(s["sq_ready"], count(n, KC, KC))
                if not is_first(n):
                    pe.wait_ge(s["recT_ready"], count(n - 1, 1, 1))
                sums(hn[:, :, HALO:], s["st1_ps"])

            def head_rows(n):
                pe.wait_ge(s["rms1_ready"], count(n, 1, 1))
                pe.wait_ge(s["h_ready"], count(n, KC, 1))
                if not is_first(n):
                    pe.wait_ge(s["o_ready"], count(n - 1, KC, KC))
                rows_of(bank[0], rms1, s["r1_ps"])

            def step(n, j, p):
                m, m2 = n - 1, n - 2
                front, back, late, head = has(n), has(m), has_late(n), has(n + 1)

                def chunk(c):
                    if not back:
                        return
                    if c == 0:
                        pe.wait_ge(s["hn2_hi"], count(m, KC, KC))
                        pe.wait_ge(s["hn2_lo"], count(m, KC, KC))
                        reuse(pe, s["x1_ready"], count(m, 2, 0))
                    else:
                        pe.wait_ge(s["gate_a"], count(m, CHUNKS, c))
                    dense(bank[6][:, :], W_1, INTER_PAD, c * P, n_hi, n_lo, s["a_ps"])
                    if c > 0:
                        pe.wait_ge(s["prod"], count(m, CHUNKS, c))
                    dense(bank[7][:, :], W_2, INTER_PAD, c * P, n_hi, n_lo, s["b_ps"])

                def w3(c):
                    if not back:
                        return
                    if c == 0 and late:
                        pe.wait_ge(s["hT_ready"], count(m2, KC, KC))
                    pe.wait_ge(s["p_hi_done"], count(m, CHUNKS, c + 1))
                    pe.wait_ge(s["p_lo_done"], count(m, CHUNKS, c + 1))
                    for f in range(KC):
                        product(bank[4 + f][:, :],
                                [(w(w_hi, W_3, c, HID, f * P), w(w_lo, W_3, c, HID, f * P),
                                  p_hi[:, c % 2, :], p_lo[:, c % 2, :])],
                                s["f_ps"] if c == CHUNKS - 1 and f == 0 else s["w3_used"] if f == 1 else None,
                                start=c == 0, stop=c == CHUNKS - 1)

                if front:
                    pe.wait_ge(s["hn_hi"], count(n, KC, KC))
                    pe.wait_ge(s["hn_lo"], count(n, KC, KC))
                    if is_first(n):
                        pe.wait_ge(s["w_lo_done"], -(-W_PW // PIECE))
                    else:
                        pe.wait_ge(s["att_hi"], count(m, KC, 1))
                    dense(bank[2][:, :], W_QKV, 3 * HID, HID, a_hi, a_lo, s["k_ps"])
                    reuse(pe, s["thm"], count(n, KC, -1))
                    dense(bank[1][:, :], W_QKV, 3 * HID, HID + P, a_hi, a_lo, s["k_ps"])
                    reuse(pe, s["thm"], count(n, KC, 0))
                    dense(bank[0][:, :], W_QKV, 3 * HID, 2 * HID, a_hi, a_lo, s["v_ps"])
                if back:
                    pe.wait_ge(s["sq2"], count(m, KC, KC))
                    if front:
                        pe.wait_ge(s["ms1"], count(n, 1, 1))
                    else:
                        pe.wait_ge(s["recT_ready"], count(m, 1, 1))
                    sums(kvb, s["st2_ps"])
                if front:
                    pe.wait_ge(s["k_ready"], count(n, KC, 1))
                    dense(bank[2][:, :], W_QKV, 3 * HID, 2 * HID + P, a_hi, a_lo, s["v_ps"])
                if back:
                    pe.wait_ge(s["rms2_ready"], count(m, 1, 1))
                    reuse(pe, s["y_ready"], count(m, KC, 0))
                    rows_of(bank[4], rms2, s["r2_ps"])
                if front:
                    pe.wait_ge(s["k_ready"], count(n, KC, 2))
                    dense(bank[1][:, :], W_QKV, 3 * HID, 0, a_hi, a_lo, s["q_ps"])
                    pe.wait_ge(s["v_ready"], count(n, KC, 1))
                    dense(bank[0][:, :], W_QKV, 3 * HID, P, a_hi, a_lo, s["q_ps"])
                chunk(0)
                chunk(1)
                if late:
                    pe.wait_ge(s["ht_add"], count(m2, 1, 1))
                    if back:
                        pe.wait_ge(s["hn2"], count(m, KC, KC))
                    for f in range(KC):
                        for b in range(BLK):
                            last_ = pe.transpose(bank[4 + f][:, b * P:(b + 1) * P], ht[:, b, f * P:(f + 1) * P], ident)
                        last_.then_inc(s["hT_ps"], 1)
                if front:
                    pe.wait_ge(s["s_hi_done"], count(n, KC, KC))
                    pe.wait_ge(s["s_lo_done"], count(n, KC, KC))
                    pe.wait_ge(s["v_ready"], count(n, KC, 2))
                    dense(bank[2][:, :], W_PW, HID, 0, s_hi, s_lo, s["l_ps"])
                    pe.wait_ge(s["q_ready"], count(n, KC, 1))
                    dense(bank[1][:, :], W_PW, HID, P, s_hi, s_lo, s["l_ps"])
                if late:
                    pe.wait_ge(s["hT_ready"], count(m2, KC, KC))
                    if back:
                        pe.wait_ge(s["ms2"], count(m, 1, 1))
                    for b in range(BLK):
                        for f in range(KC):
                            last_ = mm(small[:, b * EXPERTS:(b + 1) * EXPERTS], hT[:, f, b * P:(b + 1) * P],
                                       par[:, C_RW + f * EXPERTS:C_RW + (f + 1) * EXPERTS], start=f == 0, stop=f == KC - 1)
                    last_.then_inc(s["lg_ps"], 1)
                w3(0)
                chunk(2)
                if head:
                    head_t(n + 1)
                w3(1)
                if front:
                    pe.wait_ge(s["qk"], count(n, KC, KC))
                    if late:
                        pe.wait_ge(s["lg"], count(m2, 1, 1))
                    elif back:
                        pe.wait_ge(s["ms2"], count(m, 1, 1))
                    else:
                        pe.wait_ge(s["ms1"], 1)
                    for b in range(BLK):
                        for f in range(KC):
                            last_ = mm(small[:, b * HEADS:(b + 1) * HEADS], kb[:, f, b * P:(b + 1) * P],
                                       head_sum[:, f, :], start=f == 0, stop=f == KC - 1)
                    last_.then_inc(s["den_ps"], 1)
                chunk(3)
                if front:
                    pe.wait_ge(s["den_rec"], count(n, 1, 1))
                    for b in range(BLK):
                        last_ = pe.transpose(small[0:32, b * P:(b + 1) * P], rec_tok[:, 32 * b:32 * b + 32], ident)
                    last_.then_inc(s["recT_ps"], 1)
                w3(2)
                if front:
                    pe.wait_ge(s["recT_ready"], count(n, 1, 1))
                    pe.wait_ge(s["loc"], count(n, KC, KC))
                    mm(bank[1][:, :], head_spread[:, 0, :], recT[:, :], start=True, stop=True).then_inc(s["rec_ps"], 1)
                    if head:
                        pe.wait_ge(s["h_ready"], count(n + 1, KC, 1))
                    else:
                        pe.wait_ge(s["q_ready"], count(n, KC, KC))
                    mm(bank[0][:, :], head_spread[:, 1, :], recT[:, :], start=True, stop=True).then_inc(s["rec_ps"], 1)
                chunk(4)
                w3(3)
                if front:
                    pe.wait_ge(s["o_hi"], count(n, KC, KC))
                    pe.wait_ge(s["o_lo"], count(n, KC, KC))
                    if head:
                        pe.wait_ge(s["h_ready"], count(n + 1, KC, KC))
                    if is_first(n):
                        pe.wait_ge(s["w_lo_done"], len(PIECES))
                    dense(bank[2][:, :], W_GATE, HID, 0, t_hi, t_lo, s["g_ps"])
                    dense(bank[1][:, :], W_GATE, HID, P, t_hi, t_lo, s["g_ps"])
                chunk(5)
                w3(4)
                if head:
                    head_sums(n + 1)
                if front:
                    pe.wait_ge(s["o2_hi"], count(n, KC, KC))
                    pe.wait_ge(s["o2_lo"], count(n, KC, KC))
                    pe.wait_ge(s["thg"], count(n, KC, KC))
                    dense(bank[2][:, :], W_OUT, HID, 0, s_hi, s_lo, s["o_ps"])
                    dense(bank[1][:, :], W_OUT, HID, P, s_hi, s_lo, s["o_ps"])
                w3(5)
                if head:
                    head_rows(n + 1)
                if front:
                    pe.wait_ge(s["loc_hi"], count(n, KC, KC))
                    pe.wait_ge(s["loc_lo"], count(n, KC, KC))
                    pe.wait_ge(s["att_hi"], count(n, KC, KC))
                    pe.wait_ge(s["att_lo"], count(n, KC, KC))
                    for f, bk in ((0, 1), (1, 0)):
                        if f == 1 and head:
                            pe.wait_ge(s["hn_ready"], count(n + 1, KC, KC))
                        product(bank[bk][:, :],
                                [(w(w_hi, W_MIX, kc, HID, f * P), w(w_lo, W_MIX, kc, HID, f * P),
                                  (l_hi if kc < KC else t_hi)[:, kc % KC, :], (l_lo if kc < KC else t_lo)[:, kc % KC, :])
                                 for kc in range(2 * KC)], s["m_ps"])
                if back:
                    pe.wait_ge(s["y_ready"], count(m, KC, KC))
                    pe.wait_ge(s["prod"], count(m, CHUNKS, CHUNKS))
                    for i in range(2):
                        for b in range(2):
                            for f in range(KC):
                                last_ = pe.transpose(bank[6 + i][:, b * HID + f * P:b * HID + (f + 1) * P],
                                                     x2[:, f, (2 * i + b) * P:(2 * i + b + 1) * P], ident)
                        last_.then_inc(s["y_ps"], 1)

            pe.wait_ge(s["con_in"], 16)
            pe.wait_ge(s["mod_done"], 1)
            pe.wait_ge(s["ones_set"], 1)
            head_t(0)
            head_sums(0)
            head_rows(0)
            pipeline(pe, step)

            onehot = rt[2][:, :, :].rearrange("p k e -> p (k e)")
            pe.wait_ge(s["route"], 9)
            mm(bank[0][:, 0:HID], con[:, K_TRI:K_TRI + P], onehot, start=True, stop=True)
            mm(bank[1][:, 0:HID], ones[:, 0:1].to_broadcast([P, P]), onehot, start=True, stop=True).then_inc(s["count_ps"], 1)
            for b in range(NBLK):
                pe.wait_ge(s["place_oh"], b + 1)
                if b % BLK == 0:
                    pe.wait_ge(s["place_id"], 3 * (b // BLK + 1))
                mm(bank[2][:, 0:3 * SP_], lane_oh(b), slot_oh(b), start=b == 0, stop=b == NBLK - 1).then_inc(s["place_ps"], 1)

            def turn(t, i, r):
                pe.wait_ge(g_in[r], 16 * (i + 1))
                reuse(pe, s["th_lo"], t - RING + 1)
                for kc in range(KC):
                    last_ = pe.transpose(bank[r][:, kc * P:(kc + 1) * P], rows_in[r][:, kc * P:(kc + 1) * P], ident)
                last_.then_inc(s["tr_ps"], 1)

            def expert(t, i, r):
                e = nc.values_load(slot_e[0:1, bass.ds(t, 1)], engines=[mybir.EngineType.PE], min_val=0, max_val=EXPERTS - 1,
                                   skip_runtime_bounds_check_because="slot_e is a count of experts, at most EXPERTS - 1")
                pe.wait_ge(s["th_lo"], t + 1)
                pe.wait_ge(s["th_hi"], t + 1)
                reuse(pe, s["y_e"], t - RING + 1)
                k = 0
                for a, wt in ((hs_hi[r], w_hi), (hs_hi[r], w_lo), (hs_lo[r], w_hi)):
                    for kc in range(KC):
                        last_ = mm(bank[4 + r][:, 0:HID], a[:, kc * P:(kc + 1) * P],
                                   wt[:, bass.ds(e * (KC * HID) + kc * HID, HID)], start=k == 0, stop=k == 2 * KC + 1)
                        k += 1
                last_.then_inc(s["y_e_ps"], 1)

            def body(t, i, r):
                if not (isinstance(t, int) and t == SLOTS - 1):
                    turn(t + 1, i if r < RING - 1 else i + 1, (r + 1) % RING)
                if isinstance(t, int) and t == 0:
                    pe.wait_ge(s["we_lo_done"], 4)
                expert(t, i, r)

            pe.wait_ge(s["place_done"], 1)
            turn(0, 0, 0)
            slots(pe, body)

        @block.scalar
        def _(act):
            A = act.activation
            act.wait_ge(s["par_in"], 16)
            A(cth[:, :], par[:, C_C:C_C + 4], ACT.Tanh, scale=0.5).then_inc(s["hc_th"], 1)
            A(dec[:, :], par[:, C_DEC:C_DEC + KC], ACT.Tanh, scale=0.5).then_inc(s["hc_th"], 1)
            def norm1(n, p):
                act.wait_ge(s["ln1_nm"], count(n, 1, 1))
                reuse(act, s["t_ps"], count(n, KC, 0))
                for b in range(BLK):
                    A(xn[:, b, :], xln[p][:, b, :], ACT.Identity, scale=rs1[:, b:b + 1],
                      bias=nm1[:, b:b + 1]).then_inc(s["xn_ready"], 1)

            def head_h(n, p):
                for f, bk in ((0, 0), (1, 2)):
                    act.wait_ge(s["t_ps"], count(n, KC, f + 1))
                    if f == 0 and not (isinstance(n, int) and n < 2):
                        act.wait_ge(s["hatt"], count(n - 2, KC, KC))
                    A(h[p][:, f, :], bank[bk][:, :], ACT.Identity, scale=mod[:, 2 + f, p:p + 1],
                      bias=mod[:, f, p:p + 1]).then_inc(s["h_ready"], 1)

            def head_sq(n, p):
                reuse(act, s["conv"], count(n, KC * TAPS, 0))
                reuse(act, s["halo_in"], count(n, 2, 0))
                for f in range(KC):
                    act.wait_ge(s["h_ready"], count(n, KC, f + 1))
                    A(hn[:, f, HALO:], h[p][:, f, :], ACT.Square).then_inc(s["sq_ready"], 1)

            act.wait_ge(s["mod_done"], 1)
            norm1(0, 0)
            head_h(0, 0)
            head_sq(0, 0)
            for i, (a, m) in enumerate(PIECES):
                act.wait_ge(w_in[i % 4], 16 * (i // 4 + 1))
                A(w_hi[:, a:a + m], stage[i % 4][:, :, :].rearrange("p f t -> p (f t)")[:, 0:m],
                  ACT.Copy).then_inc(s["w_hi_done"], 1)

            def round_hi(n, dst, src, ready, done):
                for f in range(KC):
                    act.wait_ge(ready, count(n, KC, f + 1))
                    A(dst[:, f, :], src[:, f, :], ACT.Copy).then_inc(done, 1)

            round_hi(0, a_hi, hn[:, :, HALO:], s["hn_ready"], s["hn_hi"])

            def step(n, j, p):
                m, m2 = n - 1, n - 2
                front, back, late, head = has(n), has(m), has_late(n), has(n + 1)
                q, jq = (1, j - 1) if p == 0 else (0, j)

                def gate(c):
                    if not back:
                        return
                    act.wait_ge(s["a_ps"], count(m, CHUNKS, c + 1))
                    reuse(act, s["gate_a"], count(m, CHUNKS, c - 1))
                    A(tha[:, c % 2, :], bank[6][:, :], ACT.Tanh, scale=0.5).then_inc(s["th_a"], 1)

                def split(c):
                    if not back:
                        return
                    act.wait_ge(s["prod"], count(m, CHUNKS, c + 1))
                    reuse(act, s["w3_used"], count(m, CHUNKS, c - 1))
                    A(p_hi[:, c % 2, :], gated[:, c % 2, :], ACT.Copy).then_inc(s["p_hi_done"], 1)

                if back:
                    for f, bk in ((0, 1), (1, 0)):
                        act.wait_ge(s["m_ps"], count(m, KC, f + 1))
                        A(th[:, f, :], bank[bk][:, :], ACT.Tanh, scale=0.5).then_inc(s["thm"], 1)
                    act.wait_ge(s["o2_lo"], count(m, KC, KC))
                    for f in range(KC):
                        act.wait_ge(s["x2_ready"], count(m, KC, f + 1))
                        A(kvb[:, f, :], x2[:, f, :], ACT.Square).then_inc(s["sq2"], 1)
                if front:
                    for f, bk in ((0, 2), (1, 1)):
                        act.wait_ge(s["k_ps"], count(n, KC, f + 1))
                        A(esq[:, f, :], bank[bk][:, :], ACT.Exp).then_inc(s["ek"], 1)
                    for f, bk in ((0, 0), (1, 2)):
                        act.wait_ge(s["v_ps"], count(n, KC, f + 1))
                        A(vb[:, f, :], bank[bk][:, :], ACT.Copy).then_inc(s["v_ready"], 1)
                    act.wait_ge(s["k_ready"], count(n, KC, 2))
                    act.wait_ge(s["q_ps"], count(n, KC, 1))
                    A(esq[:, 0, :], bank[1][:, :], ACT.Exp).then_inc(s["eq"], 1)
                if back:
                    round_hi(m, n_hi, kvb, s["hn2"], s["hn2_hi"])
                if late:
                    dst = tile_of(act, rec_flat, 2 * HID, p, j - 1)
                    act.wait_ge(s["ln2_nm"], count(m2, 1, 1))
                    act.wait_ge(s["x1_ready"], count(m2, 2, 2))
                    act.dma_start(dst[:, :, HID:2 * HID], x1[:, :, :]).then_inc(s["x1_stored"], 16)
                    for b in range(BLK):
                        A(ht[:, b, :], x1[:, b, :], ACT.Identity, scale=rs2[:, b:b + 1],
                          bias=nm2[:, b:b + 1]).then_inc(s["xn2"], 1)
                if front:
                    act.wait_ge(s["q_ps"], count(n, KC, 2))
                    A(esq[:, 1, :], bank[0][:, :], ACT.Exp).then_inc(s["eq"], 1)
                gate(0)
                if front:
                    for f in range(KC):
                        act.wait_ge(s["conv"], count(n, KC * TAPS, KC * (TAPS - 1) + f + 1))
                        A(th[:, f, :], cbuf[:, f, :], ACT.Tanh, scale=0.5).then_inc(s["ths"], 1)
                split(0)
                if front:
                    round_hi(n, s_hi, cbuf, s["s_ready"], s["s_hi_done"])
                gate(1)
                if late:
                    for f in range(KC):
                        act.wait_ge(s["hT_ps"], count(m2, KC, f + 1))
                        A(hT[:, f, :], bank[4 + f][:, :], ACT.Copy).then_inc(s["hT_ready"], 1)
                    act.dma_start(dst[:, :, 0:HID], ht[:, :, :]).then_inc(s["h_stored"], 16)
                split(1)
                if front:
                    for f, bk in ((0, 2), (1, 1)):
                        act.wait_ge(s["l_ps"], count(n, KC, f + 1))
                        A(cbuf[:, f, :], bank[bk][:, :], ACT.Copy, scale=0.5).then_inc(s["loc"], 1)
                if head:
                    norm1(n + 1, 1 - p)
                gate(2)
                if front:
                    round_hi(n, l_hi, cbuf, s["loc"], s["loc_hi"])
                split(2)
                if head:
                    head_h(n + 1, 1 - p)
                gate(3)
                if front:
                    act.wait_ge(s["recT_ps"], count(n, 1, 1))
                    A(recT[:, :], small[0:32, :], ACT.Copy).then_inc(s["recT_ready"], 1)
                split(3)
                if head:
                    head_sq(n + 1, 1 - p)
                if back:
                    for f in range(KC):
                        act.wait_ge(s["hn2"], count(m, KC, f + 1))
                        A(x2[:, f, :], x2[:, f, :], ACT.Copy, scale=mod[:, 4 + f, q:q + 1]).then_inc(s["x2g"], 1)
                gate(4)
                if front:
                    round_hi(n, t_hi, kvb, s["o_ready"], s["o_hi"])
                split(4)
                if back:
                    src = tile_of(act, x_flat, HID, q, jq)
                    if late:
                        act.wait_ge(s["x1_stored"], count(m2, 16, 16))
                        act.wait_ge(s["h_stored"], count(m2, 16, 16))
                    act.dma_start(x1[:, :, :], src).then_inc(s["xres_in"], 16)
                if front:
                    for f, bk in ((0, 2), (1, 1)):
                        act.wait_ge(s["g_ps"], count(n, KC, f + 1))
                        A(th[:, f, :], bank[bk][:, :], ACT.Tanh, scale=0.5, bias=hgb[:, f:f + 1]).then_inc(s["thg"], 1)
                gate(5)
                if front:
                    round_hi(n, s_hi, kvb, s["o2"], s["o2_hi"])
                split(5)
                if front:
                    for f, bk in ((0, 2), (1, 1)):
                        act.wait_ge(s["o_ps"], count(n, KC, f + 1))
                        A(qb[:, f, :], bank[bk][:, :], ACT.Copy).then_inc(s["att"], 1)
                        A(t_hi[:, f, :], bank[bk][:, :], ACT.Copy).then_inc(s["att_hi"], 1)
                if head:
                    round_hi(n + 1, a_hi, hn[:, :, HALO:], s["hn_ready"], s["hn_hi"])

            pipeline(act, step)
            act.wait_ge(s["route"], 2)
            A(rt[1], rt[0], ACT.Exp).then_inc(s["route_exp"], 1)
            for i in range(4):
                act.wait_ge(we_in[i], 16)
                A(w_hi[:, i * PIECE:(i + 1) * PIECE], stage[i][:, :, :].rearrange("p f t -> p (f t)"),
                  ACT.Copy).then_inc(s["we_hi_done"], 1)

            def body(t, i, r):
                act.wait_ge(s["tr_ps"], t + 1)
                reuse(act, s["y_e_ps"], t - RING + 1)
                A(hs_hi[r], bank[r][:, 0:HID], ACT.Copy).then_inc(s["th_hi"], 1)

            slots(act, body)

        @block.vector
        def _(dve):
            TT, TS, STT = dve.tensor_tensor, dve.tensor_scalar, dve.scalar_tensor_tensor
            dve.memset(ones[:, :], 1.0).then_inc(s["ones_set"], 1)
            dve.memset(rec_tok[:, :], 0.0).then_inc(s["prep"], 1)
            for p in range(2):
                dve.memset(halo[p][:, :, :], 0.0).then_inc(s["prep"], 1)
                dve.memset(kss_c[p][:, :], 0.0).then_inc(s["prep"], 1)
                dve.memset(kvs_c[p][:, :], 0.0).then_inc(s["prep"], 1)
            dve.wait_ge(s["hc_th"], 1)
            STT(out=csil[:, :], in0=cth[:, :], scalar=1.0, in1=par[:, C_C:C_C + 4], op0=ALU.add,
                op1=ALU.mult).then_inc(s["hc_silu"], 1)
            dve.wait_ge(s["hc_silu"], 1)
            TS(csil[:, :], csil[:, :], 0.5, None, ALU.mult).then_inc(s["hc_silu"], 1)
            dve.wait_ge(s["hc_th"], 2)
            TS(dec[:, :], dec[:, :], 0.5, 0.5, ALU.mult, ALU.add).then_inc(s["prep"], 1)
            dve.wait_ge(s["prep"], 8)
            TS(dec[:, :], dec[:, :], 1e-8, None, ALU.max).then_inc(s["prep"], 1)
            TS(hgb[:, :], par[:, C_GB:C_GB + KC], 0.5, None, ALU.mult).then_inc(s["prep"], 1)

            def stats(n, xt, bn, sm, dm, ve, stat, comb):
                for b in range(BLK):
                    dve.bn_stats(bn[:, b, :], xt[:, b, :]).then_inc(stat, 1)
                dve.wait_ge(stat, count(n, BLK, BLK))
                TT(sm[:, :], bn[:, :, 1], bn[:, :, 4], ALU.add).then_inc(comb, 1)
                TT(dm[:, :], bn[:, :, 1], bn[:, :, 4], ALU.subtract).then_inc(comb, 1)
                TT(ve[:, :], bn[:, :, 2], bn[:, :, 5], ALU.add).then_inc(comb, 1)
                dve.wait_ge(comb, count(n, 6, 2))
                STT(out=dm[:, :], in0=dm[:, :], scalar=0.25, in1=dm[:, :], op0=ALU.mult, op1=ALU.mult).then_inc(comb, 1)
                dve.wait_ge(comb, count(n, 6, 3))
                TS(ve[:, :], ve[:, :], 1.0 / HID, LN_EPS, ALU.mult, ALU.add).then_inc(comb, 1)
                dve.wait_ge(comb, count(n, 6, 5))
                TT(ve[:, :], ve[:, :], dm[:, :], ALU.add).then_inc(comb, 1)

            def stats1(n, j, p):
                dve.wait_ge(x_in[p], count(j, 16, 16))
                stats(n, xln[p], bn1, sm1, dm1, ve1, s["ln1_bn"], s["ln1_ve"])

            def neg_mean(n, sm, rs, nm, ready, done):
                dve.wait_ge(ready, count(n, 1, 1))
                STT(out=nm[:, :], in0=sm[:, :], scalar=-0.5, in1=rs[:, :], op0=ALU.mult, op1=ALU.mult).then_inc(done, 1)

            stats1(0, 0, 0)
            neg_mean(0, sm1, rs1, nm1, s["ln1_rstd"], s["ln1_nm"])
            dve.wait_ge(s["mod_ps"], 1)
            TS(mod[:, 0:2, :], small[:, 0:4].rearrange("p (i b) -> p i b", b=2), 0.0, None, ALU.add).then_inc(s["prep"], 1)
            TS(mod[:, 2:4, :], small[:, 4:8].rearrange("p (i b) -> p i b", b=2), 1.0, None, ALU.add).then_inc(s["prep"], 1)
            ga = small[:, 8:12].rearrange("p (i b) -> p i b", b=2)
            TS(mods[:, :, :], ga, -1.0, None, ALU.mult).then_inc(s["prep"], 1)
            TS(mod[:, 4:6, :], ga, 0.0, 2.0, ALU.is_ge, ALU.mult).then_inc(s["prep"], 1)
            for b in range(BATCH):
                dve.tensor_copy(sbt[:, b, :], bank[b][:, 0:HID]).then_inc(s["prep"], 1)
                TS(cbt[:, b, :], bank[4 + b][:, 0:HID], 1.0, None, ALU.add).then_inc(s["prep"], 1)
                TS(gneg[:, b, :], bank[4 + b][:, HID:], -1.0, None, ALU.mult).then_inc(s["prep"], 1)
                TS(gbt[:, b, :], bank[4 + b][:, HID:], 0.0, 2.0, ALU.is_ge, ALU.mult).then_inc(s["prep"], 1)
            dve.wait_ge(s["prep"], 22)
            STT(out=mods[:, :, :], in0=ga, scalar=0.25, in1=mods[:, :, :], op0=ALU.max, op1=ALU.max).then_inc(s["prep"], 1)
            for b in range(BATCH):
                STT(out=gneg[:, b, :], in0=bank[4 + b][:, HID:], scalar=0.25, in1=gneg[:, b, :], op0=ALU.max,
                    op1=ALU.max).then_inc(s["prep"], 1)
            dve.wait_ge(s["prep"], 25)
            STT(out=mod[:, 4:6, :], in0=mod[:, 4:6, :], scalar=-1.0, in1=mods[:, :, :], op0=ALU.add,
                op1=ALU.mult).then_inc(s["prep"], 1)
            STT(out=gbt[:, :, :], in0=gbt[:, :, :], scalar=-1.0, in1=gneg, op0=ALU.add, op1=ALU.mult).then_inc(s["mod_done"], 1)

            def rms1_in(n):
                dve.wait_ge(s["st1_ps"], count(n, 1, 1))
                TS(mse1[:, :], small[:, 0:BLK], 1.0 / HID, RMS_EPS, ALU.mult, ALU.add).then_inc(s["ms1"], 1)

            def norm_h(n, p):
                if is_first(n):
                    dve.wait_ge(s["prep"], 7)
                dve.tensor_copy(hn[:, :, 0:HALO], halo[p][:, :, :]).then_inc(s["halo_in"], 1)
                dve.wait_ge(s["r1_ps"], count(n, 1, 1))
                for f in range(KC):
                    STT(out=hn[:, f, HALO:], in0=h[p][:, f, :], scalar=par[:, C_N1 + f:C_N1 + f + 1], in1=bank[0][:, :],
                        op0=ALU.mult, op1=ALU.mult).then_inc(s["hn_ready"], 1)
                dve.wait_ge(s["hn_ready"], count(n, KC, KC))
                dve.wait_ge(s["halo_in"], count(n, 2, 1))
                dve.tensor_copy(halo[p][:, :, :], hn[:, :, TILE:TILE + HALO]).then_inc(s["halo_in"], 1)

            rms1_in(0)
            norm_h(0, 0)
            for i, (a, m) in enumerate(PIECES):
                dve.wait_ge(s["w_hi_done"], i + 1)
                TT(w_lo[:, a:a + m], stage[i % 4][:, :, :].rearrange("p f t -> p (f t)")[:, 0:m],
                   w_hi[:, a:a + m].bitcast(F32), ALU.subtract).then_inc(s["w_lo_done"], 1)

            def low(n, dst, src, hi, ready, done):
                for f in range(KC):
                    dve.wait_ge(ready, count(n, KC, f + 1))
                    TT(dst[:, f, :], src[:, f, :], hi[:, f, :].bitcast(F32), ALU.subtract).then_inc(done, 1)

            low(0, a_lo, hn[:, :, HALO:], a_hi, s["hn_hi"], s["hn_lo"])

            def step(n, j, p):
                m, m2 = n - 1, n - 2
                front, back, late, head = has(n), has(m), has_late(n), has(n + 1)
                q = 1 - p

                def glu(c):
                    if not back:
                        return
                    dve.wait_ge(s["th_a"], count(m, CHUNKS, c + 1))
                    reuse(dve, s["p_lo_done"], count(m, CHUNKS, c - 1))
                    STT(out=gated[:, c % 2, :], in0=tha[:, c % 2, :], scalar=1.0, in1=bank[6][:, :], op0=ALU.add,
                        op1=ALU.mult).then_inc(s["gate_a"], 1)
                    dve.wait_ge(s["b_ps"], count(m, CHUNKS, c + 1))
                    dve.wait_ge(s["gate_a"], count(m, CHUNKS, c + 1))
                    STT(out=gated[:, c % 2, :], in0=gated[:, c % 2, :], scalar=0.5, in1=bank[7][:, :], op0=ALU.mult,
                        op1=ALU.mult).then_inc(s["prod"], 1)

                def elu1(bk, dst, e, em, done):
                    for f in range(KC):
                        dve.wait_ge(e, count(n, KC, f + 1))
                        TS(esq[:, f, :], esq[:, f, :], 1.0, None, ALU.min).then_inc(em, 1)
                    for f in range(KC):
                        dve.wait_ge(em, count(n, KC, f + 1))
                        STT(out=dst[:, f, :], in0=bank[bk[f]][:, :], scalar=0.0, in1=esq[:, f, :], op0=ALU.max,
                            op1=ALU.add).then_inc(done, 1)

                def scan(buf, carry, done):
                    for f in range(KC):
                        dve.tensor_tensor_scan(buf[:, f, :], dec[:, f:f + 1].to_broadcast([P, TILE]), buf[:, f, :],
                                               carry[:, f:f + 1], ALU.mult, ALU.add).then_inc(done, 1)
                    for f in range(KC):
                        dve.wait_ge(done, count(n, KC, f + 1))
                        dve.tensor_copy(carry[:, f:f + 1], buf[:, f, TILE - 1:TILE]).then_inc(s["carry"], 1)

                def conv(taps):
                    for t in taps:
                        for f in range(KC):
                            tap = par[:, C_CW + f * TAPS + t:C_CW + f * TAPS + t + 1]
                            src = hn[:, f, t:t + TILE]
                            if t == 0:
                                last = TS(cbuf[:, f, :], src, tap, par[:, C_CB + f:C_CB + f + 1], ALU.mult, ALU.add)
                            else:
                                dve.wait_ge(s["conv"], count(n, KC * TAPS, KC * (t - 1) + f + 1))
                                last = STT(out=cbuf[:, f, :], in0=src, scalar=tap, in1=cbuf[:, f, :], op0=ALU.mult, op1=ALU.add)
                            last.then_inc(s["conv"], 1)

                if back:
                    for f in range(KC):
                        dve.wait_ge(s["thm"], count(m, KC, f + 1))
                        dve.wait_ge(s["dmix"], count(m, KC, f + 1))
                        STT(out=cbuf[:, f, :], in0=th[:, f, :], scalar=1.0, in1=cbuf[:, f, :], op0=ALU.add,
                            op1=ALU.mult).then_inc(s["umix"], 1)
                        dve.wait_ge(s["umix"], count(m, KC, f + 1))
                        dve.wait_ge(s["hatt"], count(m, KC, f + 1))
                        if f == 0:
                            reuse(dve, s["y_ps"], count(m, 2, 0))
                        STT(out=x2[:, f, :], in0=cbuf[:, f, :], scalar=0.5, in1=qb[:, f, :], op0=ALU.mult,
                            op1=ALU.add).then_inc(s["x2_ready"], 1)
                if front:
                    elu1((2, 1), kb, s["ek"], s["ekm"], s["k_ready"])
                if back:
                    dve.wait_ge(s["st2_ps"], count(m, 1, 1))
                    TS(mse2[:, :], small[:, 0:BLK], 1.0 / HID, RMS_EPS, ALU.mult, ALU.add).then_inc(s["ms2"], 1)
                if late:
                    dve.wait_ge(s["xres_in"], count(m2, 16, 16))
                    for i in range(2):
                        dve.wait_ge(s["y_ps"], count(m2, 2, i + 1))
                        TT(x1[:, 2 * i:2 * i + 2, :], bank[6 + i][:, :].rearrange("p (b d) -> p b d", b=2),
                           x1[:, 2 * i:2 * i + 2, :], ALU.add).then_inc(s["x1_ready"], 1)
                    dve.wait_ge(s["x1_ready"], count(m2, 2, 2))
                    stats(m2, x1, bn2, sm2, dm2, ve2, s["ln2_bn"], s["ln2_ve"])
                if front:
                    if back:
                        dve.wait_ge(s["x2_ready"], count(m, KC, KC))
                    conv((0,))
                if late:
                    neg_mean(m2, sm2, rs2, nm2, s["ln2_rstd"], s["ln2_nm"])
                if front:
                    conv((1,))
                if back:
                    dve.wait_ge(s["r2_ps"], count(m, 1, 1))
                    for f in range(KC):
                        STT(out=kvb[:, f, :], in0=x2[:, f, :], scalar=par[:, C_N2 + f:C_N2 + f + 1], in1=bank[4][:, :],
                            op0=ALU.mult, op1=ALU.mult).then_inc(s["hn2"], 1)
                    low(m, n_lo, kvb, n_hi, s["hn2_hi"], s["hn2_lo"])
                if front:
                    conv((2, 3))
                glu(0)
                if front:
                    for f in range(KC):
                        dve.wait_ge(s["ths"], count(n, KC, f + 1))
                        STT(out=cbuf[:, f, :], in0=th[:, f, :], scalar=1.0, in1=cbuf[:, f, :], op0=ALU.add,
                            op1=ALU.mult).then_inc(s["s_ready"], 1)
                    low(n, s_lo, cbuf, s_hi, s["s_hi_done"], s["s_lo_done"])
                    elu1((1, 0), qb, s["eq"], s["eqm"], s["q_ready"])
                glu(1)
                if front:
                    dve.wait_ge(s["kv_ready"], count(n, KC, KC))
                    if is_first(n):
                        dve.wait_ge(s["prep"], 9)
                    scan(kb, kss_c[p], s["kss"])
                if head:
                    dve.wait_ge(s["xn_ready"], count(n, BLK, BLK))
                    if p == 0:
                        stats1(n + 1, j, 1)
                    else:
                        stats1(n + 1, j + 1, 0)
                if front:
                    scan(kvb, kvs_c[p], s["kvs"])
                if head:
                    neg_mean(n + 1, sm1, rs1, nm1, s["ln1_rstd"], s["ln1_nm"])
                if late:
                    dve.wait_ge(s["lg_ps"], count(m2, 1, 1))
                    dst = logits[:, p, bass.ds((j - 1) * BLK, BLK), :]
                    TT(dst, small[:, 0:BLK * EXPERTS].rearrange("p (b e) -> p b e", e=EXPERTS),
                       par[:, C_RB:C_RB + EXPERTS].rearrange("p (o e) -> p o e", o=1).to_broadcast([P, BLK, EXPERTS]),
                       ALU.add).then_inc(s["lg"], 1)
                glu(2)
                if front:
                    dve.wait_ge(s["den_ps"], count(n, 1, 1))
                    TS(den[:, :, :], small[:, 0:BLK * HEADS].rearrange("p (b h) -> p b h", h=HEADS), 1e-6, None,
                       ALU.max).then_inc(s["den_max"], 1)
                    dve.wait_ge(s["den_max"], count(n, 1, 1))
                    dve.reciprocal(rec_diag, den[:, :, :]).then_inc(s["den_rec"], 1)
                glu(3)
                if front:
                    for f, bk in ((0, 1), (1, 0)):
                        dve.wait_ge(s["qv"], count(n, KC, f + 1))
                        dve.wait_ge(s["rec_ps"], count(n, KC, f + 1))
                        TT(kvb[:, f, :], kvb[:, f, :], bank[bk][:, :], ALU.mult).then_inc(s["o_ready"], 1)
                    low(n, t_lo, kvb, t_hi, s["o_hi"], s["o_lo"])
                glu(4)
                if front:
                    for f in range(KC):
                        dve.wait_ge(s["thg"], count(n, KC, f + 1))
                        dve.wait_ge(s["dgate"], count(n, KC, f + 1))
                        STT(out=th[:, f, :], in0=th[:, f, :], scalar=1.0, in1=kvb[:, f, :], op0=ALU.add,
                            op1=ALU.mult).then_inc(s["ugate"], 1)
                        dve.wait_ge(s["ugate"], count(n, KC, f + 1))
                        STT(out=kvb[:, f, :], in0=th[:, f, :], scalar=0.5, in1=vb[:, f, :], op0=ALU.mult,
                            op1=ALU.add).then_inc(s["o2"], 1)
                    low(n, s_lo, kvb, s_hi, s["o2_hi"], s["o2_lo"])
                glu(5)
                if head:
                    rms1_in(n + 1)
                if front:
                    low(n, t_lo, qb, t_hi, s["att_hi"], s["att_lo"])
                if head:
                    norm_h(n + 1, 1 - p)
                if back:
                    dve.wait_ge(s["w3_used"], count(m, CHUNKS, CHUNKS))
                    for f in range(KC):
                        dve.wait_ge(s["x2g"], count(m, KC, f + 1))
                        STT(out=x2[:, f, :], in0=bank[4 + f][:, :], scalar=mod[:, 4 + f, q:q + 1], in1=x2[:, f, :],
                            op0=ALU.mult, op1=ALU.add).then_inc(s["y_ready"], 1)
                if head:
                    low(n + 1, a_lo, hn[:, :, HALO:], a_hi, s["hn_hi"], s["hn_lo"])

            pipeline(dve, step)

            k = [0]

            def routed(ins):
                k[0] += 1
                ins.then_inc(s["route"], 1)
                dve.wait_ge(s["route"], k[0])

            def bc(a):
                return a.rearrange("p (k o) -> p k o", o=1).to_broadcast([P, NBLK, EXPERTS])

            best, esum, gate, best_rank, pos, slot_f, lane_f, gate_hi = (by_blk[:, i, :] for i in range(8))
            dve.wait_ge(s["lg"], TILES)
            routed(dve.tensor_reduce(best, lall, mybir.AxisListType.X, ALU.max))
            routed(TT(rt[0], lall, bc(best), ALU.subtract))
            routed(TS(rt[2], rt[0], 0.0, None, ALU.is_ge))
            rank = con[:, K_RANK:K_RANK + EXPERTS].rearrange("p (o e) -> p o e", o=1).to_broadcast([P, NBLK, EXPERTS])
            routed(TT(rt[2], rt[2], rank, ALU.mult))
            routed(dve.tensor_reduce(best_rank, rt[2], mybir.AxisListType.X, ALU.max))
            routed(TT(rt[2], rt[2], bc(best_rank), ALU.is_equal))
            dve.wait_ge(s["route_exp"], 1)
            routed(dve.tensor_reduce(esum, rt[1], mybir.AxisListType.X, ALU.add))
            routed(dve.reciprocal(gate, esum))
            routed(dve.tensor_copy(grt[:, :], gate))
            dve.wait_ge(s["count_ps"], 1)
            tot = bank[1][:, 0:HID].rearrange("p (k e) -> p e k", e=EXPERTS)
            cnt, nslots, ends, first, _, _ = (by_exp[:, i, :] for i in range(6))
            routed(dve.tensor_reduce(cnt, tot, mybir.AxisListType.X, ALU.add))
            routed(TS(by_exp_i[:, :], cnt, float(P - 1), None, ALU.add))
            routed(TS(by_exp_i[:, :], by_exp_i[:, :], 7, None, ALU.logical_shift_right))
            routed(dve.tensor_copy(nslots, by_exp_i[:, :]))
            routed(dve.tensor_tensor_scan(ends, ones[:, 0:1].to_broadcast([P, EXPERTS]), nslots, 0.0, ALU.mult, ALU.add))
            routed(TT(first, ends, nslots, ALU.subtract))
            routed(TS(first, first, float(P), None, ALU.mult))
            dve.wait_ge(s["x1_stored"], 16 * TILES)
            se = x1[0:1, 0:2, :].rearrange("p k d -> p (k d)")[:, 0:SLOTS * EXPERTS].rearrange("p (s e) -> p s e", e=EXPERTS)
            routed(TT(se, ends[0:1, :].rearrange("p (o e) -> p o e", o=1).to_broadcast([1, SLOTS, EXPERTS]),
                      con[0:1, K_IOTA:K_IOTA + SLOTS].rearrange("p (k o) -> p k o", o=1).to_broadcast([1, SLOTS, EXPERTS]),
                      ALU.is_le))
            routed(dve.tensor_reduce(slot_sum[:, :], se, mybir.AxisListType.X, ALU.add))
            routed(TS(slot_e[:, :], slot_sum[:, :], float(EXPERTS - 1), None, ALU.min))
            for e in range(EXPERTS):
                last = dve.tensor_tensor_scan(rt[1][:, :, e], ones[:, 0:1].to_broadcast([P, NBLK]), tot[:, e, :],
                                              first[:, e:e + 1], ALU.mult, ALU.add)
            routed(last)
            routed(TT(rt[1], rt[1], bank[1][:, 0:HID].rearrange("p (k e) -> p k e", e=EXPERTS), ALU.subtract))
            routed(TT(rt[1], rt[1], bank[0][:, 0:HID].rearrange("p (k e) -> p k e", e=EXPERTS), ALU.add))
            routed(TT(rt[1], rt[1], rt[2], ALU.mult))
            routed(dve.tensor_reduce(pos, rt[1], mybir.AxisListType.X, ALU.add))
            routed(dve.tensor_copy(pos_i[:, 0, :], pos))
            routed(TS(pos_i[:, 1, :], pos_i[:, 0, :], 7, None, ALU.logical_shift_right))
            routed(TS(pos_i[:, 2, :], pos_i[:, 0, :], P - 1, None, ALU.bitwise_and))
            routed(dve.tensor_copy(slot_f, pos_i[:, 1, :]))
            routed(dve.tensor_copy(lane_f, pos_i[:, 2, :]))
            tok = con[:, K_TOK:K_TOK + NBLK]
            for g in range(NBLK // BLK):
                def bs(a):
                    return a[:, g * BLK:(g + 1) * BLK].rearrange("p (k o) -> p k o", o=1).to_broadcast([P, BLK, SP_])
                oh = place_hi[:, (g % 2) * BLK * SP_:(g % 2 + 1) * BLK * SP_].rearrange("p (k t) -> p k t", t=SP_)
                if g == 0:
                    routed(TT(gate_lo_t[:, :], gate, grt[:, :].bitcast(F32), ALU.subtract))
                routed(TT(oh, con[:, K_IOTA:K_IOTA + SP_].rearrange("p (o t) -> p o t", o=1).to_broadcast([P, BLK, SP_]),
                          bs(slot_f), ALU.is_equal))
                reuse(dve, s["place_ps"], (g - 1) * BLK)
                for v, val in enumerate((tok, gate, None)):
                    dst = slot_oh_all[:, (g % 2) * BLK:(g % 2 + 1) * BLK, v * SP_:(v + 1) * SP_]
                    if v < 2:
                        TT(dst, oh, bs(val), ALU.mult).then_inc(s["place_id"], 1)
                    else:
                        dve.wait_ge(s["place_id"], 3 * g + 2)
                        TT(dst, oh, bs(gate_lo_t[:, :]), ALU.mult).then_inc(s["place_id"], 1)
                for b in range(g * BLK, (g + 1) * BLK):
                    TS(lane_oh(b), con[:, K_IOTA:K_IOTA + P], lane_f[:, b:b + 1], None, ALU.is_equal).then_inc(s["place_oh"], 1)
            dve.wait_ge(s["place_ps"], NBLK)
            tok_ps = bank[2][:, 0:SLOTS]
            routed(TS(place_hi[:, 0:SLOTS], tok_ps, 0.0, float(2 * BATCH * SEQ), ALU.is_equal, ALU.mult))
            routed(STT(out=slot_idx[:, :], in0=tok_ps, scalar=-1.0, in1=place_hi[:, 0:SLOTS], op0=ALU.add, op1=ALU.add))
            routed(TS(slot_meta[:, :, 1], tok_ps, float(SEQ) + 0.5, None, ALU.is_gt))
            routed(dve.tensor_copy(slot_meta[:, :, 0], bank[2][:, SP_:SP_ + SLOTS]))
            routed(TT(slot_meta[:, :, 0], slot_meta[:, :, 0], bank[2][:, 2 * SP_:2 * SP_ + SLOTS], ALU.add))
            TT(gbt[:, 1, :], gbt[:, 1, :], gbt[:, 0, :], ALU.subtract).then_inc(s["place_done"], 1)
            for i in range(4):
                dve.wait_ge(s["we_hi_done"], i + 1)
                TT(w_lo[:, i * PIECE:(i + 1) * PIECE], stage[i][:, :, :].rearrange("p f t -> p (f t)"),
                   w_hi[:, i * PIECE:(i + 1) * PIECE].bitcast(F32), ALU.subtract).then_inc(s["we_lo_done"], 1)

            def low(t, i, r):
                dve.wait_ge(s["th_hi"], t + 1)
                reuse(dve, s["y_e_ps"], t - RING + 1)
                TT(hs_lo[r], bank[r][:, 0:HID], hs_hi[r].bitcast(F32), ALU.subtract).then_inc(s["th_lo"], 1)

            def finish(t, i, r):
                e = nc.values_load(slot_e[0:1, bass.ds(t, 1)], engines=[mybir.EngineType.DVE], min_val=0, max_val=EXPERTS - 1,
                                   skip_runtime_bounds_check_because="slot_e is a count of experts, at most EXPERTS - 1")
                dve.tensor_copy(meta_now[r][:, :], slot_meta[:, bass.ds(t, 1), :].rearrange("p o m -> p (o m)")).then_inc(s["meta_c"], 1)
                dve.wait_ge(s["meta_c"], t + 1)
                STT(out=gb_rows[r], in0=gbt[:, 1, :], scalar=meta_now[r][:, 1:2], in1=gbt[:, 0, :], op0=ALU.mult,
                    op1=ALU.add).then_inc(s["gb_row"], 1)
                dve.wait_ge(s["y_e_ps"], t + 1)
                TT(with_bias[r], bank[4 + r][:, 0:HID], ebt[:, bass.ds(e * HID, HID)], ALU.add).then_inc(s["y_e"], 1)
                dve.wait_ge(s["y_e"], t + 1)
                dve.wait_ge(s["gb_row"], t + 1)
                STT(out=with_bias[r], in0=with_bias[r], scalar=meta_now[r][:, 0:1], in1=gb_rows[r], op0=ALU.mult,
                    op1=ALU.mult).then_inc(s["scaled"], 1)
                dve.wait_ge(s["scaled"], t + 1)
                if not (isinstance(i, int) and i == 0):
                    dve.wait_ge(sc_done[r], 16 * i)
                TT(rows_out[r], with_bias[r], rows_in[r][:, HID:2 * HID], ALU.add).then_inc(s["fin"], 1)

            def body(t, i, r):
                if not (isinstance(t, int) and t == SLOTS - 1):
                    low(t + 1, i if r < RING - 1 else i + 1, (r + 1) % RING)
                finish(t, i, r)

            dve.wait_ge(s["ebias_in"], 16)
            low(0, 0, 0)
            slots(dve, body)

        @block.gpsimd
        def _(pool):
            TT = pool.tensor_tensor
            pool.memset(mhalf[:, :], -0.5).then_inc(s["mhalf_set"], 1)
            pool.wait_ge(s["mhalf_set"], 1)

            def rsqrt(n, dst, src, ready, done, per=1):
                pool.wait_ge(ready, count(n, per, per))
                TT(dst[:, :], src[:, :], mhalf[:, :], ALU.pow).then_inc(done, 1)

            def low(n, dst, src, hi, ready, done):
                for f in range(KC):
                    pool.wait_ge(ready, count(n, KC, f + 1))
                    TT(dst[:, f, :], src[:, f, :], hi[:, f, :].bitcast(F32), ALU.subtract).then_inc(done, 1)

            rsqrt(0, rs1, ve1, s["ln1_ve"], s["ln1_rstd"], 6)
            rsqrt(0, rms1, mse1, s["ms1"], s["rms1_ready"])

            def step(n, j, p):
                m, m2 = n - 1, n - 2
                front, back, late, head = has(n), has(m), has_late(n), has(n + 1)

                def split(c):
                    if not back:
                        return
                    pool.wait_ge(s["p_hi_done"], count(m, CHUNKS, c + 1))
                    TT(p_lo[:, c % 2, :], gated[:, c % 2, :], p_hi[:, c % 2, :].bitcast(F32),
                       ALU.subtract).then_inc(s["p_lo_done"], 1)

                if back:
                    rsqrt(m, rms2, mse2, s["ms2"], s["rms2_ready"])
                if late:
                    rsqrt(m2, rs2, ve2, s["ln2_ve"], s["ln2_rstd"], 6)
                    pool.wait_ge(s["xn2"], count(m2, BLK, BLK))
                    TT(ht[:, :, :], ht[:, :, :], cbt[:, p:p + 1, :].to_broadcast([P, BLK, HID]), ALU.mult).then_inc(s["ht_mul"], 1)
                    pool.wait_ge(s["ht_mul"], count(m2, 1, 1))
                    TT(ht[:, :, :], ht[:, :, :], sbt[:, p:p + 1, :].to_broadcast([P, BLK, HID]), ALU.add).then_inc(s["ht_add"], 1)
                if front:
                    if back:
                        pool.wait_ge(s["hn2_lo"], count(m, KC, KC))
                    for f in range(KC):
                        pool.wait_ge(s["v_ready"], count(n, KC, f + 1))
                        pool.wait_ge(s["k_ready"], count(n, KC, f + 1))
                        TT(kvb[:, f, :], kb[:, f, :], vb[:, f, :], ALU.mult).then_inc(s["kv_ready"], 1)
                split(0)
                split(1)
                if head:
                    rsqrt(n + 1, rs1, ve1, s["ln1_ve"], s["ln1_rstd"], 6)
                if front:
                    pool.wait_ge(s["carry"], count(n, 2 * KC, KC))
                    for f in range(KC):
                        pool.wait_ge(s["q_ready"], count(n, KC, f + 1))
                        TT(kb[:, f, :], kb[:, f, :], qb[:, f, :], ALU.mult).then_inc(s["qk"], 1)
                    pool.wait_ge(s["carry"], count(n, 2 * KC, 2 * KC))
                    for f in range(KC):
                        TT(kvb[:, f, :], kvb[:, f, :], qb[:, f, :], ALU.mult).then_inc(s["qv"], 1)
                split(2)
                if front:
                    low(n, l_lo, cbuf, l_hi, s["loc_hi"], s["loc_lo"])
                split(3)
                if front:
                    for f in range(KC):
                        pool.wait_ge(s["o_lo"], count(n, KC, f + 1))
                        TT(kvb[:, f, :], kvb[:, f, :], vb[:, f, :], ALU.subtract).then_inc(s["dgate"], 1)
                split(4)
                if head:
                    rsqrt(n + 1, rms1, mse1, s["ms1"], s["rms1_ready"])
                split(5)
                if front:
                    for f in range(KC):
                        pool.wait_ge(s["att"], count(n, KC, f + 1))
                        pool.wait_ge(s["loc_lo"], count(n, KC, KC))
                        TT(cbuf[:, f, :], cbuf[:, f, :], qb[:, f, :], ALU.subtract).then_inc(s["dmix"], 1)
                    pool.wait_ge(s["dmix"], count(n, KC, KC))
                    for f in range(KC):
                        pool.wait_ge(s["att_lo"], count(n, KC, f + 1))
                        TT(qb[:, f, :], qb[:, f, :], h[p][:, f, :], ALU.add).then_inc(s["hatt"], 1)

            pipeline(pool, step)

            h1 = rec
            for r in range(RING):
                pool.memset(rows_in[r], 0.0).then_inc(s["g_clear"], 1)
            pool.wait_ge(s["g_clear"], RING)
            pool.wait_ge(s["h_stored"], 16 * TILES)
            pool.wait_ge(s["x1_stored"], 16 * TILES)
            pool.wait_ge(s["place_done"], 1)

            def gather(t):
                r = t % RING
                reuse(pool, s["fin"], t - RING + 1)
                pool.indirect_dma_start(out=rows_in[r], out_offset=None, in_=rec,
                                        in_offset=bass.IndirectOffsetOnAxis(ap=slot_idx[:, t:t + 1], axis=0),
                                        bounds_check=BATCH * SEQ - 1, oob_is_err=False).then_inc(g_in[r], 16)

            gather(0)
            gather(1)
            for t in range(SLOTS):
                if t + 2 < SLOTS:
                    gather(t + 2)
                pool.wait_ge(s["fin"], t + 1)
                pool.indirect_dma_start(out=out.rearrange("b t d -> (b t) d"),
                                        out_offset=bass.IndirectOffsetOnAxis(ap=slot_idx[:, t:t + 1], axis=0),
                                        in_=rows_out[t % RING], in_offset=None,
                                        bounds_check=BATCH * SEQ - 1, oob_is_err=False).then_inc(sc_done[t % RING], 16)


def kernel(L0_attn_x, L0_attn_qkv_w, L0_attn_out_proj_w, L0_attn_out_gate_w, L0_attn_out_gate_b, L0_attn_decay_param,
           L0_attn_conv_w, L0_attn_conv_b, L0_attn_pw_w, L0_attn_gate_w, L0_attn_w1, L0_attn_w2, L0_attn_w3,
           L0_attn_norm1_w, L0_attn_norm2_w, L0_ffn_router_w, L0_ffn_router_b, L0_ffn_expert_w, L0_ffn_expert_b,
           L0_c, L0_wmod):
    import numpy as np
    import concourse.bacc as bacc
    from concourse.bass_utils import run_bass_kernel_spmd

    def rows(a, pad_to=None):
        t = np.asarray(a).T
        if pad_to:
            full = np.zeros(pad_to, t.dtype)
            full[:t.shape[0], :t.shape[1]] = t
            t = full
        return t.reshape(t.shape[0] // P, P, t.shape[1]).transpose(1, 0, 2).reshape(P, -1)

    def cols(v):
        return np.asarray(v).reshape(KC, P).T

    wall = np.ascontiguousarray(np.concatenate([
        rows(L0_attn_qkv_w), rows(L0_attn_pw_w), rows(L0_attn_out_gate_w), rows(L0_attn_out_proj_w), rows(L0_attn_gate_w),
        rows(L0_attn_w1, (HID, INTER_PAD)), rows(L0_attn_w2, (HID, INTER_PAD)), rows(L0_attn_w3, (INTER_PAD, HID))], axis=1))
    wexp = np.ascontiguousarray(np.asarray(L0_ffn_expert_w).reshape(EXPERTS, KC, P, HID).transpose(2, 0, 1, 3)
                                .reshape(P, EXPERTS * KC * HID))
    wmod = np.ascontiguousarray(np.asarray(L0_wmod).reshape(KC, P, 6 * HID).transpose(1, 0, 2))
    params = np.ascontiguousarray(np.concatenate([
        cols(L0_attn_norm1_w), cols(L0_attn_norm2_w),
        np.asarray(L0_attn_conv_w).reshape(KC, P, TAPS).transpose(1, 0, 2).reshape(P, KC * TAPS),
        cols(L0_attn_conv_b), cols(L0_attn_out_gate_b), cols(np.repeat(np.asarray(L0_attn_decay_param), HID // HEADS)),
        np.asarray(L0_c).reshape(BATCH, KC, P).transpose(2, 1, 0).reshape(P, KC * BATCH),
        np.asarray(L0_ffn_router_w).reshape(KC, P, EXPERTS).transpose(1, 0, 2).reshape(P, KC * EXPERTS),
        np.broadcast_to(np.asarray(L0_ffn_router_b), (P, EXPERTS))], axis=1))
    consts = np.zeros((P, K_COLS), np.float32)
    consts[:, K_ID:K_ID + P] = np.eye(P)
    per_head = HID // HEADS
    for f in range(KC):
        for r in range(P):
            head = (f * P + r) // per_head
            consts[r, K_HS + f * HEADS + head] = 1.0
            for b in range(BLK):
                consts[b * HEADS + head, K_HX + f * P + r] = 1.0
    consts[:, K_TRI:K_TRI + P] = np.triu(np.ones((P, P)), 1)
    consts[:, K_IOTA:K_IOTA + P] = np.arange(P)
    consts[:, K_RANK:K_RANK + EXPERTS] = EXPERTS - np.arange(EXPERTS)
    consts[:, K_TOK:] = 1 + np.arange(NBLK) * P + np.arange(P)[:, None]
    ebias = np.ascontiguousarray(np.broadcast_to(np.asarray(L0_ffn_expert_b).reshape(1, -1), (P, EXPERTS * HID)))

    arrays = {"x": np.ascontiguousarray(L0_attn_x), "wall": wall, "wexp": wexp, "wmod": wmod, "params": params,
              "consts": consts, "ebias": ebias}
    nc = bacc.Bacc("TRN2", target_bir_lowering=False, num_devices=1)
    aps = [nc.dram_tensor(f"in_{k}", a.shape, F32, kind="ExternalInput").ap() for k, a in arrays.items()]
    out = nc.dram_tensor("out_0", (BATCH, SEQ, HID), F32, kind="ExternalOutput").ap()
    rec = nc.dram_tensor("rec", (BATCH * SEQ, 2 * HID), F32, kind="Internal").ap()
    build(nc, *aps, out, rec)
    r = run_bass_kernel_spmd(nc, [{f"in_{k}": a for k, a in arrays.items()}], core_ids=[0])
    return r.results[0]["out_0"]
```

```python
from contextlib import ExitStack

import concourse.bass as bass
from concourse import mybir

ALU = mybir.AluOpType
ACT = mybir.ActivationFunctionType
F32 = mybir.dt.float32
F32R = mybir.dt.float32r
P = 128

BATCH, SEQ, HID = 2, 2048, 256
KC = HID // P
HEADS, TAPS, INTER, EXPERTS = 8, 4, 704, 8
TILE = 512
BLK = TILE // P
TILES = BATCH * SEQ // TILE
CHUNKS = -(-INTER // P)
WHOLE = INTER // P * P
REST = INTER - WHOLE
assert 2 * REST == P
HALO = TAPS - 1
LN_EPS, RMS_EPS = 1e-5, 1e-6

W_QKV = 0
W_PW = W_QKV + KC * 3 * HID
W_GATE = W_PW + KC * HID
W_OUT = W_GATE + KC * HID
W_MIX = W_OUT + KC * HID
W_1 = W_MIX + 2 * KC * HID
W_2 = W_1 + KC * WHOLE
W_12 = W_2 + KC * WHOLE
W_3 = W_12 + KC * P
W_COLS = W_3 + CHUNKS * HID
PIECE = KC * TILE

C_N1, C_N2, C_CW, C_CB, C_GB, C_DEC, C_C, C_RW, C_RB = 0, 2, 4, 12, 14, 16, 18, 22, 38
C_COLS = 46
K_ID, K_HS, K_HX = 0, 128, 144
K_TRI = K_HX + 2 * P
K_IOTA = K_TRI + P
K_RANK = K_IOTA + P
K_TOK = K_RANK + EXPERTS
K_COLS = K_TOK + BATCH * SEQ // P

NBLK = BATCH * SEQ // P
RING = 8
NEAR = 4
USED = NBLK + EXPERTS - 1
GROUPS = -(-USED // RING)
SLOTS = RING * GROUPS
LEAD = 5
PLACE = 8


def count(n, per, k):
    return per * n + k


def reuse(eng, sem, value):
    if isinstance(value, int) and value <= 0:
        return
    eng.wait_ge(sem, value)


def build(nc, x, wall, wexp, wmod, params, consts, ebias, out, rec):
    with ExitStack() as ctx:
        def sb(name, shape, dt=F32):
            return ctx.enter_context(nc.sbuf_tensor(name, shape, dt))

        def sem(name):
            return ctx.enter_context(nc.semaphore(name))

        bank = [ctx.enter_context(nc.psum_tensor(f"bank{i}", [P, TILE], F32)) for i in range(8)]
        small = bank[3]

        w_hi, w_lo = sb("w_hi", [P, W_COLS], F32R), sb("w_lo", [P, W_COLS], F32R)
        par, con = sb("par", [P, C_COLS]), sb("con", [P, K_COLS])
        ident = con[:, K_ID:K_ID + P]
        head_sum = con[:, K_HS:K_HS + 16].rearrange("p (f h) -> p f h", f=KC)
        ones = sb("ones", [P, 2])
        xln_all = sb("xln", [P, 2, BLK, HID])
        xln = [xln_all[:, p] for p in range(2)]
        xn = sb("xn", [P, BLK, HID])
        h = [sb(f"h{p}", [P, KC, TILE]) for p in range(2)]
        esq = sb("esq", [P, KC, TILE])
        hn = sb("hn", [P, KC, HALO + TILE])
        halo = [sb(f"halo{p}", [P, KC, HALO]) for p in range(2)]
        a_hi, a_lo = sb("a_hi", [P, KC, TILE], F32R), sb("a_lo", [P, KC, TILE], F32R)
        s_hi, s_lo = sb("s_hi", [P, KC, TILE], F32R), sb("s_lo", [P, KC, TILE], F32R)
        l_hi, l_lo = sb("l_hi", [P, KC, TILE], F32R), sb("l_lo", [P, KC, TILE], F32R)
        t_hi, t_lo = sb("t_hi", [P, KC, TILE], F32R), sb("t_lo", [P, KC, TILE], F32R)
        n_hi, n_lo = sb("n_hi", [P, KC, TILE], F32R), sb("n_lo", [P, KC, TILE], F32R)
        p_hi, p_lo = sb("p_hi", [P, 2, TILE], F32R), sb("p_lo", [P, 2, TILE], F32R)
        cbuf = sb("cbuf", [P, KC, TILE])
        th = sb("th", [P, KC, TILE])
        qb, kb = sb("qb", [P, KC, TILE]), sb("kb", [P, KC, TILE])
        vb, kvb = sb("vb", [P, KC, TILE]), sb("kvb", [P, KC, TILE])
        x2 = sb("x2", [P, KC, TILE])
        tha = sb("tha", [P, 2, TILE])
        gated = sb("gated", [P, 2, TILE])
        x1 = sb("x1", [P, BLK, HID])
        ht = sb("ht", [P, BLK, HID])
        hT = sb("hT", [P, KC, TILE])
        logits = sb("logits", [P, BATCH, SEQ // P, EXPERTS])
        bn1, bn2 = sb("bn1", [P, BLK, 6]), sb("bn2", [P, BLK, 6])
        sm1, sm2 = sb("sm1", [P, BLK]), sb("sm2", [P, BLK])
        dm1, dm2 = sb("dm1", [P, BLK]), sb("dm2", [P, BLK])
        ve1, ve2 = sb("ve1", [P, BLK]), sb("ve2", [P, BLK])
        rs1, rs2 = sb("rs1", [P, BLK]), sb("rs2", [P, BLK])
        nm1, nm2 = sb("nm1", [P, BLK]), sb("nm2", [P, BLK])
        mse1, mse2 = sb("mse1", [P, BLK]), sb("mse2", [P, BLK])
        rms1, rms2 = sb("rms1", [P, BLK]), sb("rms2", [P, BLK])
        mhalf = sb("mhalf", [P, BLK])
        den = sb("den", [P, BLK, HEADS])
        rec_tok = sb("rec_tok", [P, 160])
        rec_diag = rec_tok[:, :].rearrange("p (b c) -> p b c", c=40)[:, :, 0:HEADS]
        recT = sb("recT", [64, TILE], F32R)
        spread = sb("spread", [64, KC * P], F32R)
        dec = sb("dec", [P, KC])
        kss_c = [sb(f"kss_c{p}", [P, KC]) for p in range(2)]
        kvs_c = [sb(f"kvs_c{p}", [P, KC]) for p in range(2)]
        csil = sb("csil", [P, KC * BATCH])
        cth = sb("cth", [P, KC * BATCH])
        hgb = sb("hgb", [P, KC])
        mod = sb("mod", [P, 6, BATCH])
        mods = sb("mods", [P, 2, BATCH])
        sbt = sb("sbt", [P, BATCH, HID])
        cbt = sb("cbt", [P, BATCH, HID])
        gbt = sb("gbt", [P, BATCH, HID])

        names = """par_in con_in wmod_in hc_th hc_silu mod_ps mod_done prep w_hi_done w_lo_done ones_set mhalf_set
            ln1_bn ln1_ve ln1_rstd ln1_nm xn_ready t_ps h_ready sq_ready st1_ps ms1 rms1_ready r1_ps hn_ready hn_hi
            hn_lo halo_in conv k_ps q_ps v_ps ek ekm k_ready eq eqm q_ready v_ready kv_ready kss kvs carry
            ths s_ready s_hi_done s_lo_done l_ps loc loc_hi loc_lo qk den_ps den_max den_rec recT_ps recT_hi_done recT_lo_done rec_ps
            qv o_ready o_hi o_lo g_ps thg dgate ugate o2 o2_hi o2_lo o_ps att att_hi att_lo m_ps thm dmix hatt umix
            x2_ready sq2 st2_ps ms2 rms2_ready r2_ps hn2 hn2_hi hn2_lo a_ps b_ps th_a gate_a prod p_hi_done p_lo_done
             w3_used x2g y_ready y_ps x1_ready ln2_bn ln2_ve ln2_rstd ln2_nm xn2 ht_mul ht_add hT_ps hT_ready
            lg_ps lg xres_in h_stored x1_stored
            ebias_in we_hi_done we_lo_done route route_exp count_ps place_oh slot_is place_id place_ps place_done g_clear tr_ps th_hi th_lo y_e_ps meta_c gb_row scaled fin""".split()
        s = {n: sem(n) for n in names}
        w_in = [sem(f"w_in{i}") for i in range(4)]
        x_in = [sem(f"x_in{p}") for p in range(2)]
        g_in = [sem(f"g_in{r}") for r in range(RING)]
        sc_done = [sem(f"sc_done{r}") for r in range(NEAR)]

        x_flat = x.rearrange("b t d -> (b t d)")
        rec_flat = rec.rearrange("t d -> (t d)")
        stage = [b[:, :, :].rearrange("p a d -> p (a d)") for b in (qb, kb, vb, kvb, cbuf, tha, gated, th, ht)]
        GROUP = [0, 0, 1, 1, 1, 2, 2, 3, 3]
        PIECES = [(a, min(PIECE, W_COLS - a)) for a in range(0, W_COLS, PIECE)]
        assert len(PIECES) == len(stage)
        wm = [esq[:, :, :], x2[:, :, :], hT[:, :, :]]

        def w(t, base, kc, width, a, m=P):
            return t[:, base + kc * width + a:base + kc * width + a + m]

        ebt = xln_all[0:1, :, :, :].rearrange("p a k d -> p (a k d)")

        def quarter(b, r):
            return b[:, :, :].rearrange("p f t -> p (f t)")[:, r * HID:(r + 1) * HID]

        rows_in = [b[:, i, :] for b in (cbuf, th, h[0], h[1]) for i in range(2)]
        hs_hi, hs_lo = [quarter(a_hi, r) for r in range(NEAR)], [quarter(a_lo, r) for r in range(NEAR)]
        rows_out = [quarter(hT, r) for r in range(NEAR)]
        scaled, gb_rows = [quarter(esq, r) for r in range(NEAR)], [quarter(tha, r) for r in range(NEAR)]
        lall = logits[:, :, :, :].rearrange("p b k e -> p (b k) e")
        rt = [xn[:, i, :].rearrange("p (k e) -> p k e", e=EXPERTS) for i in range(BLK)]
        small_f, used = gated[:, :, :].rearrange("p f t -> p (f t)"), [0]
        INT = mybir.dt.int32

        def part(n):
            used[0] += n
            return small_f[:, used[0] - n:used[0]]

        by_blk = part(8 * NBLK).rearrange("p (i k) -> p i k", k=NBLK)
        by_exp = part(6 * EXPERTS).rearrange("p (i e) -> p i e", e=EXPERTS)
        by_exp_i = part(EXPERTS).bitcast(INT)
        pos_i = part(2 * NBLK).bitcast(INT).rearrange("p (i k) -> p i k", k=NBLK)
        place_vals = part(3 * NBLK).rearrange("p (k v) -> p k v", v=3)
        slot_meta = part(2 * SLOTS).rearrange("p (s m) -> p s m", m=2)
        slot_sum = part(SLOTS)[0:1, :]
        slot_e = part(SLOTS).bitcast(INT)[0:1, :]
        meta_now = [part(2) for r in range(NEAR)]
        slot_idx = part(SLOTS).bitcast(INT)
        grt = p_hi[:, 0, 0:NBLK]
        slot_is = [x1[:, :, :].rearrange("p k d -> p (k d)")[:, i * PLACE * SLOTS:(i + 1) * PLACE * SLOTS].rearrange(
            "p (k t) -> p k t", t=SLOTS) for i in range(2)]
        place = x1[:, :, :].rearrange("p k d -> p (k d)")
        assert NBLK * EXPERTS == HID
        gneg = x1[:, 0:BATCH, :]

        block = ctx.enter_context(nc.Block())

        def pipeline(eng, step):
            step(0, 0, 0)
            step(1, 0, 1)
            with eng.Fori(1, TILES // 2 - 1) as j:
                step(2 * j, j, 0)
                step(2 * j + 1, j, 1)
            for n in range(TILES - 2, TILES + 2):
                step(n, n // 2, n % 2)

        def width(c):
            return P if c < CHUNKS - 1 else REST

        def has(n):
            return not isinstance(n, int) or 0 <= n < TILES

        def has_late(n):
            return not isinstance(n, int) or n >= 2

        def slots(eng, body):
            def group(i):
                for r in range(RING):
                    if not isinstance(i, int) or RING * i + r < USED:
                        body(RING * i + r, i, r)
            group(0)
            with eng.Fori(1, GROUPS - 1) as i:
                group(i)
            group(GROUPS - 1)

        def is_first(n):
            return isinstance(n, int) and n == 0

        def tile_of(eng, flat, width, q, jq):
            at = q * SEQ * width + jq * (TILE * width)
            if not isinstance(at, int):
                at = eng.snap(at)
            return flat[bass.ds(at, TILE * width)].rearrange("(k p d) -> p k d", p=P, d=width)

        slot_oh = [b[:, :, :].rearrange("p f t -> p (f t)")[:, 0:PLACE * 3 * SLOTS].rearrange(
            "p (k v s) -> p k v s", v=3, s=SLOTS) for b in (l_hi, l_lo)]
        lane_oh = [b[:, :, :].rearrange("p f t -> p (f t)").rearrange("p (k l) -> p k l", l=P) for b in (s_hi, s_lo)]
        assert PLACE * 3 * SLOTS <= KC * TILE and PLACE * P <= KC * TILE and SLOTS <= P

        def split_low(eng, n, c):
            k = width(c)
            eng.wait_ge(s["p_hi_done"], count(n, CHUNKS, c + 1))
            eng.tensor_tensor(p_lo[0:k, c % 2, :], gated[0:k, c % 2, :], p_hi[0:k, c % 2, :].bitcast(F32),
                              ALU.subtract).then_inc(s["p_lo_done"], 1)

        def modulate(eng, n, p):
            eng.wait_ge(s["xn2"], count(n, BLK, BLK))
            eng.tensor_tensor(ht[:, :, :], ht[:, :, :], cbt[:, p:p + 1, :].to_broadcast([P, BLK, HID]),
                              ALU.mult).then_inc(s["ht_mul"], 1)
            eng.wait_ge(s["ht_mul"], count(n, 1, 1))
            eng.tensor_tensor(ht[:, :, :], ht[:, :, :], sbt[:, p:p + 1, :].to_broadcast([P, BLK, HID]),
                              ALU.add).then_inc(s["ht_add"], 1)

        @block.sync
        def _(sp):
            sp.dma_start(xln[0][:, :, :], tile_of(sp, x_flat, HID, 0, 0)).then_inc(x_in[0], 16)
            sp.dma_start(par[:, :], params).then_inc(s["par_in"], 16)
            sp.dma_start(con[:, :], consts).then_inc(s["con_in"], 16)
            for i in range(3):
                sp.dma_start(wm[i], wmod[:, :, i * TILE:(i + 1) * TILE]).then_inc(s["wmod_in"], 16)
            for i, (a, m) in enumerate(PIECES):
                sp.dma_start(stage[i][:, 0:m], wall[:, a:a + m]).then_inc(w_in[GROUP[i]], 16)

            def step(n, j, p):
                if has(n + 1):
                    q, jq = (1, j) if p == 0 else (0, j + 1)
                    src = tile_of(sp, x_flat, HID, q, jq)
                    if not is_first(n):
                        sp.wait_ge(s["xn_ready"], count(n, BLK, 0))
                    sp.dma_start(xln[q][:, :, :], src).then_inc(x_in[q], 16)

            pipeline(sp, step)
            sp.wait_ge(s["xn_ready"], count(TILES - 1, BLK, BLK))
            sp.dma_start(ebt, ebias).then_inc(s["ebias_in"], 16)
            for i, (name, per) in enumerate((("x2_ready", KC), ("den_ps", 1), ("o2", KC), ("hn2_lo", KC))):
                sp.wait_ge(s[name], per * TILES)
                sp.dma_start(stage[i], wexp[:, i * PIECE:(i + 1) * PIECE]).then_inc(w_in[i], 16)
            for r in range(NEAR):
                sp.wait_ge(sc_done[r], 16 * len(range(r, USED, NEAR)))

        @block.tensor
        def _(pe):
            mm = pe.matmul
            pe.wait_ge(s["hc_silu"], 2)
            pe.wait_ge(s["wmod_in"], 48)
            for i in range(6):
                for kc in range(KC):
                    a = i * P
                    ins = mm(small[:, 2 * i:2 * i + 2], wm[a // TILE][:, kc, a % TILE:a % TILE + P],
                             csil[:, kc * BATCH:(kc + 1) * BATCH], start=kc == 0, stop=kc == 1)
            ins.then_inc(s["mod_ps"], 1)

            def mod_rows():
                for b in range(BATCH):
                    for out_, src in ((bank[6 + b][:, 0:HID], wm[1][:, :, HID:]), (bank[4 + b][:, :], wm[2])):
                        for kc in range(KC):
                            lhs = csil[:, kc * BATCH + b:kc * BATCH + b + 1].to_broadcast([P, P])
                            last_ = mm(out_, lhs, src[:, kc, :], start=kc == 0, stop=kc == 1)
                last_.then_inc(s["mod_ps"], 1)

            def product(out_, terms, done, start=True, stop=True):
                k, last_ = 0, None
                todo = [(wh, ah) for wh, wl, ah, al in terms] + [(wl, ah) for wh, wl, ah, al in terms] + [
                    (wh, al) for wh, wl, ah, al in terms]
                for k, (a, b) in enumerate(todo):
                    last_ = mm(out_, a, b, start=start and k == 0, stop=stop and k == len(todo) - 1)
                if done is not None:
                    last_.then_inc(done, 1)
                return last_

            def dense(out_, base, width, a, hi, lo, done):
                product(out_, [(w(w_hi, base, kc, width, a), w(w_lo, base, kc, width, a), hi[:, kc, :], lo[:, kc, :])
                               for kc in range(KC)], done)

            def rows_of(bk, col, done):
                for b in range(BLK):
                    last_ = mm(bk[:, b * P:(b + 1) * P], col[:, b:b + 1].to_broadcast([P, P]), ident, start=True, stop=True)
                last_.then_inc(done, 1)

            def sums(src, done):
                for b in range(BLK):
                    for f in range(KC):
                        last_ = mm(small[:, b:b + 1], src[:, f, b * P:(b + 1) * P], ones[:, 0:1],
                                   start=f == 0, stop=f == KC - 1)
                last_.then_inc(done, 1)

            def head_t(n):
                pe.wait_ge(s["xn_ready"], count(n, BLK, BLK))
                for f, bk in ((0, 0), (1, 2)):
                    if not is_first(n):
                        pe.wait_ge(s["loc" if f else "q_ready"], count(n - 1, KC, KC - f))
                    for b in range(BLK):
                        last_ = pe.transpose(bank[bk][:, b * P:(b + 1) * P], xn[:, b, f * P:(f + 1) * P], ident)
                    last_.then_inc(s["t_ps"], 1)

            def head_sums(n):
                pe.wait_ge(s["sq_ready"], count(n, KC, KC))
                if not is_first(n):
                    pe.wait_ge(s["recT_lo_done"], count(n - 1, 1, 1))
                sums(hn[:, :, HALO:], s["st1_ps"])

            def head_rows(n):
                pe.wait_ge(s["rms1_ready"], count(n, 1, 1))
                pe.wait_ge(s["h_ready"], count(n, KC, 1))
                if not is_first(n):
                    pe.wait_ge(s["o_ready"], count(n - 1, KC, KC))
                rows_of(bank[0], rms1, s["r1_ps"])

            def step(n, j, p):
                m, m2 = n - 1, n - 2
                front, back, late, head = has(n), has(m), has_late(n), has(n + 1)

                def chunk(c):
                    if not back:
                        return
                    if c == 0:
                        pe.wait_ge(s["hn2_hi"], count(m, KC, KC))
                        pe.wait_ge(s["hn2_lo"], count(m, KC, KC))
                        reuse(pe, s["x1_ready"], count(m, 2, 0))
                    else:
                        pe.wait_ge(s["gate_a"], count(m, CHUNKS, c))
                    if c == CHUNKS - 1:
                        dense(bank[6][:, :], W_12, P, 0, n_hi, n_lo, s["a_ps"])
                        return
                    dense(bank[6][:, :], W_1, WHOLE, c * P, n_hi, n_lo, s["a_ps"])
                    if c > 0:
                        pe.wait_ge(s["prod"], count(m, CHUNKS, c))
                    dense(bank[7][:, :], W_2, WHOLE, c * P, n_hi, n_lo, s["b_ps"])

                def w3(c):
                    if not back:
                        return
                    if c == 0 and late:
                        pe.wait_ge(s["hT_ready"], count(m2, KC, KC))
                    pe.wait_ge(s["p_hi_done"], count(m, CHUNKS, c + 1))
                    pe.wait_ge(s["p_lo_done"], count(m, CHUNKS, c + 1))
                    k = width(c)
                    for f in range(KC):
                        product(bank[4 + f][:, :],
                                [(w(w_hi, W_3, c, HID, f * P)[0:k], w(w_lo, W_3, c, HID, f * P)[0:k],
                                  p_hi[0:k, c % 2, :], p_lo[0:k, c % 2, :])],
                                s["w3_used"] if f == 1 else None,
                                start=c == 0, stop=c == CHUNKS - 1)

                if front:
                    pe.wait_ge(s["hn_hi"], count(n, KC, KC))
                    pe.wait_ge(s["hn_lo"], count(n, KC, KC))
                    if is_first(n):
                        pe.wait_ge(s["w_lo_done"], -(-W_PW // PIECE))
                    else:
                        pe.wait_ge(s["att_hi"], count(m, KC, 1))
                    dense(bank[2][:, :], W_QKV, 3 * HID, HID, a_hi, a_lo, s["k_ps"])
                    reuse(pe, s["thm"], count(n, KC, -1))
                    dense(bank[1][:, :], W_QKV, 3 * HID, HID + P, a_hi, a_lo, s["k_ps"])
                    reuse(pe, s["thm"], count(n, KC, 0))
                    dense(bank[0][:, :], W_QKV, 3 * HID, 2 * HID, a_hi, a_lo, s["v_ps"])
                if is_first(m):
                    pe.wait_ge(s["mod_done"], 2)
                if back:
                    pe.wait_ge(s["sq2"], count(m, KC, KC))
                    if front:
                        pe.wait_ge(s["ms1"], count(n, 1, 1))
                    else:
                        pe.wait_ge(s["recT_lo_done"], count(m, 1, 1))
                    sums(kvb, s["st2_ps"])
                if front:
                    pe.wait_ge(s["k_ready"], count(n, KC, 1))
                    dense(bank[2][:, :], W_QKV, 3 * HID, 2 * HID + P, a_hi, a_lo, s["v_ps"])
                if back:
                    pe.wait_ge(s["rms2_ready"], count(m, 1, 1))
                    reuse(pe, s["y_ready"], count(m, KC, 0))
                    rows_of(bank[4], rms2, s["r2_ps"])
                if front:
                    pe.wait_ge(s["k_ready"], count(n, KC, 2))
                    dense(bank[1][:, :], W_QKV, 3 * HID, 0, a_hi, a_lo, s["q_ps"])
                    pe.wait_ge(s["v_ready"], count(n, KC, 1))
                    dense(bank[0][:, :], W_QKV, 3 * HID, P, a_hi, a_lo, s["q_ps"])
                if is_first(n):
                    mod_rows()
                chunk(0)
                chunk(1)
                if late:
                    pe.wait_ge(s["ht_add"], count(m2, 1, 1))
                    if back:
                        pe.wait_ge(s["hn2"], count(m, KC, KC))
                    for f in range(KC):
                        for b in range(BLK):
                            last_ = pe.transpose(bank[4 + f][:, b * P:(b + 1) * P], ht[:, b, f * P:(f + 1) * P], ident)
                        last_.then_inc(s["hT_ps"], 1)
                chunk(2)
                w3(0)
                if front:
                    pe.wait_ge(s["s_hi_done"], count(n, KC, KC))
                    pe.wait_ge(s["s_lo_done"], count(n, KC, KC))
                    pe.wait_ge(s["v_ready"], count(n, KC, 2))
                    dense(bank[2][:, :], W_PW, HID, 0, s_hi, s_lo, s["l_ps"])
                    pe.wait_ge(s["q_ready"], count(n, KC, 1))
                    dense(bank[1][:, :], W_PW, HID, P, s_hi, s_lo, s["l_ps"])
                if late:
                    pe.wait_ge(s["hT_ready"], count(m2, KC, KC))
                    if back:
                        pe.wait_ge(s["ms2"], count(m, 1, 1))
                    for b in range(BLK):
                        for f in range(KC):
                            last_ = mm(small[:, b * EXPERTS:(b + 1) * EXPERTS], hT[:, f, b * P:(b + 1) * P],
                                       par[:, C_RW + f * EXPERTS:C_RW + (f + 1) * EXPERTS], start=f == 0, stop=f == KC - 1)
                    last_.then_inc(s["lg_ps"], 1)
                w3(1)
                chunk(3)
                if front:
                    pe.wait_ge(s["qk"], count(n, KC, KC))
                    if late:
                        pe.wait_ge(s["lg"], count(m2, 1, 1))
                    elif back:
                        pe.wait_ge(s["ms2"], count(m, 1, 1))
                    else:
                        pe.wait_ge(s["ms1"], 1)
                    for b in range(BLK):
                        for f in range(KC):
                            last_ = mm(small[:, b * HEADS:(b + 1) * HEADS], kb[:, f, b * P:(b + 1) * P],
                                       head_sum[:, f, :], start=f == 0, stop=f == KC - 1)
                    last_.then_inc(s["den_ps"], 1)
                if head:
                    head_t(n + 1)
                if front:
                    pe.wait_ge(s["den_rec"], count(n, 1, 1))
                    for b in range(BLK):
                        last_ = pe.transpose(small[0:32, b * P:(b + 1) * P], rec_tok[:, 32 * b:32 * b + 32], ident)
                    last_.then_inc(s["recT_ps"], 1)
                w3(2)
                if front:
                    pe.wait_ge(s["recT_lo_done"], count(n, 1, 1))
                    pe.wait_ge(s["loc"], count(n, KC, KC))
                    mm(bank[1][:, :], spread[:, 0:P], recT[:, :], start=True, stop=True).then_inc(s["rec_ps"], 1)
                    if head:
                        pe.wait_ge(s["h_ready"], count(n + 1, KC, 1))
                    else:
                        pe.wait_ge(s["q_ready"], count(n, KC, KC))
                    mm(bank[0][:, :], spread[:, P:2 * P], recT[:, :], start=True, stop=True).then_inc(s["rec_ps"], 1)
                chunk(4)
                w3(3)
                if front:
                    pe.wait_ge(s["o_hi"], count(n, KC, KC))
                    pe.wait_ge(s["o_lo"], count(n, KC, KC))
                    if head:
                        pe.wait_ge(s["h_ready"], count(n + 1, KC, KC))
                    if is_first(n):
                        pe.wait_ge(s["w_lo_done"], len(PIECES))
                    dense(bank[2][:, :], W_GATE, HID, 0, t_hi, t_lo, s["g_ps"])
                    dense(bank[1][:, :], W_GATE, HID, P, t_hi, t_lo, s["g_ps"])
                chunk(5)
                w3(4)
                if head:
                    head_sums(n + 1)
                if front:
                    pe.wait_ge(s["o2_hi"], count(n, KC, KC))
                    pe.wait_ge(s["o2_lo"], count(n, KC, KC))
                    pe.wait_ge(s["thg"], count(n, KC, KC))
                    dense(bank[2][:, :], W_OUT, HID, 0, s_hi, s_lo, s["o_ps"])
                    dense(bank[1][:, :], W_OUT, HID, P, s_hi, s_lo, s["o_ps"])
                if head:
                    head_rows(n + 1)
                w3(5)
                if front:
                    pe.wait_ge(s["loc_hi"], count(n, KC, KC))
                    pe.wait_ge(s["loc_lo"], count(n, KC, KC))
                    pe.wait_ge(s["att_hi"], count(n, KC, KC))
                    pe.wait_ge(s["att_lo"], count(n, KC, KC))
                    for f, bk in ((0, 1), (1, 0)):
                        if f == 1 and head:
                            pe.wait_ge(s["hn_ready"], count(n + 1, KC, KC))
                        product(bank[bk][:, :],
                                [(w(w_hi, W_MIX, kc, HID, f * P), w(w_lo, W_MIX, kc, HID, f * P),
                                  (l_hi if kc < KC else t_hi)[:, kc % KC, :], (l_lo if kc < KC else t_lo)[:, kc % KC, :])
                                 for kc in range(2 * KC)], s["m_ps"])
                if back:
                    pe.wait_ge(s["y_ready"], count(m, KC, KC))
                    pe.wait_ge(s["prod"], count(m, CHUNKS, CHUNKS))
                    for i in range(2):
                        for b in range(2):
                            for f in range(KC):
                                last_ = pe.transpose(bank[6 + i][:, b * HID + f * P:b * HID + (f + 1) * P],
                                                     x2[:, f, (2 * i + b) * P:(2 * i + b + 1) * P], ident)
                        last_.then_inc(s["y_ps"], 1)

            pe.wait_ge(s["con_in"], 16)
            head_t(0)
            pe.wait_ge(s["ones_set"], 1)
            pe.wait_ge(s["mod_done"], 1)
            head_sums(0)
            head_rows(0)
            pipeline(pe, step)

            onehot = rt[2][:, :, :].rearrange("p k e -> p (k e)")
            pe.wait_ge(s["route"], 6)
            mm(bank[0][:, 0:HID], con[:, K_TRI:K_TRI + P], onehot, start=True, stop=True)
            mm(bank[1][:, 0:HID], ones[:, 0:1].to_broadcast([P, P]), onehot, start=True, stop=True).then_inc(s["count_ps"], 1)
            for b in range(NBLK):
                g = b // PLACE
                if b % PLACE == 0:
                    pe.wait_ge(s["place_id"], g + 1)
                pe.wait_ge(s["place_oh"], b + 1)
                mm(bank[2][:, 0:3 * SLOTS], lane_oh[g % 2][:, b % PLACE, :],
                   slot_oh[g % 2][:, b % PLACE, :, :].rearrange("p v s -> p (v s)"), start=b == 0,
                   stop=b == NBLK - 1).then_inc(s["place_ps"], 1)

            def turn(t, i, r):
                pe.wait_ge(g_in[r], 16 * (i + 1))
                reuse(pe, s["th_lo"], t - NEAR + 1)
                for kc in range(KC):
                    last_ = pe.transpose(bank[r % NEAR][:, kc * P:(kc + 1) * P], rows_in[r][:, kc * P:(kc + 1) * P], ident)
                last_.then_inc(s["tr_ps"], 1)

            def expert(t, i, r):
                e = nc.values_load(slot_e[0:1, bass.ds(t, 1)], engines=[mybir.EngineType.PE], min_val=0, max_val=EXPERTS - 1,
                                   skip_runtime_bounds_check_because="slot_e is a count of experts, at most EXPERTS - 1")
                y = bank[NEAR + r % NEAR][:, 0:HID]
                pe.wait_ge(s["th_lo"], t + 1)
                pe.wait_ge(s["th_hi"], t + 1)
                reuse(pe, s["scaled"], t - NEAR + 1)
                mm(y, ones[0:1, 0:1].to_broadcast([1, P]), ebt[:, bass.ds(e * HID, HID)],
                   start=True, stop=False)
                k = 0
                for a, wt in ((hs_hi[r % NEAR], w_hi), (hs_hi[r % NEAR], w_lo), (hs_lo[r % NEAR], w_hi)):
                    for kc in range(KC):
                        k += 1
                        last_ = mm(y, a[:, kc * P:(kc + 1) * P],
                                   wt[:, bass.ds(e * (KC * HID) + kc * HID, HID)], start=False, stop=k == 3 * KC)
                last_.then_inc(s["y_e_ps"], 1)

            def body(t, i, r):
                if not (isinstance(t, int) and t == USED - 1):
                    turn(t + 1, i if r < RING - 1 else i + 1, (r + 1) % RING)
                if isinstance(t, int) and t == 0:
                    pe.wait_ge(s["we_lo_done"], 4)
                    pe.wait_ge(s["ebias_in"], 16)
                expert(t, i, r)

            pe.wait_ge(s["place_done"], 1)
            turn(0, 0, 0)
            slots(pe, body)

        @block.scalar
        def _(act):
            A = act.activation
            act.wait_ge(s["par_in"], 16)
            A(cth[:, :], par[:, C_C:C_C + 4], ACT.Tanh, scale=0.5).then_inc(s["hc_th"], 1)
            A(dec[:, :], par[:, C_DEC:C_DEC + KC], ACT.Tanh, scale=0.5).then_inc(s["hc_th"], 1)
            def norm1(n, p):
                act.wait_ge(s["ln1_nm"], count(n, 1, 1))
                reuse(act, s["t_ps"], count(n, KC, 0))
                for b in range(BLK):
                    A(xn[:, b, :], xln[p][:, b, :], ACT.Identity, scale=rs1[:, b:b + 1],
                      bias=nm1[:, b:b + 1]).then_inc(s["xn_ready"], 1)

            def head_h(n, p):
                for f, bk in ((0, 0), (1, 2)):
                    act.wait_ge(s["t_ps"], count(n, KC, f + 1))
                    if f == 0 and not (isinstance(n, int) and n < 2):
                        act.wait_ge(s["hatt"], count(n - 2, KC, KC))
                    A(h[p][:, f, :], bank[bk][:, :], ACT.Identity, scale=mod[:, 2 + f, p:p + 1],
                      bias=mod[:, f, p:p + 1]).then_inc(s["h_ready"], 1)

            def head_sq(n, p):
                reuse(act, s["conv"], count(n, KC * TAPS, 0))
                reuse(act, s["halo_in"], count(n, 2, 0))
                for f in range(KC):
                    act.wait_ge(s["h_ready"], count(n, KC, f + 1))
                    A(hn[:, f, HALO:], h[p][:, f, :], ACT.Square).then_inc(s["sq_ready"], 1)

            def weight_hi(pieces):
                for i in pieces:
                    a, m = PIECES[i]
                    act.wait_ge(w_in[GROUP[i]], 16 * GROUP.count(GROUP[i]))
                    A(w_hi[:, a:a + m], stage[i][:, 0:m], ACT.Copy).then_inc(s["w_hi_done"], 1)

            norm1(0, 0)
            act.wait_ge(s["con_in"], 16)
            A(spread[:, :], con[0:64, K_HX:K_HX + KC * P], ACT.Copy)
            weight_hi(range(0, 2))
            act.wait_ge(s["mod_done"], 1)
            head_h(0, 0)
            head_sq(0, 0)
            weight_hi(range(2, 5))
            def round_hi(n, dst, src, ready, done):
                for f in range(KC):
                    act.wait_ge(ready, count(n, KC, f + 1))
                    A(dst[:, f, :], src[:, f, :], ACT.Copy).then_inc(done, 1)

            round_hi(0, a_hi, hn[:, :, HALO:], s["hn_ready"], s["hn_hi"])
            weight_hi(range(5, len(PIECES)))

            def step(n, j, p):
                m, m2 = n - 1, n - 2
                front, back, late, head = has(n), has(m), has_late(n), has(n + 1)
                q, jq = (1, j - 1) if p == 0 else (0, j)

                def gate(c):
                    if not back:
                        return
                    act.wait_ge(s["a_ps"], count(m, CHUNKS, c + 1))
                    if c == 0:
                        reuse(act, s["prod"], count(m, CHUNKS, 0))
                    reuse(act, s["gate_a"], count(m, CHUNKS, c - 1 if c < CHUNKS - 1 else c))
                    k = width(c)
                    if k < P:
                        A(tha[0:k, 1 - c % 2, :], bank[6][k:2 * k, :], ACT.Copy)
                    A(tha[0:k, c % 2, :], bank[6][0:k, :], ACT.Tanh, scale=0.5).then_inc(s["th_a"], 1)

                def split(c):
                    if not back:
                        return
                    act.wait_ge(s["prod"], count(m, CHUNKS, c + 1))
                    reuse(act, s["w3_used"], count(m, CHUNKS, c - 1))
                    k = width(c)
                    A(p_hi[0:k, c % 2, :], gated[0:k, c % 2, :], ACT.Copy).then_inc(s["p_hi_done"], 1)

                if back:
                    for f, bk in ((0, 1), (1, 0)):
                        act.wait_ge(s["m_ps"], count(m, KC, f + 1))
                        A(th[:, f, :], bank[bk][:, :], ACT.Tanh, scale=0.5).then_inc(s["thm"], 1)
                    act.wait_ge(s["o2_lo"], count(m, KC, KC))
                    for f in range(KC):
                        act.wait_ge(s["x2_ready"], count(m, KC, f + 1))
                        A(kvb[:, f, :], x2[:, f, :], ACT.Square).then_inc(s["sq2"], 1)
                if front:
                    for f, bk in ((0, 2), (1, 1)):
                        act.wait_ge(s["k_ps"], count(n, KC, f + 1))
                        A(esq[:, f, :], bank[bk][:, :], ACT.Exp).then_inc(s["ek"], 1)
                    for f, bk in ((0, 0), (1, 2)):
                        act.wait_ge(s["v_ps"], count(n, KC, f + 1))
                        A(vb[:, f, :], bank[bk][:, :], ACT.Copy).then_inc(s["v_ready"], 1)
                if back:
                    round_hi(m, n_hi, kvb, s["hn2"], s["hn2_hi"])
                if late:
                    dst = tile_of(act, rec_flat, 2 * HID, p, j - 1)
                    act.wait_ge(s["ln2_nm"], count(m2, 1, 1))
                    act.wait_ge(s["x1_ready"], count(m2, 2, 2))
                    act.dma_start(dst[:, :, HID:2 * HID], x1[:, :, :]).then_inc(s["x1_stored"], 16)
                    for b in range(BLK):
                        A(ht[:, b, :], x1[:, b, :], ACT.Identity, scale=rs2[:, b:b + 1],
                          bias=nm2[:, b:b + 1]).then_inc(s["xn2"], 1)
                if front:
                    act.wait_ge(s["k_ready"], count(n, KC, 2))
                    act.wait_ge(s["q_ps"], count(n, KC, 1))
                    A(esq[:, 0, :], bank[1][:, :], ACT.Exp).then_inc(s["eq"], 1)
                gate(0)
                if not back and late:
                    act.wait_ge(s["m_ps"], KC * TILES)
                    for i in range(4):
                        act.wait_ge(w_in[i], 16 * (GROUP.count(i) + 1))
                        A(w_hi[:, i * PIECE:(i + 1) * PIECE], stage[i], ACT.Copy).then_inc(s["we_hi_done"], 1)
                if front:
                    act.wait_ge(s["q_ps"], count(n, KC, 2))
                    A(esq[:, 1, :], bank[0][:, :], ACT.Exp).then_inc(s["eq"], 1)
                split(0)
                gate(1)
                if front:
                    for f in range(KC):
                        act.wait_ge(s["conv"], count(n, KC * TAPS, KC * (TAPS - 1) + f + 1))
                        A(th[:, f, :], cbuf[:, f, :], ACT.Tanh, scale=0.5).then_inc(s["ths"], 1)
                if late:
                    for f in range(KC):
                        act.wait_ge(s["hT_ps"], count(m2, KC, f + 1))
                        A(hT[:, f, :], bank[4 + f][:, :], ACT.Copy).then_inc(s["hT_ready"], 1)
                    act.dma_start(dst[:, :, 0:HID], ht[:, :, :]).then_inc(s["h_stored"], 16)
                split(1)
                if front:
                    round_hi(n, s_hi, cbuf, s["s_ready"], s["s_hi_done"])
                gate(2)
                split(2)
                if front:
                    for f, bk in ((0, 2), (1, 1)):
                        act.wait_ge(s["l_ps"], count(n, KC, f + 1))
                        A(cbuf[:, f, :], bank[bk][:, :], ACT.Copy, scale=0.5).then_inc(s["loc"], 1)
                if head:
                    norm1(n + 1, 1 - p)
                if front:
                    round_hi(n, l_hi, cbuf, s["loc"], s["loc_hi"])
                gate(3)
                if front:
                    act.wait_ge(s["recT_ps"], count(n, 1, 1))
                    A(recT[0:32, :], small[0:32, :], ACT.Copy).then_inc(s["recT_hi_done"], 1)
                if head:
                    head_h(n + 1, 1 - p)
                split(3)
                if head:
                    head_sq(n + 1, 1 - p)
                if front:
                    round_hi(n, t_hi, kvb, s["o_ready"], s["o_hi"])
                gate(4)
                if back:
                    for f in range(KC):
                        act.wait_ge(s["hn2"], count(m, KC, f + 1))
                        A(x2[:, f, :], x2[:, f, :], ACT.Copy, scale=mod[:, 4 + f, q:q + 1]).then_inc(s["x2g"], 1)
                split(4)
                if back:
                    src = tile_of(act, x_flat, HID, q, jq)
                    if is_first(m):
                        act.wait_ge(s["mod_done"], 2)
                    if late:
                        act.wait_ge(s["x1_stored"], count(m2, 16, 16))
                        act.wait_ge(s["h_stored"], count(m2, 16, 16))
                    act.dma_start(x1[:, :, :], src).then_inc(s["xres_in"], 16)
                if front:
                    for f, bk in ((0, 2), (1, 1)):
                        act.wait_ge(s["g_ps"], count(n, KC, f + 1))
                        A(th[:, f, :], bank[bk][:, :], ACT.Tanh, scale=0.5, bias=hgb[:, f:f + 1]).then_inc(s["thg"], 1)
                gate(5)
                if front:
                    round_hi(n, s_hi, kvb, s["o2"], s["o2_hi"])
                split(5)
                if front:
                    for f, bk in ((0, 2), (1, 1)):
                        act.wait_ge(s["o_ps"], count(n, KC, f + 1))
                        A(qb[:, f, :], bank[bk][:, :], ACT.Copy).then_inc(s["att"], 1)
                        A(t_hi[:, f, :], bank[bk][:, :], ACT.Copy).then_inc(s["att_hi"], 1)
                if head:
                    round_hi(n + 1, a_hi, hn[:, :, HALO:], s["hn_ready"], s["hn_hi"])

            pipeline(act, step)
            act.wait_ge(s["route"], 2)
            A(rt[1], rt[0], ACT.Exp).then_inc(s["route_exp"], 1)
            def body(t, i, r):
                act.wait_ge(s["tr_ps"], t + 1)
                reuse(act, s["y_e_ps"], t - NEAR + 1)
                A(hs_hi[r % NEAR], bank[r % NEAR][:, 0:HID], ACT.Copy).then_inc(s["th_hi"], 1)

            slots(act, body)

        @block.vector
        def _(dve):
            TT, TS, STT = dve.tensor_tensor, dve.tensor_scalar, dve.scalar_tensor_tensor
            dve.memset(ones[:, :], 1.0).then_inc(s["ones_set"], 1)
            dve.memset(rec_tok[:, :], 0.0).then_inc(s["prep"], 1)
            for p in range(2):
                dve.memset(halo[p][:, :, :], 0.0).then_inc(s["prep"], 1)
                dve.memset(kss_c[p][:, :], 0.0).then_inc(s["prep"], 1)
                dve.memset(kvs_c[p][:, :], 0.0).then_inc(s["prep"], 1)
            dve.wait_ge(s["hc_th"], 1)
            STT(out=csil[:, :], in0=cth[:, :], scalar=1.0, in1=par[:, C_C:C_C + 4], op0=ALU.add,
                op1=ALU.mult).then_inc(s["hc_silu"], 1)
            dve.wait_ge(s["hc_silu"], 1)
            TS(csil[:, :], csil[:, :], 0.5, None, ALU.mult).then_inc(s["hc_silu"], 1)
            dve.wait_ge(s["hc_th"], 2)
            TS(dec[:, :], dec[:, :], 0.5, 0.5, ALU.mult, ALU.add).then_inc(s["prep"], 1)
            dve.wait_ge(s["prep"], 8)
            TS(dec[:, :], dec[:, :], 1e-8, None, ALU.max).then_inc(s["prep"], 1)
            TS(hgb[:, :], par[:, C_GB:C_GB + KC], 0.5, None, ALU.mult).then_inc(s["prep"], 1)

            def stats(n, xt, bn, sm, dm, ve, stat, comb):
                for b in range(BLK):
                    dve.bn_stats(bn[:, b, :], xt[:, b, :]).then_inc(stat, 1)
                dve.wait_ge(stat, count(n, BLK, BLK))
                TT(sm[:, :], bn[:, :, 1], bn[:, :, 4], ALU.add).then_inc(comb, 1)
                TT(dm[:, :], bn[:, :, 1], bn[:, :, 4], ALU.subtract).then_inc(comb, 1)
                TT(ve[:, :], bn[:, :, 2], bn[:, :, 5], ALU.add).then_inc(comb, 1)
                dve.wait_ge(comb, count(n, 6, 2))
                STT(out=dm[:, :], in0=dm[:, :], scalar=0.25, in1=dm[:, :], op0=ALU.mult, op1=ALU.mult).then_inc(comb, 1)
                dve.wait_ge(comb, count(n, 6, 3))
                TS(ve[:, :], ve[:, :], 1.0 / HID, LN_EPS, ALU.mult, ALU.add).then_inc(comb, 1)
                dve.wait_ge(comb, count(n, 6, 5))
                TT(ve[:, :], ve[:, :], dm[:, :], ALU.add).then_inc(comb, 1)

            def stats1(n, j, p):
                dve.wait_ge(x_in[p], count(j, 16, 16))
                stats(n, xln[p], bn1, sm1, dm1, ve1, s["ln1_bn"], s["ln1_ve"])

            def neg_mean(n, sm, rs, nm, ready, done):
                dve.wait_ge(ready, count(n, 1, 1))
                STT(out=nm[:, :], in0=sm[:, :], scalar=-0.5, in1=rs[:, :], op0=ALU.mult, op1=ALU.mult).then_inc(done, 1)

            stats1(0, 0, 0)
            neg_mean(0, sm1, rs1, nm1, s["ln1_rstd"], s["ln1_nm"])
            dve.wait_ge(s["mod_ps"], 1)
            TS(mod[:, 0:2, :], small[:, 0:4].rearrange("p (i b) -> p i b", b=2), 0.0, None, ALU.add).then_inc(s["prep"], 1)
            TS(mod[:, 2:4, :], small[:, 4:8].rearrange("p (i b) -> p i b", b=2), 1.0, None, ALU.add).then_inc(s["prep"], 1)
            ga = small[:, 8:12].rearrange("p (i b) -> p i b", b=2)
            TS(mods[:, :, :], ga, -1.0, None, ALU.mult).then_inc(s["prep"], 1)
            TS(mod[:, 4:6, :], ga, 0.0, 2.0, ALU.is_ge, ALU.mult).then_inc(s["prep"], 1)
            dve.wait_ge(s["prep"], 14)
            STT(out=mods[:, :, :], in0=ga, scalar=0.25, in1=mods[:, :, :], op0=ALU.max, op1=ALU.max).then_inc(s["prep"], 1)
            dve.wait_ge(s["prep"], 15)
            STT(out=mod[:, 4:6, :], in0=mod[:, 4:6, :], scalar=-1.0, in1=mods[:, :, :], op0=ALU.add,
                op1=ALU.mult).then_inc(s["mod_done"], 1)

            def mod_rows():
                dve.wait_ge(s["mod_ps"], 2)
                for b in range(BATCH):
                    dve.tensor_copy(sbt[:, b, :], bank[6 + b][:, 0:HID]).then_inc(s["prep"], 1)
                    TS(cbt[:, b, :], bank[4 + b][:, 0:HID], 1.0, None, ALU.add).then_inc(s["prep"], 1)
                    TS(gneg[:, b, :], bank[4 + b][:, HID:], -1.0, None, ALU.mult).then_inc(s["prep"], 1)
                    TS(gbt[:, b, :], bank[4 + b][:, HID:], 0.0, 2.0, ALU.is_ge, ALU.mult).then_inc(s["prep"], 1)
                dve.wait_ge(s["prep"], 23)
                for b in range(BATCH):
                    STT(out=gneg[:, b, :], in0=bank[4 + b][:, HID:], scalar=0.25, in1=gneg[:, b, :], op0=ALU.max,
                        op1=ALU.max).then_inc(s["prep"], 1)
                dve.wait_ge(s["prep"], 25)
                STT(out=gbt[:, :, :], in0=gbt[:, :, :], scalar=-1.0, in1=gneg, op0=ALU.add, op1=ALU.mult).then_inc(s["mod_done"], 1)

            def weight_lo(pieces):
                for i in pieces:
                    a, m = PIECES[i]
                    dve.wait_ge(s["w_hi_done"], i + 1)
                    TT(w_lo[:, a:a + m], stage[i][:, 0:m], w_hi[:, a:a + m].bitcast(F32), ALU.subtract).then_inc(s["w_lo_done"], 1)

            def rms1_in(n):
                dve.wait_ge(s["st1_ps"], count(n, 1, 1))
                TS(mse1[:, :], small[:, 0:BLK], 1.0 / HID, RMS_EPS, ALU.mult, ALU.add).then_inc(s["ms1"], 1)

            def norm_h(n, p):
                if is_first(n):
                    dve.wait_ge(s["prep"], 7)
                dve.tensor_copy(hn[:, :, 0:HALO], halo[p][:, :, :]).then_inc(s["halo_in"], 1)
                dve.wait_ge(s["r1_ps"], count(n, 1, 1))
                for f in range(KC):
                    STT(out=hn[:, f, HALO:], in0=h[p][:, f, :], scalar=par[:, C_N1 + f:C_N1 + f + 1], in1=bank[0][:, :],
                        op0=ALU.mult, op1=ALU.mult).then_inc(s["hn_ready"], 1)
                dve.wait_ge(s["hn_ready"], count(n, KC, KC))
                dve.wait_ge(s["halo_in"], count(n, 2, 1))
                dve.tensor_copy(halo[p][:, :, :], hn[:, :, TILE:TILE + HALO]).then_inc(s["halo_in"], 1)

            def low(n, dst, src, hi, ready, done):
                for f in range(KC):
                    dve.wait_ge(ready, count(n, KC, f + 1))
                    TT(dst[:, f, :], src[:, f, :], hi[:, f, :].bitcast(F32), ALU.subtract).then_inc(done, 1)

            weight_lo(range(0, 2))
            rms1_in(0)
            weight_lo(range(2, 4))
            norm_h(0, 0)
            low(0, a_lo, hn[:, :, HALO:], a_hi, s["hn_hi"], s["hn_lo"])
            weight_lo(range(4, len(PIECES)))

            def step(n, j, p):
                m, m2 = n - 1, n - 2
                front, back, late, head = has(n), has(m), has_late(n), has(n + 1)
                q = 1 - p

                def glu(c):
                    if not back:
                        return
                    dve.wait_ge(s["th_a"], count(m, CHUNKS, c + 1))
                    reuse(dve, s["p_lo_done"], count(m, CHUNKS, c - 1))
                    k = width(c)
                    STT(out=gated[0:k, c % 2, :], in0=tha[0:k, c % 2, :], scalar=1.0, in1=bank[6][0:k, :], op0=ALU.add,
                        op1=ALU.mult).then_inc(s["gate_a"], 1)
                    if k == P:
                        dve.wait_ge(s["b_ps"], count(m, CHUNKS - 1, c + 1))
                    dve.wait_ge(s["gate_a"], count(m, CHUNKS, c + 1))
                    value = bank[7][:, :] if k == P else tha[0:k, 1 - c % 2, :]
                    STT(out=gated[0:k, c % 2, :], in0=gated[0:k, c % 2, :], scalar=0.5, in1=value, op0=ALU.mult,
                        op1=ALU.mult).then_inc(s["prod"], 1)
                    if not front:
                        split_low(dve, m, c)

                def elu1(bk, dst, e, em, done):
                    for f in range(KC):
                        dve.wait_ge(e, count(n, KC, f + 1))
                        TS(esq[:, f, :], esq[:, f, :], 1.0, None, ALU.min).then_inc(em, 1)
                    for f in range(KC):
                        dve.wait_ge(em, count(n, KC, f + 1))
                        STT(out=dst[:, f, :], in0=bank[bk[f]][:, :], scalar=0.0, in1=esq[:, f, :], op0=ALU.max,
                            op1=ALU.add).then_inc(done, 1)

                def scan(buf, carry, done):
                    for f in range(KC):
                        dve.tensor_tensor_scan(buf[:, f, :], dec[:, f:f + 1].to_broadcast([P, TILE]), buf[:, f, :],
                                               carry[:, f:f + 1], ALU.mult, ALU.add).then_inc(done, 1)
                    for f in range(KC):
                        dve.wait_ge(done, count(n, KC, f + 1))
                        dve.tensor_copy(carry[:, f:f + 1], buf[:, f, TILE - 1:TILE]).then_inc(s["carry"], 1)

                def conv(taps):
                    for t in taps:
                        for f in range(KC):
                            tap = par[:, C_CW + f * TAPS + t:C_CW + f * TAPS + t + 1]
                            src = hn[:, f, t:t + TILE]
                            if t == 0:
                                last = TS(cbuf[:, f, :], src, tap, par[:, C_CB + f:C_CB + f + 1], ALU.mult, ALU.add)
                            else:
                                dve.wait_ge(s["conv"], count(n, KC * TAPS, KC * (t - 1) + f + 1))
                                last = STT(out=cbuf[:, f, :], in0=src, scalar=tap, in1=cbuf[:, f, :], op0=ALU.mult, op1=ALU.add)
                            last.then_inc(s["conv"], 1)

                if back:
                    for f in range(KC):
                        dve.wait_ge(s["thm"], count(m, KC, f + 1))
                        dve.wait_ge(s["dmix"], count(m, KC, f + 1))
                        STT(out=cbuf[:, f, :], in0=th[:, f, :], scalar=1.0, in1=cbuf[:, f, :], op0=ALU.add,
                            op1=ALU.mult).then_inc(s["umix"], 1)
                        dve.wait_ge(s["umix"], count(m, KC, f + 1))
                        dve.wait_ge(s["hatt"], count(m, KC, f + 1))
                        if f == 0:
                            reuse(dve, s["y_ps"], count(m, 2, 0))
                        STT(out=x2[:, f, :], in0=cbuf[:, f, :], scalar=0.5, in1=qb[:, f, :], op0=ALU.mult,
                            op1=ALU.add).then_inc(s["x2_ready"], 1)
                if late:
                    dve.wait_ge(s["xres_in"], count(m2, 16, 16))
                    for i in range(2):
                        dve.wait_ge(s["y_ps"], count(m2, 2, i + 1))
                        TT(x1[:, 2 * i:2 * i + 2, :], bank[6 + i][:, :].rearrange("p (b d) -> p b d", b=2),
                           x1[:, 2 * i:2 * i + 2, :], ALU.add).then_inc(s["x1_ready"], 1)
                if front:
                    elu1((2, 1), kb, s["ek"], s["ekm"], s["k_ready"])
                if back:
                    dve.wait_ge(s["st2_ps"], count(m, 1, 1))
                    TS(mse2[:, :], small[:, 0:BLK], 1.0 / HID, RMS_EPS, ALU.mult, ALU.add).then_inc(s["ms2"], 1)
                if late:
                    dve.wait_ge(s["x1_ready"], count(m2, 2, 2))
                    stats(m2, x1, bn2, sm2, dm2, ve2, s["ln2_bn"], s["ln2_ve"])
                if back:
                    dve.wait_ge(s["r2_ps"], count(m, 1, 1))
                    for f in range(KC):
                        STT(out=kvb[:, f, :], in0=x2[:, f, :], scalar=par[:, C_N2 + f:C_N2 + f + 1], in1=bank[4][:, :],
                            op0=ALU.mult, op1=ALU.mult).then_inc(s["hn2"], 1)
                if late:
                    neg_mean(m2, sm2, rs2, nm2, s["ln2_rstd"], s["ln2_nm"])
                if not back and late:
                    modulate(dve, m2, p)
                    for i in range(4):
                        dve.wait_ge(s["we_hi_done"], i + 1)
                        TT(w_lo[:, i * PIECE:(i + 1) * PIECE], stage[i],
                           w_hi[:, i * PIECE:(i + 1) * PIECE].bitcast(F32), ALU.subtract).then_inc(s["we_lo_done"], 1)
                if back:
                    low(m, n_lo, kvb, n_hi, s["hn2_hi"], s["hn2_lo"])
                if front:
                    if back:
                        dve.wait_ge(s["x2_ready"], count(m, KC, KC))
                    conv((0, 1))
                glu(0)
                if front:
                    conv((2, 3))
                glu(1)
                if front:
                    for f in range(KC):
                        dve.wait_ge(s["ths"], count(n, KC, f + 1))
                        STT(out=cbuf[:, f, :], in0=th[:, f, :], scalar=1.0, in1=cbuf[:, f, :], op0=ALU.add,
                            op1=ALU.mult).then_inc(s["s_ready"], 1)
                    low(n, s_lo, cbuf, s_hi, s["s_hi_done"], s["s_lo_done"])
                    elu1((1, 0), qb, s["eq"], s["eqm"], s["q_ready"])
                if front:
                    dve.wait_ge(s["kv_ready"], count(n, KC, KC))
                    if is_first(n):
                        dve.wait_ge(s["prep"], 9)
                    scan(kb, kss_c[p], s["kss"])
                glu(2)
                if head:
                    dve.wait_ge(s["xn_ready"], count(n, BLK, BLK))
                    if p == 0:
                        stats1(n + 1, j, 1)
                    else:
                        stats1(n + 1, j + 1, 0)
                if front:
                    scan(kvb, kvs_c[p], s["kvs"])
                if head:
                    neg_mean(n + 1, sm1, rs1, nm1, s["ln1_rstd"], s["ln1_nm"])
                if late:
                    dve.wait_ge(s["lg_ps"], count(m2, 1, 1))
                    dst = logits[:, p, bass.ds((j - 1) * BLK, BLK), :]
                    TT(dst, small[:, 0:BLK * EXPERTS].rearrange("p (b e) -> p b e", e=EXPERTS),
                       par[:, C_RB:C_RB + EXPERTS].rearrange("p (o e) -> p o e", o=1).to_broadcast([P, BLK, EXPERTS]),
                       ALU.add).then_inc(s["lg"], 1)
                if front:
                    dve.wait_ge(s["den_ps"], count(n, 1, 1))
                    TS(den[:, :, :], small[:, 0:BLK * HEADS].rearrange("p (b h) -> p b h", h=HEADS), 1e-6, None,
                       ALU.max).then_inc(s["den_max"], 1)
                    dve.wait_ge(s["den_max"], count(n, 1, 1))
                    dve.reciprocal(rec_diag, den[:, :, :]).then_inc(s["den_rec"], 1)
                glu(3)
                if front:
                    dve.wait_ge(s["recT_hi_done"], count(n, 1, 1))
                    TT(recT[32:64, :], small[0:32, :], recT[0:32, :].bitcast(F32), ALU.subtract).then_inc(s["recT_lo_done"], 1)
                    for f, bk in ((0, 1), (1, 0)):
                        dve.wait_ge(s["qv"], count(n, KC, f + 1))
                        dve.wait_ge(s["rec_ps"], count(n, KC, f + 1))
                        TT(kvb[:, f, :], kvb[:, f, :], bank[bk][:, :], ALU.mult).then_inc(s["o_ready"], 1)
                    low(n, t_lo, kvb, t_hi, s["o_hi"], s["o_lo"])
                glu(4)
                if front:
                    for f in range(KC):
                        dve.wait_ge(s["thg"], count(n, KC, f + 1))
                        dve.wait_ge(s["dgate"], count(n, KC, f + 1))
                        STT(out=th[:, f, :], in0=th[:, f, :], scalar=1.0, in1=kvb[:, f, :], op0=ALU.add,
                            op1=ALU.mult).then_inc(s["ugate"], 1)
                        dve.wait_ge(s["ugate"], count(n, KC, f + 1))
                        STT(out=kvb[:, f, :], in0=th[:, f, :], scalar=0.5, in1=vb[:, f, :], op0=ALU.mult,
                            op1=ALU.add).then_inc(s["o2"], 1)
                    low(n, s_lo, kvb, s_hi, s["o2_hi"], s["o2_lo"])
                glu(5)
                if head:
                    rms1_in(n + 1)
                if front:
                    low(n, t_lo, qb, t_hi, s["att_hi"], s["att_lo"])
                if head:
                    norm_h(n + 1, 1 - p)
                if back:
                    dve.wait_ge(s["w3_used"], count(m, CHUNKS, CHUNKS))
                    for f in range(KC):
                        dve.wait_ge(s["x2g"], count(m, KC, f + 1))
                        STT(out=x2[:, f, :], in0=bank[4 + f][:, :], scalar=mod[:, 4 + f, q:q + 1], in1=x2[:, f, :],
                            op0=ALU.mult, op1=ALU.add).then_inc(s["y_ready"], 1)
                if head:
                    low(n + 1, a_lo, hn[:, :, HALO:], a_hi, s["hn_hi"], s["hn_lo"])
                if is_first(n):
                    mod_rows()

            pipeline(dve, step)

            k = [0]

            def routed(ins):
                k[0] += 1
                ins.then_inc(s["route"], 1)
                dve.wait_ge(s["route"], k[0])

            def bc(a):
                return a.rearrange("p (k o) -> p k o", o=1).to_broadcast([P, NBLK, EXPERTS])

            best, esum, gate, best_rank, pos, slot_f, lane_f = (by_blk[:, i, :] for i in range(7))
            dve.wait_ge(s["lg"], TILES)
            routed(dve.tensor_reduce(best, lall, mybir.AxisListType.X, ALU.max))
            routed(TT(rt[0], lall, bc(best), ALU.subtract))
            routed(TS(rt[2], rt[0], 0.0, None, ALU.is_ge))
            rank = con[:, K_RANK:K_RANK + EXPERTS].rearrange("p (o e) -> p o e", o=1).to_broadcast([P, NBLK, EXPERTS])
            routed(TT(rt[2], rt[2], rank, ALU.mult))
            routed(dve.tensor_reduce(best_rank, rt[2], mybir.AxisListType.X, ALU.max))
            routed(TT(rt[2], rt[2], bc(best_rank), ALU.is_equal))
            dve.wait_ge(s["route_exp"], 1)
            routed(dve.tensor_reduce(esum, rt[1], mybir.AxisListType.X, ALU.add))
            routed(dve.reciprocal(gate, esum))
            routed(dve.tensor_copy(grt[:, :], gate))
            dve.tensor_copy(place_vals[:, :, 0], con[:, K_TOK:K_TOK + NBLK])
            dve.tensor_copy(place_vals[:, :, 1], grt[:, :].bitcast(F32))
            routed(TT(place_vals[:, :, 2], gate, grt[:, :].bitcast(F32), ALU.subtract))
            dve.wait_ge(s["count_ps"], 1)
            tot = bank[1][:, 0:HID].rearrange("p (k e) -> p e k", e=EXPERTS)
            cnt, nslots, ends, first, _, _ = (by_exp[:, i, :] for i in range(6))
            routed(dve.tensor_reduce(cnt, tot, mybir.AxisListType.X, ALU.add))
            routed(TS(by_exp_i[:, :], cnt, float(P - 1), None, ALU.add))
            routed(TS(by_exp_i[:, :], by_exp_i[:, :], 7, None, ALU.logical_shift_right))
            routed(dve.tensor_copy(nslots, by_exp_i[:, :]))
            routed(dve.tensor_tensor_scan(ends, ones[:, 0:1].to_broadcast([P, EXPERTS]), nslots, 0.0, ALU.mult, ALU.add))
            routed(TT(first, ends, nslots, ALU.subtract))
            routed(TS(first, first, float(P), None, ALU.mult))
            for e in range(EXPERTS):
                last = dve.tensor_tensor_scan(rt[1][:, :, e], ones[:, 0:1].to_broadcast([P, NBLK]), tot[:, e, :],
                                              first[:, e:e + 1], ALU.mult, ALU.add)
            routed(last)
            routed(TT(rt[1], rt[1], bank[0][:, 0:HID].rearrange("p (k e) -> p k e", e=EXPERTS), ALU.add))
            routed(TT(rt[1], rt[1], rt[2], ALU.mult))
            routed(dve.tensor_reduce(pos, rt[1], mybir.AxisListType.X, ALU.add))
            routed(dve.tensor_copy(pos_i[:, 0, :], pos))
            routed(TS(pos_i[:, 1, :], pos_i[:, 0, :], 7, None, ALU.logical_shift_right))
            routed(dve.tensor_copy(slot_f, pos_i[:, 1, :]))
            routed(STT(out=lane_f, in0=slot_f, scalar=-float(P), in1=pos, op0=ALU.mult, op1=ALU.add))
            iota = con[:, K_IOTA:K_IOTA + SLOTS].rearrange("p (o t) -> p o t", o=1).to_broadcast([P, PLACE, SLOTS])
            dve.wait_ge(s["x1_stored"], 16 * TILES)
            for g in range(NBLK // PLACE):
                blocks = slice(g * PLACE, (g + 1) * PLACE)
                reuse(dve, s["place_ps"], (g - 1) * PLACE)
                TT(slot_is[g % 2], iota, slot_f[:, blocks].rearrange("p (k o) -> p k o", o=1).to_broadcast([P, PLACE, SLOTS]),
                   ALU.is_equal).then_inc(s["slot_is"], 1)
                for b in range(PLACE):
                    at = g * PLACE + b
                    TS(lane_oh[g % 2][:, b, :], con[:, K_IOTA:K_IOTA + P], lane_f[:, at:at + 1], None,
                       ALU.is_equal).then_inc(s["place_oh"], 1)
            se = place[0:1, 2 * PLACE * SLOTS:(2 * PLACE + EXPERTS) * SLOTS].rearrange("p (s e) -> p s e", e=EXPERTS)
            routed(TT(se, ends[0:1, :].rearrange("p (o e) -> p o e", o=1).to_broadcast([1, SLOTS, EXPERTS]),
                      con[0:1, K_IOTA:K_IOTA + SLOTS].rearrange("p (k o) -> p k o", o=1).to_broadcast([1, SLOTS, EXPERTS]),
                      ALU.is_le))
            routed(dve.tensor_reduce(slot_sum[:, :], se, mybir.AxisListType.X, ALU.add))
            routed(TS(slot_e[:, :], slot_sum[:, :], float(EXPERTS - 1), None, ALU.min))
            dve.wait_ge(s["place_ps"], NBLK)
            tok_ps = bank[2][:, 0:SLOTS]
            routed(TS(place[:, 0:SLOTS], tok_ps, 0.0, float(2 * BATCH * SEQ), ALU.is_equal, ALU.mult))
            STT(out=slot_idx[:, :], in0=tok_ps, scalar=-1.0, in1=place[:, 0:SLOTS], op0=ALU.add,
                op1=ALU.add).then_inc(s["place_done"], 1)
            routed(TS(slot_meta[:, :, 1], tok_ps, float(SEQ) + 0.5, None, ALU.is_gt))
            routed(dve.tensor_copy(slot_meta[:, :, 0], bank[2][:, SLOTS:2 * SLOTS]))
            routed(TT(slot_meta[:, :, 0], slot_meta[:, :, 0], bank[2][:, 2 * SLOTS:3 * SLOTS], ALU.add))
            routed(TT(gbt[:, 1, :], gbt[:, 1, :], gbt[:, 0, :], ALU.subtract))
            def low_rows(t, i, r):
                dve.wait_ge(s["th_hi"], t + 1)
                reuse(dve, s["y_e_ps"], t - NEAR + 1)
                TT(hs_lo[r % NEAR], bank[r % NEAR][:, 0:HID], hs_hi[r % NEAR].bitcast(F32), ALU.subtract).then_inc(s["th_lo"], 1)

            def finish(t, i, r):
                v = r % NEAR
                dve.tensor_copy(meta_now[v][:, :], slot_meta[:, bass.ds(t, 1), :].rearrange("p o m -> p (o m)")).then_inc(s["meta_c"], 1)
                dve.wait_ge(s["meta_c"], t + 1)
                STT(out=gb_rows[v], in0=gbt[:, 1, :], scalar=meta_now[v][:, 1:2], in1=gbt[:, 0, :], op0=ALU.mult,
                    op1=ALU.add).then_inc(s["gb_row"], 1)
                dve.wait_ge(s["y_e_ps"], t + 1)
                dve.wait_ge(s["gb_row"], t + 1)
                STT(out=scaled[v], in0=bank[NEAR + v][:, 0:HID], scalar=meta_now[v][:, 0:1], in1=gb_rows[v], op0=ALU.mult,
                    op1=ALU.mult).then_inc(s["scaled"], 1)
                dve.wait_ge(s["scaled"], t + 1)
                reuse(dve, sc_done[v], 16 * (i * (RING // NEAR) + r // NEAR))
                TT(rows_out[v], scaled[v], rows_in[r][:, HID:2 * HID], ALU.add).then_inc(s["fin"], 1)

            def body(t, i, r):
                if not (isinstance(t, int) and t == USED - 1):
                    low_rows(t + 1, i if r < RING - 1 else i + 1, (r + 1) % RING)
                finish(t, i, r)

            low_rows(0, 0, 0)
            slots(dve, body)

        @block.gpsimd
        def _(pool):
            TT = pool.tensor_tensor
            pool.memset(mhalf[:, :], -0.5).then_inc(s["mhalf_set"], 1)
            pool.wait_ge(s["mhalf_set"], 1)

            def rsqrt(n, dst, src, ready, done, per=1):
                pool.wait_ge(ready, count(n, per, per))
                TT(dst[:, :], src[:, :], mhalf[:, :], ALU.pow).then_inc(done, 1)

            def low(n, dst, src, hi, ready, done):
                for f in range(KC):
                    pool.wait_ge(ready, count(n, KC, f + 1))
                    TT(dst[:, f, :], src[:, f, :], hi[:, f, :].bitcast(F32), ALU.subtract).then_inc(done, 1)

            rsqrt(0, rs1, ve1, s["ln1_ve"], s["ln1_rstd"], 6)
            rsqrt(0, rms1, mse1, s["ms1"], s["rms1_ready"])

            def step(n, j, p):
                m, m2 = n - 1, n - 2
                front, back, late, head = has(n), has(m), has_late(n), has(n + 1)
                if is_first(m):
                    pool.wait_ge(s["mod_done"], 2)

                def split(c):
                    if not back or not front:
                        return
                    split_low(pool, m, c)

                if back:
                    rsqrt(m, rms2, mse2, s["ms2"], s["rms2_ready"])
                if late:
                    rsqrt(m2, rs2, ve2, s["ln2_ve"], s["ln2_rstd"], 6)
                    if back:
                        modulate(pool, m2, p)
                if front:
                    if back:
                        pool.wait_ge(s["hn2_lo"], count(m, KC, KC))
                    for f in range(KC):
                        pool.wait_ge(s["v_ready"], count(n, KC, f + 1))
                        pool.wait_ge(s["k_ready"], count(n, KC, f + 1))
                        TT(kvb[:, f, :], kb[:, f, :], vb[:, f, :], ALU.mult).then_inc(s["kv_ready"], 1)
                split(0)
                split(1)
                if front:
                    pool.wait_ge(s["carry"], count(n, 2 * KC, KC))
                    for f in range(KC):
                        pool.wait_ge(s["q_ready"], count(n, KC, f + 1))
                        TT(kb[:, f, :], kb[:, f, :], qb[:, f, :], ALU.mult).then_inc(s["qk"], 1)
                if head:
                    rsqrt(n + 1, rs1, ve1, s["ln1_ve"], s["ln1_rstd"], 6)
                if front:
                    pool.wait_ge(s["carry"], count(n, 2 * KC, 2 * KC))
                    for f in range(KC):
                        TT(kvb[:, f, :], kvb[:, f, :], qb[:, f, :], ALU.mult).then_inc(s["qv"], 1)
                split(2)
                if front:
                    low(n, l_lo, cbuf, l_hi, s["loc_hi"], s["loc_lo"])
                split(3)
                if front:
                    for f in range(KC):
                        pool.wait_ge(s["o_lo"], count(n, KC, f + 1))
                        TT(kvb[:, f, :], kvb[:, f, :], vb[:, f, :], ALU.subtract).then_inc(s["dgate"], 1)
                split(4)
                if head:
                    rsqrt(n + 1, rms1, mse1, s["ms1"], s["rms1_ready"])
                split(5)
                if front:
                    for f in range(KC):
                        pool.wait_ge(s["att"], count(n, KC, f + 1))
                        pool.wait_ge(s["loc_lo"], count(n, KC, KC))
                        TT(cbuf[:, f, :], cbuf[:, f, :], qb[:, f, :], ALU.subtract).then_inc(s["dmix"], 1)
                    pool.wait_ge(s["dmix"], count(n, KC, KC))
                    for f in range(KC):
                        pool.wait_ge(s["att_lo"], count(n, KC, f + 1))
                        TT(qb[:, f, :], qb[:, f, :], h[p][:, f, :], ALU.add).then_inc(s["hatt"], 1)

            pipeline(pool, step)

            for r in range(RING):
                pool.memset(rows_in[r], 0.0).then_inc(s["g_clear"], 1)
            pool.wait_ge(s["g_clear"], RING)
            for g in range(NBLK // PLACE):
                pool.wait_ge(s["slot_is"], g + 1)
                reuse(pool, s["place_ps"], (g - 1) * PLACE)
                TT(slot_oh[g % 2], slot_is[g % 2].rearrange("p k (o t) -> p k o t", o=1).to_broadcast([P, PLACE, 3, SLOTS]),
                   place_vals[:, g * PLACE:(g + 1) * PLACE, :].rearrange("p k (v o) -> p k v o", o=1).to_broadcast(
                       [P, PLACE, 3, SLOTS]), ALU.mult).then_inc(s["place_id"], 1)
            pool.wait_ge(s["h_stored"], 16 * TILES)
            pool.wait_ge(s["x1_stored"], 16 * TILES)
            pool.wait_ge(s["place_done"], 1)

            def gather(t):
                r = t % RING
                reuse(pool, s["fin"], t - RING + 1)
                pool.indirect_dma_start(out=rows_in[r], out_offset=None, in_=rec,
                                        in_offset=bass.IndirectOffsetOnAxis(ap=slot_idx[:, t:t + 1], axis=0),
                                        bounds_check=BATCH * SEQ - 1, oob_is_err=False).then_inc(g_in[r], 16)

            for t in range(LEAD):
                gather(t)
            for t in range(USED):
                if t + LEAD < USED:
                    gather(t + LEAD)
                pool.wait_ge(s["fin"], t + 1)
                pool.indirect_dma_start(out=out.rearrange("b t d -> (b t) d"),
                                        out_offset=bass.IndirectOffsetOnAxis(ap=slot_idx[:, t:t + 1], axis=0),
                                        in_=rows_out[t % NEAR], in_offset=None,
                                        bounds_check=BATCH * SEQ - 1, oob_is_err=False).then_inc(sc_done[t % NEAR], 16)


def kernel(L0_attn_x, L0_attn_qkv_w, L0_attn_out_proj_w, L0_attn_out_gate_w, L0_attn_out_gate_b, L0_attn_decay_param,
           L0_attn_conv_w, L0_attn_conv_b, L0_attn_pw_w, L0_attn_gate_w, L0_attn_w1, L0_attn_w2, L0_attn_w3,
           L0_attn_norm1_w, L0_attn_norm2_w, L0_ffn_router_w, L0_ffn_router_b, L0_ffn_expert_w, L0_ffn_expert_b,
           L0_c, L0_wmod):
    import numpy as np
    import concourse.bacc as bacc
    from concourse.bass_utils import run_bass_kernel_spmd

    def rows(a):
        t = np.asarray(a).T
        full = np.zeros((-(-t.shape[0] // P) * P, t.shape[1]), t.dtype)
        full[:t.shape[0]] = t
        t = full
        return t.reshape(t.shape[0] // P, P, t.shape[1]).transpose(1, 0, 2).reshape(P, -1)

    def cols(v):
        return np.asarray(v).reshape(KC, P).T

    wall = np.ascontiguousarray(np.concatenate([
        rows(L0_attn_qkv_w), rows(L0_attn_pw_w), rows(L0_attn_out_gate_w), rows(L0_attn_out_proj_w), rows(L0_attn_gate_w),
        rows(L0_attn_w1[:WHOLE]), rows(L0_attn_w2[:WHOLE]),
        rows(np.concatenate([np.asarray(L0_attn_w1)[WHOLE:], np.asarray(L0_attn_w2)[WHOLE:]])), rows(L0_attn_w3)], axis=1))
    wexp = np.ascontiguousarray(np.asarray(L0_ffn_expert_w).reshape(EXPERTS, KC, P, HID).transpose(2, 0, 1, 3)
                                .reshape(P, EXPERTS * KC * HID))
    wmod = np.ascontiguousarray(np.asarray(L0_wmod).reshape(KC, P, 6 * HID).transpose(1, 0, 2))
    params = np.ascontiguousarray(np.concatenate([
        cols(L0_attn_norm1_w), cols(L0_attn_norm2_w),
        np.asarray(L0_attn_conv_w).reshape(KC, P, TAPS).transpose(1, 0, 2).reshape(P, KC * TAPS),
        cols(L0_attn_conv_b), cols(L0_attn_out_gate_b), cols(np.repeat(np.asarray(L0_attn_decay_param), HID // HEADS)),
        np.asarray(L0_c).reshape(BATCH, KC, P).transpose(2, 1, 0).reshape(P, KC * BATCH),
        np.asarray(L0_ffn_router_w).reshape(KC, P, EXPERTS).transpose(1, 0, 2).reshape(P, KC * EXPERTS),
        np.broadcast_to(np.asarray(L0_ffn_router_b), (P, EXPERTS))], axis=1))
    consts = np.zeros((P, K_COLS), np.float32)
    consts[:, K_ID:K_ID + P] = np.eye(P)
    per_head = HID // HEADS
    for f in range(KC):
        for r in range(P):
            head = (f * P + r) // per_head
            consts[r, K_HS + f * HEADS + head] = 1.0
            for b in range(BLK):
                consts[b * HEADS + head, K_HX + f * P + r] = 1.0
                consts[32 + b * HEADS + head, K_HX + f * P + r] = 1.0
    consts[:, K_TRI:K_TRI + P] = np.triu(np.ones((P, P)), 1) - 1
    consts[:, K_IOTA:K_IOTA + P] = np.arange(P)
    consts[:, K_RANK:K_RANK + EXPERTS] = EXPERTS - np.arange(EXPERTS)
    consts[:, K_TOK:] = 1 + np.arange(NBLK) * P + np.arange(P)[:, None]
    ebias = np.ascontiguousarray(np.asarray(L0_ffn_expert_b).reshape(1, -1))

    arrays = {"x": np.ascontiguousarray(L0_attn_x), "wall": wall, "wexp": wexp, "wmod": wmod, "params": params,
              "consts": consts, "ebias": ebias}
    nc = bacc.Bacc("TRN2", target_bir_lowering=False, num_devices=1)
    aps = [nc.dram_tensor(f"in_{k}", a.shape, F32, kind="ExternalInput").ap() for k, a in arrays.items()]
    out = nc.dram_tensor("out_0", (BATCH, SEQ, HID), F32, kind="ExternalOutput").ap()
    rec = nc.dram_tensor("rec", (BATCH * SEQ, 2 * HID), F32, kind="Internal").ap()
    build(nc, *aps, out, rec)
    r = run_bass_kernel_spmd(nc, [{f"in_{k}": a for k, a in arrays.items()}], core_ids=[0])
    return r.results[0]["out_0"]
```
